# Optimizing a Trainium2 kernel written in Bass

```python
import numpy as np
import jax
import jax.numpy as jnp

def _softmax(x, axis=-1):
    return jax.nn.softmax(x, axis=axis)

def _gelu(x):
    return jax.nn.gelu(x, approximate=True)

def _silu(x):
    return jax.nn.silu(x)

def _sigmoid(x):
    return jax.nn.sigmoid(x)

def _layernorm(x, axis=-1, eps=1e-05):
    m = jnp.mean(x, axis=axis, keepdims=True)
    v = jnp.var(x, axis=axis, keepdims=True)
    return (x - m) / jnp.sqrt(v + eps)

def _scatter_add(tgt, idx, src, axis=0):
    return tgt.at[idx].add(src)

def _segment_sum(src, seg, n):
    return jax.ops.segment_sum(src, seg, n)
kernel_name = 'mk_gnn_preln_d2_gnn_r64_068601'

def setup_inputs(seed: int=0):
    np.random.seed(seed)
    _w = jnp.asarray

    def _rec_inputs():
        import jax
        import jax.numpy as jnp
        _gk = jax.random.key(seed)
        x = -0.000202 + 1 * jax.random.normal(jax.random.fold_in(_gk, 1), (100000, 128), jnp.float32)
        src = jax.random.randint(jax.random.fold_in(_gk, 2), (50000,), 0, 100000, jnp.int32)
        dst = jax.random.randint(jax.random.fold_in(_gk, 3), (50000,), 0, 100000, jnp.int32)
        _o = jnp.argsort(dst, stable=True)
        src = src[_o]
        dst = dst[_o]
        edge_type_64 = jax.random.randint(jax.random.fold_in(_gk, 13), (50000,), 0, 64, jnp.int32)
        return (x, src, dst, edge_type_64)
    x, src, dst, edge_type_64 = _rec_inputs()

    def _L0_gnn_setup():
        import jax, jax.numpy as jnp
        import numpy as np
        N_NODES = 50000
        N_EDGES = 12500
        C_IN = 128
        HID = 128
        C_OUT = 128

        def _glorot(key, shape):
            fan_in, fan_out = shape
            lim = (6.0 / (fan_in + fan_out)) ** 0.5
            return jax.random.uniform(key, shape, jnp.float32, -lim, lim)

        def _edge_conv(x, src, dst, W1, b1, W2, b2, n_nodes):
            xi = x[dst]
            xj = x[src]
            m = jnp.concatenate([xi, xj - xi], axis=-1)
            h = jax.nn.relu(m @ W1 + b1) @ W2 + b2
            agg = jax.ops.segment_max(h, dst, num_segments=n_nodes)
            return jnp.where(jnp.isfinite(agg), agg, 0.0)
        key = jax.random.key(seed)
        ks = jax.random.split(key, 8)
        x = jax.random.normal(ks[0], (N_NODES, C_IN), jnp.float32)
        edge_index = jax.random.randint(ks[1], (2, N_EDGES), 0, N_NODES, jnp.int32)
        return {'x': x, 'edge_index': edge_index, 'W1_in': _glorot(ks[2], (2 * C_IN, HID)), 'b1_in': jnp.zeros((HID,), jnp.float32), 'W2_in': _glorot(ks[3], (HID, HID)), 'b2_in': jnp.zeros((HID,), jnp.float32), 'W1_hid': _glorot(ks[4], (2 * HID, HID)), 'b1_hid': jnp.zeros((HID,), jnp.float32), 'W2_hid': _glorot(ks[5], (HID, HID)), 'b2_hid': jnp.zeros((HID,), jnp.float32), 'W1_out': _glorot(ks[6], (2 * HID, HID)), 'b1_out': jnp.zeros((HID,), jnp.float32), 'W2_out': _glorot(ks[7], (HID, C_OUT)), 'b2_out': jnp.zeros((C_OUT,), jnp.float32)}
    _L0_gnn_all = _L0_gnn_setup()
    _L0_gnn_in = {k: v for k, v in _L0_gnn_all.items() if k in ('W1_in', 'b1_in', 'W2_in', 'b2_in', 'W1_hid', 'b1_hid', 'W2_hid', 'b2_hid', 'W1_out', 'b1_out', 'W2_out', 'b2_out')}
    del _L0_gnn_all

    def _L1_gnn_setup():
        import jax, jax.numpy as jnp
        import numpy as np
        from jax import lax
        EMBED_DIM = 128
        N_RELATIONS = 64
        N_ENTITIES = 100000
        N_EDGES = 9375
        key = jax.random.key(seed)
        k1, k2, k3, k4, k5, k6 = jax.random.split(key, 6)
        entity_emb = jax.random.normal(k1, (N_ENTITIES, EMBED_DIM), dtype=jnp.float32)
        heads = jax.random.randint(k2, (N_EDGES,), 0, N_ENTITIES)
        rels = jax.random.randint(k3, (N_EDGES,), 0, N_RELATIONS)
        tails = jax.random.randint(k4, (N_EDGES,), 0, N_ENTITIES)
        rel_embed_weight = 0.01 * jax.random.normal(k5, (N_RELATIONS, EMBED_DIM), dtype=jnp.float32)
        xavier = float(np.sqrt(6.0 / (EMBED_DIM + EMBED_DIM)))
        W = jax.random.uniform(k6, (EMBED_DIM, EMBED_DIM), dtype=jnp.float32, minval=-xavier, maxval=xavier)
        return {'entity_emb': entity_emb, 'rel_embed_weight': rel_embed_weight, 'W': W, 'heads': heads, 'rels': rels, 'tails': tails}
    _L1_gnn_all = _L1_gnn_setup()
    _L1_gnn_in = {k: v for k, v in _L1_gnn_all.items() if k in ('rel_embed_weight', 'W')}
    del _L1_gnn_all
    return {'x': x, 'src': src, 'dst': dst, 'edge_type_64': edge_type_64, 'L0_gnn_W1_in': _L0_gnn_in['W1_in'], 'L0_gnn_b1_in': _L0_gnn_in['b1_in'], 'L0_gnn_W2_in': _L0_gnn_in['W2_in'], 'L0_gnn_b2_in': _L0_gnn_in['b2_in'], 'L0_gnn_W1_hid': _L0_gnn_in['W1_hid'], 'L0_gnn_b1_hid': _L0_gnn_in['b1_hid'], 'L0_gnn_W2_hid': _L0_gnn_in['W2_hid'], 'L0_gnn_b2_hid': _L0_gnn_in['b2_hid'], 'L0_gnn_W1_out': _L0_gnn_in['W1_out'], 'L0_gnn_b1_out': _L0_gnn_in['b1_out'], 'L0_gnn_W2_out': _L0_gnn_in['W2_out'], 'L0_gnn_b2_out': _L0_gnn_in['b2_out'], 'L1_gnn_rel_embed_weight': _L1_gnn_in['rel_embed_weight'], 'L1_gnn_W': _L1_gnn_in['W']}

def reference(x, src, dst, edge_type_64, L0_gnn_W1_in, L0_gnn_b1_in, L0_gnn_W2_in, L0_gnn_b2_in, L0_gnn_W1_hid, L0_gnn_b1_hid, L0_gnn_W2_hid, L0_gnn_b2_hid, L0_gnn_W1_out, L0_gnn_b1_out, L0_gnn_W2_out, L0_gnn_b2_out, L1_gnn_rel_embed_weight, L1_gnn_W):
    import jax
    import jax.numpy as jnp

    def _L0_gnn_ref(x, edge_index, W1_in, b1_in, W2_in, b2_in, W1_hid, b1_hid, W2_hid, b2_hid, W1_out, b1_out, W2_out, b2_out):
        import jax, jax.numpy as jnp
        import numpy as np
        N_NODES = 50000
        N_EDGES = 12500
        C_IN = 128
        HID = 128
        C_OUT = 128

        def _glorot(key, shape):
            fan_in, fan_out = shape
            lim = (6.0 / (fan_in + fan_out)) ** 0.5
            return jax.random.uniform(key, shape, jnp.float32, -lim, lim)

        def _edge_conv(x, src, dst, W1, b1, W2, b2, n_nodes):
            xi = x[dst]
            xj = x[src]
            m = jnp.concatenate([xi, xj - xi], axis=-1)
            h = jax.nn.relu(m @ W1 + b1) @ W2 + b2
            agg = jax.ops.segment_max(h, dst, num_segments=n_nodes)
            return jnp.where(jnp.isfinite(agg), agg, 0.0)
        src, dst = (edge_index[0], edge_index[1])
        n = x.shape[0]
        x = _edge_conv(x, src, dst, W1_in, b1_in, W2_in, b2_in, n)
        x = jax.nn.relu(x)
        x = _edge_conv(x, src, dst, W1_hid, b1_hid, W2_hid, b2_hid, n)
        x = jax.nn.relu(x)
        x = _edge_conv(x, src, dst, W1_out, b1_out, W2_out, b2_out, n)
        return x

    def _L1_gnn_ref(entity_emb, rel_embed_weight, W, heads, rels, tails):
        import jax, jax.numpy as jnp
        import numpy as np
        from jax import lax
        EMBED_DIM = 128
        N_RELATIONS = 64
        N_ENTITIES = 100000
        N_EDGES = 9375
        n_entities = entity_emb.shape[0]
        e_h = entity_emb[heads]
        e_t = entity_emb[tails]
        e_r = rel_embed_weight[rels]
        score = jnp.sum(e_t * jnp.tanh(e_h + e_r), axis=-1)
        score_exp = jnp.exp(score - lax.stop_gradient(jnp.max(score)))
        score_sum = jax.ops.segment_sum(score_exp, heads, num_segments=n_entities)
        attn = score_exp / (score_sum[heads] + 1e-10)
        agg = jax.ops.segment_sum(attn[:, None] * e_t, heads, num_segments=n_entities)
        out = (entity_emb + agg) @ W.T
        return jax.nn.leaky_relu(out, negative_slope=0.2)
    edge_index = jnp.stack([src, dst])
    h = jnp.maximum(_layernorm(x, axis=-1), 0.0)
    x = x + _L0_gnn_ref(h, edge_index, L0_gnn_W1_in, L0_gnn_b1_in, L0_gnn_W2_in, L0_gnn_b2_in, L0_gnn_W1_hid, L0_gnn_b1_hid, L0_gnn_W2_hid, L0_gnn_b2_hid, L0_gnn_W1_out, L0_gnn_b1_out, L0_gnn_W2_out, L0_gnn_b2_out)
    h = jnp.maximum(_layernorm(x, axis=-1), 0.0)
    x = x + _L1_gnn_ref(h, L1_gnn_rel_embed_weight, L1_gnn_W, src, edge_type_64, dst)
    return x

_drawn_inputs = setup_inputs


def setup_inputs(seed=0):
    import zlib

    import numpy as np

    out = dict(_drawn_inputs(seed))
    spreads = {'L0_gnn_b1_in': (0.0, 0.489),
     'L0_gnn_b2_in': (0.0, 0.372),
     'L0_gnn_b1_hid': (0.0, 0.315),
     'L0_gnn_b2_hid': (0.0, 0.1),
     'L0_gnn_b1_out': (0.0, 0.1),
     'L0_gnn_b2_out': (0.0, 0.1)}
    factors = {'L1_gnn_rel_embed_weight': 8.0}
    for name, (base, spread) in spreads.items():
        noise = np.random.default_rng([zlib.crc32(name.encode()), seed]).standard_normal(out[name].shape)
        drawn = base * np.exp(spread * noise) if base else spread * noise
        out[name] = jnp.asarray(drawn.astype(out[name].dtype))
    for name, factor in factors.items():
        out[name] = (out[name] * factor).astype(out[name].dtype)
    return out
```

```python
import concourse.bass as bass
from concourse import mybir
from contextlib import ExitStack

F32 = mybir.dt.float32
I32 = mybir.dt.int32
ALU = mybir.AluOpType
ACT = mybir.ActivationFunctionType
AX = mybir.AxisListType

P = 128
TILES = 4
WIN = TILES * P
PIECE = 8
SUM_W = P + 4
SKIP = float(1 << 20)
HUGE = 3.0e38
EPS = 1e-5
RELATIONS = 64


def window(ap, w):
    return ap[bass.ds(w, 1)].rearrange("o p n -> (o p) n")


def hold(eng, go, sem, value):
    if not isinstance(value, int):
        value = eng.to_reg(value)
        eng.wait_ge(go, 1)
    eng.wait_ge(sem, value)


def later(i):
    return not isinstance(i, int) or i > 0


def front_and_back(eng, rounds, front, back):
    front(0, 0)
    front(0, 1)
    back(0, 0)
    front(1, 0)
    back(0, 1)
    front(1, 1)
    back(1, 0)
    with eng.Fori(2, rounds) as i:
        front(i, 0)
        back(i - 1, 1)
        front(i, 1)
        back(i, 0)
    back(rounds - 1, 1)


def lead_and_trail(eng, rounds, lead, trail):
    lead(0, 0)
    lead(0, 1)
    lead(1, 0)
    trail(0, 0)
    lead(1, 1)
    trail(0, 1)
    with eng.Fori(2, rounds) as i:
        lead(i, 0)
        trail(i - 1, 0)
        lead(i, 1)
        trail(i - 1, 1)
    trail(rounds - 1, 0)
    trail(rounds - 1, 1)


def edge_conv_pass(nc, tag, consts, *, first, last, cols, dst_row, table_in, x_rows, table_out, f_in, f_out,
                   xd_stream, weights, windows, bulk):
    backward = not first and not last
    rounds = windows // 2
    gathers = 2 * TILES if first else TILES
    ctx = ExitStack()
    with ctx:
        ctx.enter_context(nc.cleanup_on_exit())
        banks = consts["banks"]

        def sb(name, shape, dt=F32):
            return ctx.enter_context(nc.sbuf_tensor(f"{tag}_{name}", shape, dt))

        def sem(name):
            return nc.alloc_semaphore(f"{tag}_{name}")

        ident, eps_col = consts["ident"], consts["eps"]
        w1a, w1b, wd, w2 = sb("w1a", [P, P]), sb("w1b", [P, P]), sb("wd", [P, P]), sb("w2", [P, P])
        b1, b2 = sb("b1", [P, 1]), sb("b2", [P, 1])
        gather_idx = [sb(f"gather_idx{s}", [P, gathers], I32) for s in (0, 1)]
        seg = [sb(f"seg{s}", [P, 3 * TILES], I32) for s in (0, 1)]
        drow = [sb(f"drow{s}", [P, WIN + 2], I32) for s in (0, 1)]
        rows_in = [sb(f"rows_in{s}", [P, gathers, P]) for s in (0, 1)]
        keep = [sb(f"keep{s}", [P, WIN]) for s in (0, 1)]
        xiT = [sb(f"xiT{s}", [P, WIN]) for s in (0, 1)]
        xjT = [sb(f"xjT{s}", [P, WIN]) for s in (0, 1)]
        hidden = [sb(f"hidden{s}", [P, WIN]) for s in (0, 1)]
        value = [sb(f"value{s}", [P, WIN]) for s in (0, 1)]
        segmax = [sb(f"segmax{s}", [P, WIN]) for s in (0, 1)]
        rows_out = [sb(f"rows_out{s}", [P, TILES, P]) for s in (0, 1)]
        inner = [sb(f"inner{s}", [P, TILES]) for s in (0, 1)]
        scatter_idx = [sb(f"scatter_idx{s}", [P, TILES], I32) for s in (0, 1)]
        if first:
            stats = [sb(f"stats{s}", [P, gathers, 6]) for s in (0, 1)]
            mean_var = [sb(f"mean_var{s}", [P, gathers, 2]) for s in (0, 1)]
            std = [sb(f"std{s}", [P, gathers]) for s in (0, 1)]
            rstd = [sb(f"rstd{s}", [P, gathers]) for s in (0, 1)]
            shift = [sb(f"shift{s}", [P, gathers]) for s in (0, 1)]
            normed = [sb(f"normed{s}", [P, gathers, P]) for s in (0, 1)]
        else:
            scan_in = [sb(f"scan_in{s}", [P, WIN]) for s in (0, 1)]
        if last:
            penalty = [sb(f"penalty{s}", [P, WIN]) for s in (0, 1)]
            xd = [sb(f"xd{s}", [P, WIN]) for s in (0, 1)]
        ps_xj, ps_xi = banks[0:2], banks[2:4]
        ps_hidden, ps_value, ps_rows = banks[4:7]

        weights_in, wd_ready = sem("weights_in"), sem("wd_ready")
        idx_in = [sem(f"idx_in{s}") for s in (0, 1)]
        seg_in = [sem(f"seg_in{s}") for s in (0, 1)]
        drow_in = [sem(f"drow_in{s}") for s in (0, 1)]
        gathered = [sem(f"gathered{s}") for s in (0, 1)]
        scattered = [sem(f"scattered{s}") for s in (0, 1)]
        segmax_stored = [sem(f"segmax_stored{s}") for s in (0, 1)]
        if first:
            xd_stored = [sem(f"xd_stored{s}") for s in (0, 1)]
            stats_ready, mean_var_ready, std_ready = sem("stats_ready"), sem("mean_var_ready"), sem("std_ready")
            rstd_ready, shift_ready, normed_ready = sem("rstd_ready"), sem("shift_ready"), sem("normed_ready")
        else:
            scan_in_loaded = [sem(f"scan_in_loaded{s}") for s in (0, 1)]
            xi_ready = sem("xi_ready")
        if last:
            xd_in = [sem(f"xd_in{s}") for s in (0, 1)]
            penalty_ready = sem("penalty_ready")
        bulk_done = sem("bulk_done")
        keep_ready, x_transposed, xT_ready = sem("keep_ready"), sem("x_transposed"), sem("xT_ready")
        hidden_summed, hidden_ready = sem("hidden_summed"), sem("hidden_ready")
        value_summed, value_ready = sem("value_summed"), sem("value_ready")
        segmax_ready, inner_ready, scatter_idx_ready = sem("segmax_ready"), sem("inner_ready"), sem("scatter_idx_ready")
        rows_transposed, rows_ready = sem("rows_transposed"), sem("rows_ready")

        def at(i, s):
            w = i * 2 + s
            return (windows - 1) - w if backward else w

        def run(t):
            return t[:, ::-1] if backward else t[:, :]

        def end(t):
            return t[:, 0:1] if backward else t[:, WIN - 1:WIN]

        go = consts["go"]
        block = ctx.enter_context(nc.Block())

        @block.sync
        def _(sp):
            for t, a in ((w1a, weights["W1"][0:P, :]), (w1b, weights["W1"][P:2 * P, :]), (w2, weights["W2"]),
                         (b1, weights["b1"]), (b2, weights["b2"])):
                sp.dma_start(t[:, :], a).then_inc(weights_in, 16)

            def load(i, s):
                n = i * 2 + s
                if later(i):
                    hold(sp, go, gathered[s], 16 * gathers * i)
                sp.dma_start(gather_idx[s][:, :], window(cols, at(i, s))[:, :gathers]).then_inc(idx_in[s], 16)
                if later(i):
                    hold(sp, go, keep_ready, n - 1)
                sp.dma_start(drow[s][:, :], window(dst_row, at(i, s)).to_broadcast([P, WIN + 2])).then_inc(drow_in[s], 16)
                if later(i):
                    hold(sp, go, scatter_idx_ready, n - 1)
                sp.dma_start(seg[s][:, :], window(cols, at(i, s))[:, 2 * TILES:5 * TILES]).then_inc(seg_in[s], 16)
                if not first:
                    if later(i):
                        hold(sp, go, xi_ready, n - 1)
                    sp.dma_start(scan_in[s][:, :], window(f_in, at(i, s))).then_inc(scan_in_loaded[s], 16)
                if last:
                    if later(i):
                        hold(sp, go, rows_ready, n - 1)
                    sp.dma_start(xd[s][:, :], window(xd_stream, at(i, s))).then_inc(xd_in[s], 16)

            def store(i, s):
                n = i * 2 + s
                if first:
                    hold(sp, go, gathered[s], 16 * gathers * (i + 1))
                    sp.dma_start(window(xd_stream, at(i, s)),
                                 rows_in[s][:, TILES:, :].rearrange("p k f -> p (k f)")).then_inc(xd_stored[s], 16)
                hold(sp, go, segmax_ready, n + 1)
                sp.dma_start(window(f_out, at(i, s)), segmax[s][:, :]).then_inc(segmax_stored[s], 16)
                bulk(sp, n, bulk_done)

            lead_and_trail(sp, rounds, load, store)
            for s in (0, 1):
                sp.wait_ge(segmax_stored[s], 16 * rounds)
                if first:
                    sp.wait_ge(xd_stored[s], 16 * rounds)
            sp.wait_ge(bulk_done, 16 * windows)

        @block.gpsimd
        def _(pool):
            def gather(i, s):
                n = i * 2 + s
                hold(pool, go, idx_in[s], 16 * (i + 1))
                if later(i):
                    if first:
                        hold(pool, go, normed_ready, n - 1)
                        hold(pool, go, xd_stored[s], 16 * i)
                    else:
                        hold(pool, go, x_transposed, n - 1)
                for k in range(gathers):
                    pool.indirect_dma_start(
                        rows_in[s][:, k, :], None, (x_rows if first else table_in)[:, :],
                        bass.IndirectOffsetOnAxis(ap=gather_idx[s][:, k:k + 1], axis=0)).then_inc(gathered[s], 16)

            def scatter(i, s):
                n = i * 2 + s
                hold(pool, go, scatter_idx_ready, n + 1)
                hold(pool, go, rows_ready, n + 1)
                for k in range(TILES):
                    pool.indirect_dma_start(
                        table_out[:, :], bass.IndirectOffsetOnAxis(ap=scatter_idx[s][:, k:k + 1], axis=0),
                        rows_out[s][:, k, :], None,
                        bounds_check=table_out.shape[0] - 1, oob_is_err=False).then_inc(scattered[s], 16)

            lead_and_trail(pool, rounds, gather, scatter)
            for s in (0, 1):
                pool.wait_ge(scattered[s], 16 * TILES * rounds)

        @block.vector
        def _(dve):
            dve.wait_ge(weights_in, 5 * 16)
            nc.vector.tensor_tensor(wd[:, :], w1a[:, :], w1b[:, :], ALU.subtract).then_inc(wd_ready, 1)

            def front(i, s):
                n = i * 2 + s
                dve.wait_ge(drow_in[s], 16 * (i + 1))
                beside = drow[s][:, 2:] if backward else drow[s][:, :WIN]
                nc.vector.tensor_tensor(keep[s][:, :], drow[s][:, 1:WIN + 1], beside, ALU.is_equal).then_inc(keep_ready, 1)
                if last:
                    dve.wait_ge(keep_ready, n + 1)
                    nc.vector.tensor_scalar(penalty[s][:, :], keep[s][:, :], -1.0, HUGE, ALU.add, ALU.mult).then_inc(penalty_ready, 1)
                if first:
                    dve.wait_ge(gathered[s], 16 * gathers * (i + 1))
                    for k in range(gathers):
                        ins = nc.vector.bn_stats(stats[s][:, k, :], rows_in[s][:, k, :])
                    ins.then_inc(stats_ready, 1)
                    hold(dve, go, stats_ready, n + 1)
                    for k in range(gathers):
                        ins = nc.vector.bn_aggr(mean_var[s][:, k, :], stats[s][:, k, :])
                    ins.then_inc(mean_var_ready, 1)
                    dve.wait_ge(std_ready, n + 1)
                    nc.vector.reciprocal(rstd[s][:, :], std[s][:, :]).then_inc(rstd_ready, 1)
                    dve.wait_ge(rstd_ready, n + 1)
                    nc.vector.scalar_tensor_tensor(shift[s][:, :], mean_var[s][:, :, 0], -1.0, rstd[s][:, :],
                                                   ALU.mult, ALU.mult).then_inc(shift_ready, 1)
                else:
                    dve.wait_ge(scan_in_loaded[s], 16 * (i + 1))
                    dve.wait_ge(keep_ready, n + 1)
                    if later(i):
                        dve.wait_ge(hidden_summed, n - 1)
                    if later(i) or s:
                        dve.wait_ge(xi_ready, n)
                    nc.vector.tensor_tensor_scan(run(xiT[s]), run(keep[s]), run(scan_in[s]),
                                                 end(xiT[1 - s]) if later(i) or s else 0.0,
                                                 ALU.mult, ALU.max).then_inc(xi_ready, 1)

            def back(i, s):
                n = i * 2 + s
                dve.wait_ge(value_ready, n + 1)
                dve.wait_ge(keep_ready, n + 1)
                if last:
                    dve.wait_ge(penalty_ready, n + 1)
                if later(i):
                    dve.wait_ge(segmax_stored[s], 16 * i)
                    dve.wait_ge(rows_transposed, n - 1)
                if later(i) or s:
                    dve.wait_ge(segmax_ready, n)
                nc.vector.tensor_tensor_scan(run(segmax[s]), run(penalty[s] if last else keep[s]), run(value[s]),
                                             end(segmax[1 - s]) if later(i) or s else 0.0,
                                             ALU.add if last else ALU.mult, ALU.max).then_inc(segmax_ready, 1)
                dve.wait_ge(seg_in[s], 16 * (i + 1))
                beside = seg[s][:, 2 * TILES:] if backward else seg[s][:, TILES:2 * TILES]
                nc.vector.tensor_tensor(inner[s][:, :], seg[s][:, :TILES], beside, ALU.is_equal).then_inc(inner_ready, 1)
                dve.wait_ge(inner_ready, n + 1)
                if later(i):
                    dve.wait_ge(scattered[s], 16 * TILES * i)
                nc.vector.scalar_tensor_tensor(scatter_idx[s][:, :], inner[s][:, :], SKIP, seg[s][:, :TILES],
                                               ALU.mult, ALU.add).then_inc(scatter_idx_ready, 1)
                dve.wait_ge(rows_transposed, n + 1)
                out = rows_out[s][:, :, :].rearrange("p k f -> p (k f)")
                if last:
                    dve.wait_ge(xd_in[s], 16 * (i + 1))
                    nc.vector.tensor_tensor(out, ps_rows[:, :], xd[s][:, :], ALU.add).then_inc(rows_ready, 1)
                else:
                    nc.vector.tensor_copy(out, ps_rows[:, :]).then_inc(rows_ready, 1)

            front_and_back(dve, rounds, front, back)

        @block.scalar
        def _(act):
            act.wait_ge(weights_in, 5 * 16)

            def front(i, s):
                n = i * 2 + s
                if first:
                    act.wait_ge(mean_var_ready, n + 1)
                    nc.scalar.activation(std[s][:, :], mean_var[s][:, :, 1], ACT.Sqrt, bias=eps_col[:, :]).then_inc(std_ready, 1)
                    act.wait_ge(shift_ready, n + 1)
                    if later(i):
                        act.wait_ge(x_transposed, n - 1)
                    for k in range(gathers):
                        ins = nc.scalar.activation(normed[s][:, k, :], rows_in[s][:, k, :], ACT.Relu,
                                                   bias=shift[s][:, k:k + 1], scale=rstd[s][:, k:k + 1])
                    ins.then_inc(normed_ready, 1)
                act.wait_ge(x_transposed, n + 1)
                if later(i):
                    act.wait_ge(hidden_summed, n - 1)
                if first:
                    nc.scalar.copy(xiT[s][:, :], ps_xi[s][:, :])
                nc.scalar.copy(xjT[s][:, :], ps_xj[s][:, :]).then_inc(xT_ready, 1)

            def back(i, s):
                n = i * 2 + s
                act.wait_ge(hidden_summed, n + 1)
                if later(i):
                    act.wait_ge(value_summed, n - 1)
                nc.scalar.activation(hidden[s][:, :], ps_hidden[:, :], ACT.Relu, bias=b1[:, :]).then_inc(hidden_ready, 1)
                act.wait_ge(value_summed, n + 1)
                if later(i):
                    act.wait_ge(segmax_ready, n - 1)
                nc.scalar.activation(value[s][:, :], ps_value[:, :], ACT.Identity if last else ACT.Relu,
                                     bias=b2[:, :]).then_inc(value_ready, 1)

            front_and_back(act, rounds, front, back)

        @block.tensor
        def _(pe):
            def front(i, s):
                n = i * 2 + s
                if first:
                    pe.wait_ge(normed_ready, n + 1)
                else:
                    pe.wait_ge(gathered[s], 16 * gathers * (i + 1))
                if later(i):
                    pe.wait_ge(xT_ready, n - 1)
                for k in range(gathers):
                    to = (ps_xj if k < TILES else ps_xi)[s]
                    k4 = k % TILES
                    ins = nc.tensor.transpose(to[:, k4 * P:(k4 + 1) * P], (normed if first else rows_in)[s][:, k, :], ident[:, :])
                ins.then_inc(x_transposed, 1)

            def back(i, s):
                n = i * 2 + s
                pe.wait_ge(xT_ready, n + 1)
                if not first:
                    pe.wait_ge(xi_ready, n + 1)
                if later(i) or s:
                    pe.wait_ge(hidden_ready, n)
                nc.tensor.matmul(ps_hidden[:, :], w1b[:, :], xjT[s][:, :], start=True, stop=False)
                nc.tensor.matmul(ps_hidden[:, :], wd[:, :], xiT[s][:, :], start=False, stop=True).then_inc(hidden_summed, 1)
                pe.wait_ge(hidden_ready, n + 1)
                if later(i) or s:
                    pe.wait_ge(value_ready, n)
                nc.tensor.matmul(ps_value[:, :], w2[:, :], hidden[s][:, :], start=True, stop=True).then_inc(value_summed, 1)
                pe.wait_ge(segmax_ready, n + 1)
                if later(i) or s:
                    pe.wait_ge(rows_ready, n)
                for k in range(TILES):
                    ins = nc.tensor.transpose(ps_rows[:, k * P:(k + 1) * P], segmax[s][:, k * P:(k + 1) * P], ident[:, :])
                ins.then_inc(rows_transposed, 1)

            pe.wait_ge(weights_in, 5 * 16)
            pe.wait_ge(wd_ready, 1)
            front_and_back(pe, rounds, front, back)


def score_pass(nc, consts, *, cols, dst_row, type_row, x1_table, f_in, xd_stream, et_stream, rel, scores, windows):
    rounds = windows // 2
    ctx = ExitStack()
    with ctx:
        ctx.enter_context(nc.cleanup_on_exit())
        banks = consts["banks"]

        def sb(name, shape, dt=F32):
            return ctx.enter_context(nc.sbuf_tensor(f"sc_{name}", shape, dt))

        def sem(name):
            return nc.alloc_semaphore(f"sc_{name}")

        SIDES = 2 * TILES
        ident, eps_col, relation_col = consts["ident"], consts["eps"], consts["relation_col"]
        rel_sb = sb("rel", [RELATIONS, P])
        gather_idx = [sb(f"gather_idx{s}", [P, TILES], I32) for s in (0, 1)]
        drow = [sb(f"drow{s}", [P, WIN + 2], I32) for s in (0, 1)]
        trow = [sb(f"trow{s}", [RELATIONS, WIN], I32) for s in (0, 1)]
        scan_in = [sb(f"scan_in{s}", [P, WIN]) for s in (0, 1)]
        xd = [sb(f"xd{s}", [P, WIN]) for s in (0, 1)]
        keep = [sb(f"keep{s}", [P, WIN]) for s in (0, 1)]
        penalty = [sb(f"penalty{s}", [P, WIN]) for s in (0, 1)]
        full = [sb(f"full{s}", [P, WIN]) for s in (0, 1)]
        onehot = [sb(f"onehot{s}", [RELATIONS, WIN]) for s in (0, 1)]
        sides = [sb(f"sides{s}", [P, SIDES, P]) for s in (0, 1)]
        stats = [sb(f"stats{s}", [P, SIDES, 6]) for s in (0, 1)]
        mean_var = [sb(f"mean_var{s}", [P, SIDES, 2]) for s in (0, 1)]
        std = [sb(f"std{s}", [P, SIDES]) for s in (0, 1)]
        rstd = [sb(f"rstd{s}", [P, SIDES]) for s in (0, 1)]
        shift = [sb(f"shift{s}", [P, SIDES]) for s in (0, 1)]
        normed = [sb(f"normed{s}", [P, SIDES, P]) for s in (0, 1)]
        tanh_sb = [sb(f"tanh{s}", [P, WIN]) for s in (0, 1)]
        product = [sb(f"product{s}", [P, TILES, P]) for s in (0, 1)]
        ps_full, ps_arg = banks[0:2], banks[2:4]

        rel_in = sem("rel_in")
        idx_in = [sem(f"idx_in{s}") for s in (0, 1)]
        drow_in = [sem(f"drow_in{s}") for s in (0, 1)]
        trow_in = [sem(f"trow_in{s}") for s in (0, 1)]
        scan_in_loaded = [sem(f"scan_in_loaded{s}") for s in (0, 1)]
        xd_in = [sem(f"xd_in{s}") for s in (0, 1)]
        gathered = [sem(f"gathered{s}") for s in (0, 1)]
        et_stored = [sem(f"et_stored{s}") for s in (0, 1)]
        keep_ready, penalty_ready, full_ready, onehot_ready = sem("keep_ready"), sem("penalty_ready"), sem("full_ready"), sem("onehot_ready")
        full_transposed, xt_ready, stats_ready = sem("full_transposed"), sem("xt_ready"), sem("stats_ready")
        mean_var_ready, std_ready, rstd_ready, shift_ready = sem("mean_var_ready"), sem("std_ready"), sem("rstd_ready"), sem("shift_ready")
        normed_ready, arg_summed, tanh_ready = sem("normed_ready"), sem("arg_summed"), sem("tanh_ready")
        product_ready, score_ready = sem("product_ready"), sem("score_ready")

        def at(i, s):
            return (windows - 1) - (i * 2 + s)

        go = consts["go"]
        block = ctx.enter_context(nc.Block())

        @block.sync
        def _(sp):
            sp.dma_start(rel_sb[:, :], rel).then_inc(rel_in, 16)

            def load(i, s):
                n = i * 2 + s
                if later(i):
                    hold(sp, go, gathered[s], 16 * TILES * i)
                sp.dma_start(gather_idx[s][:, :], window(cols, at(i, s))[:, :TILES]).then_inc(idx_in[s], 16)
                if later(i):
                    hold(sp, go, keep_ready, n - 1)
                sp.dma_start(drow[s][:, :], window(dst_row, at(i, s)).to_broadcast([P, WIN + 2])).then_inc(drow_in[s], 16)
                if later(i):
                    hold(sp, go, onehot_ready, n - 1)
                sp.dma_start(trow[s][:, :], window(type_row, at(i, s)).to_broadcast([RELATIONS, WIN])).then_inc(trow_in[s], 16)
                if later(i):
                    hold(sp, go, full_ready, n - 1)
                sp.dma_start(scan_in[s][:, :], window(f_in, at(i, s))).then_inc(scan_in_loaded[s], 16)
                if later(i):
                    hold(sp, go, xt_ready, n - 1)
                sp.dma_start(xd[s][:, :], window(xd_stream, at(i, s))).then_inc(xd_in[s], 16)

            def store(i, s):
                hold(sp, go, normed_ready, i * 2 + s + 1)
                sp.dma_start(window(et_stream, at(i, s)),
                             normed[s][:, TILES:, :].rearrange("p k f -> p (k f)")).then_inc(et_stored[s], 16)

            lead_and_trail(sp, rounds, load, store)
            for s in (0, 1):
                sp.wait_ge(et_stored[s], 16 * rounds)

        @block.gpsimd
        def _(pool):
            def gather(i, s):
                hold(pool, go, idx_in[s], 16 * (i + 1))
                if later(i):
                    hold(pool, go, normed_ready, i * 2 + s - 1)
                for k in range(TILES):
                    pool.indirect_dma_start(
                        sides[s][:, k, :], None, x1_table[:, :],
                        bass.IndirectOffsetOnAxis(ap=gather_idx[s][:, k:k + 1], axis=0)).then_inc(gathered[s], 16)

            gather(0, 0)
            gather(0, 1)
            with pool.Fori(1, rounds) as i:
                gather(i, 0)
                gather(i, 1)

        @block.vector
        def _(dve):
            def front(i, s):
                n = i * 2 + s
                dve.wait_ge(drow_in[s], 16 * (i + 1))
                nc.vector.tensor_tensor(keep[s][:, :], drow[s][:, 1:WIN + 1], drow[s][:, 2:], ALU.is_equal).then_inc(keep_ready, 1)
                dve.wait_ge(trow_in[s], 16 * (i + 1))
                if later(i):
                    dve.wait_ge(arg_summed, n - 1)
                nc.vector.tensor_scalar(onehot[s][:, :], trow[s][:, :], relation_col[:, :], None, ALU.is_equal).then_inc(onehot_ready, 1)
                dve.wait_ge(keep_ready, n + 1)
                nc.vector.tensor_scalar(penalty[s][:, :], keep[s][:, :], -1.0, HUGE, ALU.add, ALU.mult).then_inc(penalty_ready, 1)
                dve.wait_ge(scan_in_loaded[s], 16 * (i + 1))
                dve.wait_ge(penalty_ready, n + 1)
                if later(i):
                    dve.wait_ge(full_transposed, n - 1)
                if later(i) or s:
                    dve.wait_ge(full_ready, n)
                nc.vector.tensor_tensor_scan(full[s][:, ::-1], penalty[s][:, ::-1], scan_in[s][:, ::-1],
                                             full[1 - s][:, 0:1] if later(i) or s else 0.0,
                                             ALU.add, ALU.max).then_inc(full_ready, 1)

            def back(i, s):
                n = i * 2 + s
                dve.wait_ge(gathered[s], 16 * TILES * (i + 1))
                for k in range(TILES):
                    nc.vector.bn_stats(stats[s][:, k, :], sides[s][:, k, :])
                dve.wait_ge(full_transposed, n + 1)
                dve.wait_ge(xd_in[s], 16 * (i + 1))
                if later(i):
                    dve.wait_ge(normed_ready, n - 1)
                nc.vector.tensor_tensor(sides[s][:, TILES:, :].rearrange("p k f -> p (k f)"), ps_full[s][:, :], xd[s][:, :],
                                        ALU.add).then_inc(xt_ready, 1)
                dve.wait_ge(xt_ready, n + 1)
                for k in range(TILES, SIDES):
                    ins = nc.vector.bn_stats(stats[s][:, k, :], sides[s][:, k, :])
                ins.then_inc(stats_ready, 1)
                hold(dve, go, stats_ready, n + 1)
                for k in range(SIDES):
                    ins = nc.vector.bn_aggr(mean_var[s][:, k, :], stats[s][:, k, :])
                ins.then_inc(mean_var_ready, 1)
                dve.wait_ge(std_ready, n + 1)
                nc.vector.reciprocal(rstd[s][:, :], std[s][:, :]).then_inc(rstd_ready, 1)
                dve.wait_ge(rstd_ready, n + 1)
                nc.vector.scalar_tensor_tensor(shift[s][:, :], mean_var[s][:, :, 0], -1.0, rstd[s][:, :],
                                               ALU.mult, ALU.mult).then_inc(shift_ready, 1)
                dve.wait_ge(tanh_ready, n + 1)
                nc.vector.tensor_tensor(product[s][:, :, :].rearrange("p k f -> p (k f)"), tanh_sb[s][:, :],
                                        normed[s][:, TILES:, :].rearrange("p k f -> p (k f)"), ALU.mult).then_inc(product_ready, 1)
                hold(dve, go, product_ready, n + 1)
                nc.vector.tensor_reduce(scores[:, bass.ds(at(i, s) * TILES, TILES)], product[s][:, :, :], AX.X, ALU.add).then_inc(score_ready, 1)

            front_and_back(dve, rounds, front, back)

        @block.scalar
        def _(act):
            def edges(i, s):
                n = i * 2 + s
                act.wait_ge(mean_var_ready, n + 1)
                nc.scalar.activation(std[s][:, :], mean_var[s][:, :, 1], ACT.Sqrt, bias=eps_col[:, :]).then_inc(std_ready, 1)
                act.wait_ge(shift_ready, n + 1)
                if later(i):
                    act.wait_ge(arg_summed, n - 1)
                    act.wait_ge(product_ready, n - 1)
                    act.wait_ge(et_stored[s], 16 * i)
                for k in range(SIDES):
                    ins = nc.scalar.activation(normed[s][:, k, :], sides[s][:, k, :], ACT.Relu,
                                               bias=shift[s][:, k:k + 1], scale=rstd[s][:, k:k + 1])
                ins.then_inc(normed_ready, 1)
                act.wait_ge(arg_summed, n + 1)
                nc.scalar.activation(tanh_sb[s][:, :], ps_arg[s][:, :], ACT.Tanh).then_inc(tanh_ready, 1)

            edges(0, 0)
            edges(0, 1)
            with act.Fori(1, rounds) as i:
                edges(i, 0)
                edges(i, 1)

        @block.tensor
        def _(pe):
            def front(i, s):
                n = i * 2 + s
                pe.wait_ge(full_ready, n + 1)
                if later(i):
                    pe.wait_ge(xt_ready, n - 1)
                for k in range(TILES):
                    ins = nc.tensor.transpose(ps_full[s][:, k * P:(k + 1) * P], full[s][:, k * P:(k + 1) * P], ident[:, :])
                ins.then_inc(full_transposed, 1)

            def back(i, s):
                n = i * 2 + s
                pe.wait_ge(normed_ready, n + 1)
                pe.wait_ge(onehot_ready, n + 1)
                if later(i):
                    pe.wait_ge(tanh_ready, n - 1)
                nc.tensor.matmul(ps_arg[s][:, :], ident[:, :], normed[s][:, :TILES, :].rearrange("p k f -> p (k f)"),
                                 start=True, stop=False)
                for k in range(TILES):
                    ins = nc.tensor.matmul(ps_arg[s][:, k * P:(k + 1) * P], onehot[s][:, k * P:(k + 1) * P], rel_sb[:, :],
                                           start=False, stop=k == TILES - 1)
                ins.then_inc(arg_summed, 1)

            pe.wait_ge(rel_in, 16)
            front_and_back(pe, rounds, front, back)


def softmax_pass(nc, consts, *, scores, weights, dst_all, edges_padded_from):
    ctx = ExitStack()
    with ctx:
        ctx.enter_context(nc.cleanup_on_exit())
        n = scores.shape[1]
        dst_sb = ctx.enter_context(nc.sbuf_tensor("sm_dst", [P, n], I32))
        pad = ctx.enter_context(nc.sbuf_tensor("sm_pad", [P, n], F32))
        masked = ctx.enter_context(nc.sbuf_tensor("sm_masked", [P, n], F32))
        largest = ctx.enter_context(nc.sbuf_tensor("sm_largest", [P, 1], F32))
        largest_one = ctx.enter_context(nc.sbuf_tensor("sm_largest_one", [1, 1], F32))
        as_row, on_all = consts["banks"][0][0:1, :P], consts["banks"][1][:, 0:1]
        minus_largest = ctx.enter_context(nc.sbuf_tensor("sm_minus_largest", [P, 1], F32))
        dst_in = nc.alloc_semaphore("sm_dst_in")
        masked_ready = nc.alloc_semaphore("sm_masked_ready")
        largest_ready = nc.alloc_semaphore("sm_largest_ready")
        row_ready = nc.alloc_semaphore("sm_row_ready")
        all_ready = nc.alloc_semaphore("sm_all_ready")
        minus_ready = nc.alloc_semaphore("sm_minus_ready")
        weights_ready = nc.alloc_semaphore("sm_weights_ready")
        go = consts["go"]
        block = ctx.enter_context(nc.Block())

        @block.sync
        def _(sp):
            sp.dma_start(dst_sb[:, :], dst_all).then_inc(dst_in, 16)

        @block.vector
        def _(dve):
            dve.wait_ge(dst_in, 16)
            nc.vector.tensor_scalar(pad[:, :], dst_sb[:, :], float(edges_padded_from), -HUGE, ALU.is_ge, ALU.mult).then_inc(masked_ready, 1)
            dve.wait_ge(masked_ready, 1)
            nc.vector.tensor_tensor(masked[:, :], scores[:, :], pad[:, :], ALU.add).then_inc(masked_ready, 1)
            dve.wait_ge(masked_ready, 2)
            nc.vector.tensor_reduce(largest[:, :], masked[:, :], AX.X, ALU.max).then_inc(largest_ready, 1)
            dve.wait_ge(row_ready, 1)
            nc.vector.tensor_reduce(largest_one[:, :], as_row[:, :], AX.X, ALU.max).then_inc(largest_ready, 1)
            dve.wait_ge(all_ready, 1)
            nc.vector.tensor_scalar(minus_largest[:, :], on_all[:, :], -1.0, None, ALU.mult).then_inc(minus_ready, 1)

        @block.tensor
        def _(pe):
            pe.wait_ge(largest_ready, 1)
            nc.tensor.transpose(as_row[:, :], largest[:, :], consts["ident"][:, :]).then_inc(row_ready, 1)
            pe.wait_ge(largest_ready, 2)
            nc.tensor.matmul(on_all[:, :], consts["ones"][0:1, 0, :P], largest_one[:, :], start=True, stop=True).then_inc(all_ready, 1)

        @block.scalar
        def _(act):
            act.wait_ge(minus_ready, 1)
            nc.scalar.activation(weights[:, :], masked[:, :], ACT.Exp, bias=minus_largest[:, :]).then_inc(weights_ready, 1)


def sum_pass(nc, consts, *, cols, src_row, et_stream, sums_table, weights, windows):
    rounds = windows // 2
    ctx = ExitStack()
    with ctx:
        ctx.enter_context(nc.cleanup_on_exit())
        banks = consts["banks"]

        def sb(name, shape, dt=F32):
            return ctx.enter_context(nc.sbuf_tensor(f"sum_{name}", shape, dt))

        def sem(name):
            return nc.alloc_semaphore(f"sum_{name}")

        later_mask, spare_rows = consts["later_mask"], consts["spare_rows"]
        src_cols = [sb(f"src_cols{s}", [P, TILES], I32) for s in (0, 1)]
        src_f = [sb(f"src_f{s}", [P, TILES]) for s in (0, 1)]
        srow = [sb(f"srow{s}", [P, WIN], I32) for s in (0, 1)]
        et = [sb(f"et{s}", [P, TILES, SUM_W]) for s in (0, 1)]
        wcol = [sb(f"wcol{s}", [P, TILES]) for s in (0, 1)]
        weighted = [sb(f"weighted{s}", [P, TILES, SUM_W]) for s in (0, 1)]
        equal = [sb(f"equal{s}", [P, TILES, WIN]) for s in (0, 1)]
        scrap = [sb(f"scrap{s}", [P, TILES, WIN], mybir.dt.bfloat16) for s in (0, 1)]
        n_later = [sb(f"n_later{s}", [P, TILES]) for s in (0, 1)]
        has_later = [sb(f"has_later{s}", [P, TILES]) for s in (0, 1)]
        to_spare = [sb(f"to_spare{s}", [P, TILES]) for s in (0, 1)]
        move = [sb(f"move{s}", [P, TILES]) for s in (0, 1)]
        scatter_idx = [sb(f"scatter_idx{s}", [P, TILES], I32) for s in (0, 1)]
        summed = [sb(f"summed{s}", [P, TILES, SUM_W]) for s in (0, 1)]
        ps_sum = [[t[:, :2 * SUM_W].rearrange("p (k f) -> p k f", k=2) for t in pair] for pair in (banks[0:2], banks[2:4])]

        ones_ready = sem("ones_ready")
        cols_in = [sem(f"cols_in{s}") for s in (0, 1)]
        srow_in = [sem(f"srow_in{s}") for s in (0, 1)]
        et_in = [sem(f"et_in{s}") for s in (0, 1)]
        scattered = sem("scattered")
        src_f_ready, wcol_ready, weighted_ready, equal_ready = sem("src_f_ready"), sem("wcol_ready"), sem("weighted_ready"), sem("equal_ready")
        n_later_ready, spare_ready, move_ready, idx_ready = sem("n_later_ready"), sem("spare_ready"), sem("move_ready"), sem("idx_ready")
        sums_made, summed_ready = sem("sums_made"), sem("summed_ready")

        go = consts["go"]
        block = ctx.enter_context(nc.Block())

        @block.sync
        def _(sp):
            sp.wait_ge(ones_ready, 2)

            def load(i, s):
                n = i * 2 + s
                if later(i):
                    hold(sp, go, idx_ready, n - 1)
                    hold(sp, go, equal_ready, n - 1)
                sp.dma_start(src_cols[s][:, :], window(cols, n)[:, :TILES]).then_inc(cols_in[s], 16)
                if later(i):
                    hold(sp, go, n_later_ready, n - 1)
                sp.dma_start(srow[s][:, :], window(src_row, n).to_broadcast([P, WIN])).then_inc(srow_in[s], 16)
                if later(i):
                    hold(sp, go, weighted_ready, n - 1)
                sp.dma_start(et[s][:, :, :P], window(et_stream, n).rearrange("p (k f) -> p k f", k=TILES)).then_inc(et_in[s], 16)

            load(0, 0)
            load(0, 1)
            with sp.Fori(1, rounds) as i:
                load(i, 0)
                load(i, 1)

        @block.vector
        def _(dve):
            for s in (0, 1):
                nc.vector.memset(et[s][:, :, P:], 1.0).then_inc(ones_ready, 1)

            def edges(i, s):
                n = i * 2 + s
                dve.wait_ge(cols_in[s], 16 * (i + 1))
                nc.vector.tensor_copy(src_f[s][:, :], src_cols[s][:, :]).then_inc(src_f_ready, 1)
                nc.vector.tensor_copy(wcol[s][:, :], weights[:, bass.ds(n * TILES, TILES)]).then_inc(wcol_ready, 1)
                dve.wait_ge(srow_in[s], 16 * (i + 1))
                dve.wait_ge(src_f_ready, n + 1)
                if later(i):
                    dve.wait_ge(sums_made, n - 1)
                for k in range(TILES):
                    ins = nc.vector.tensor_scalar(equal[s][:, k, :], srow[s][:, :], src_f[s][:, k:k + 1], None, ALU.is_equal)
                ins.then_inc(equal_ready, 1)
                dve.wait_ge(et_in[s], 16 * (i + 1))
                dve.wait_ge(wcol_ready, n + 1)
                nc.vector.tensor_tensor(weighted[s][:, :, :], et[s][:, :, :],
                                        wcol[s][:, :].unsqueeze(2).to_broadcast([P, TILES, SUM_W]), ALU.mult).then_inc(weighted_ready, 1)
                dve.wait_ge(equal_ready, n + 1)
                for k in range(TILES):
                    ins = nc.vector.scalar_tensor_tensor(scrap[s][:, k, :], srow[s][:, :], src_f[s][:, k:k + 1], later_mask[:, k, :],
                                                         ALU.is_equal, ALU.mult, accum_out=n_later[s][:, k:k + 1])
                ins.then_inc(n_later_ready, 1)
                nc.vector.tensor_tensor(to_spare[s][:, :], spare_rows[:, :], src_f[s][:, :], ALU.subtract).then_inc(spare_ready, 1)
                dve.wait_ge(n_later_ready, n + 1)
                dve.wait_ge(spare_ready, n + 1)
                nc.vector.scalar_tensor_tensor(move[s][:, :], n_later[s][:, :], 0.0, to_spare[s][:, :],
                                               ALU.is_gt, ALU.mult).then_inc(move_ready, 1)
                dve.wait_ge(move_ready, n + 1)
                if later(i):
                    dve.wait_ge(scattered, 16 * TILES * (n - 1))
                nc.vector.tensor_tensor(scatter_idx[s][:, :], move[s][:, :], src_f[s][:, :], ALU.add).then_inc(idx_ready, 1)

            edges(0, 0)
            edges(0, 1)
            with dve.Fori(1, rounds) as i:
                edges(i, 0)
                edges(i, 1)

        @block.tensor
        def _(pe):
            def sums(i, s):
                n = i * 2 + s
                pe.wait_ge(equal_ready, n + 1)
                pe.wait_ge(weighted_ready, n + 1)
                if later(i):
                    pe.wait_ge(summed_ready, n - 1)
                for a in range(TILES):
                    for b in range(TILES):
                        ins = nc.tensor.matmul(ps_sum[s][a // 2][:, a % 2, :], equal[s][:, b, a * P:(a + 1) * P],
                                               weighted[s][:, b, :], start=b == 0, stop=b == TILES - 1)
                ins.then_inc(sums_made, 1)

            sums(0, 0)
            sums(0, 1)
            with pe.Fori(1, rounds) as i:
                sums(i, 0)
                sums(i, 1)

        @block.scalar
        def _(act):
            def move_out(i, s):
                n = i * 2 + s
                act.wait_ge(sums_made, n + 1)
                if later(i):
                    act.wait_ge(scattered, 16 * TILES * (n - 1))
                nc.scalar.copy(summed[s][:, 0:2, :], ps_sum[s][0])
                nc.scalar.copy(summed[s][:, 2:4, :], ps_sum[s][1]).then_inc(summed_ready, 1)

            move_out(0, 0)
            move_out(0, 1)
            with act.Fori(1, rounds) as i:
                move_out(i, 0)
                move_out(i, 1)

        @block.gpsimd
        def _(pool):
            def scatter(i, s):
                n = i * 2 + s
                hold(pool, go, idx_ready, n + 1)
                hold(pool, go, summed_ready, n + 1)
                if later(i) or s:
                    hold(pool, go, scattered, 16 * TILES * n)
                for k in range(TILES):
                    pool.indirect_dma_start(
                        sums_table[:, :], bass.IndirectOffsetOnAxis(ap=scatter_idx[s][:, k:k + 1], axis=0),
                        summed[s][:, k, :], None, compute_op=ALU.add).then_inc(scattered, 16)

            scatter(0, 0)
            scatter(0, 1)
            with pool.Fori(1, rounds) as i:
                scatter(i, 0)
                scatter(i, 1)
            pool.wait_ge(scattered, 16 * TILES * windows)


def node_pass(nc, consts, *, x1_table, sums_table, wt, out, nodes):
    rows = P * PIECE
    full_pieces = nodes // rows
    tail = (nodes - full_pieces * rows) // PIECE
    pieces = full_pieces + (1 if tail else 0)
    assert tail * PIECE == nodes - full_pieces * rows and full_pieces % 2
    rounds = full_pieces // 2
    HALVES = PIECE // TILES
    ctx = ExitStack()
    with ctx:
        ctx.enter_context(nc.cleanup_on_exit())
        banks = consts["banks"]

        def sb(name, shape, dt=F32):
            return ctx.enter_context(nc.sbuf_tensor(f"n_{name}", shape, dt))

        def sem(name):
            return nc.alloc_semaphore(f"n_{name}")

        ident, eps_col = consts["ident"], consts["eps"]
        wt_sb = sb("wt", [P, P])
        x1 = [sb(f"x1{s}", [P, PIECE, P]) for s in (0, 1)]
        sums = [sb(f"sums{s}", [P, PIECE, SUM_W]) for s in (0, 1)]
        stats = [sb(f"stats{s}", [P, PIECE, 6]) for s in (0, 1)]
        mean_var = [sb(f"mean_var{s}", [P, PIECE, 2]) for s in (0, 1)]
        std = [sb(f"std{s}", [P, PIECE]) for s in (0, 1)]
        rstd = [sb(f"rstd{s}", [P, PIECE]) for s in (0, 1)]
        shift = [sb(f"shift{s}", [P, PIECE]) for s in (0, 1)]
        weight = [sb(f"weight{s}", [P, PIECE]) for s in (0, 1)]
        rweight = [sb(f"rweight{s}", [P, PIECE]) for s in (0, 1)]
        h = [sb(f"h{s}", [P, PIECE, P]) for s in (0, 1)]
        with_agg = [sb(f"with_agg{s}", [P, PIECE, P]) for s in (0, 1)]
        transposed = [sb(f"transposed{s}", [P, PIECE, P]) for s in (0, 1)]
        fifth = [sb(f"fifth{s}", [P, PIECE, P]) for s in (0, 1)]
        leaky = [sb(f"leaky{s}", [P, PIECE, P]) for s in (0, 1)]
        result = [sb(f"result{s}", [P, PIECE, P]) for s in (0, 1)]
        by_tile = [t[:, :].rearrange("p (k f) -> p k f", k=TILES) for t in banks]
        ps_t, ps_o = (by_tile[0:2], by_tile[2:4]), (by_tile[4:6], by_tile[6:8])

        wt_in = sem("wt_in")
        x1_in = [sem(f"x1_in{s}") for s in (0, 1)]
        sums_in = [sem(f"sums_in{s}") for s in (0, 1)]
        stored = [sem(f"stored{s}") for s in (0, 1)]
        stats_ready, mean_var_ready, std_ready, rstd_ready, shift_ready = (
            sem("stats_ready"), sem("mean_var_ready"), sem("std_ready"), sem("rstd_ready"), sem("shift_ready"))
        weight_ready, rweight_ready, h_ready, with_agg_ready = sem("weight_ready"), sem("rweight_ready"), sem("h_ready"), sem("with_agg_ready")
        turned, transposed_ready, multiplied = sem("turned"), sem("transposed_ready"), sem("multiplied")
        fifth_ready, leaky_ready, result_ready = sem("fifth_ready"), sem("leaky_ready"), sem("result_ready")

        go = consts["go"]
        block = ctx.enter_context(nc.Block())

        def piece(table, n, parts):
            return table[bass.ds(n * rows, parts * PIECE), :].rearrange("(p j) f -> p j f", j=PIECE)

        def in_order(eng, step):
            step(0, 0, P)
            step(0, 1, P)
            with eng.Fori(1, rounds) as i:
                step(i, 0, P)
                step(i, 1, P)
            step(rounds, 0, P)
            if tail:
                step(rounds, 1, tail)

        def staggered(eng, front, back):
            front(0, 0, P)
            front(0, 1, P)
            back(0, 0, P)
            front(1, 0, P)
            back(0, 1, P)
            front(1, 1, P)
            back(1, 0, P)
            with eng.Fori(2, rounds) as i:
                front(i, 0, P)
                back(i - 1, 1, P)
                front(i, 1, P)
                back(i, 0, P)
            front(rounds, 0, P)
            back(rounds - 1, 1, P)
            if tail:
                front(rounds, 1, tail)
            back(rounds, 0, P)
            if tail:
                back(rounds, 1, tail)

        @block.sync
        def _(sp):
            sp.dma_start(wt_sb[:, :], wt).then_inc(wt_in, 16)

            def load(i, s, parts):
                n = i * 2 + s
                if later(i):
                    hold(sp, go, result_ready, n - 1)
                sp.dma_start(x1[s][:parts, :, :], piece(x1_table, n, parts)).then_inc(x1_in[s], 16)
                if later(i):
                    hold(sp, go, with_agg_ready, n - 1)
                sp.dma_start(sums[s][:parts, :, :], piece(sums_table, n, parts)).then_inc(sums_in[s], 16)

            in_order(sp, load)

        @block.gpsimd
        def _(pool):
            def finish(i, s, parts):
                n = i * 2 + s
                hold(pool, go, leaky_ready, n + 1)
                if later(i):
                    hold(pool, go, stored[s], 16 * i)
                nc.gpsimd.tensor_tensor(result[s][:parts, :, :], leaky[s][:parts, :, :], x1[s][:parts, :, :], ALU.add).then_inc(result_ready, 1)
                hold(pool, go, result_ready, n + 1)
                pool.dma_start(piece(out, n, parts), result[s][:parts, :, :]).then_inc(stored[s], 16)

            in_order(pool, finish)
            pool.wait_ge(stored[0], 16 * (rounds + 1))
            pool.wait_ge(stored[1], 16 * (pieces - rounds - 1))

        @block.vector
        def _(dve):
            def front(i, s, parts):
                n = i * 2 + s
                dve.wait_ge(x1_in[s], 16 * (i + 1))
                for k in range(PIECE):
                    ins = nc.vector.bn_stats(stats[s][:parts, k, :], x1[s][:parts, k, :])
                ins.then_inc(stats_ready, 1)
                dve.wait_ge(sums_in[s], 16 * (i + 1))
                nc.vector.tensor_scalar(weight[s][:parts, :], sums[s][:parts, :, P], 1e-10, None, ALU.add).then_inc(weight_ready, 1)
                hold(dve, go, stats_ready, n + 1)
                for k in range(PIECE):
                    ins = nc.vector.bn_aggr(mean_var[s][:parts, k, :], stats[s][:parts, k, :])
                ins.then_inc(mean_var_ready, 1)
                dve.wait_ge(weight_ready, n + 1)
                nc.vector.reciprocal(rweight[s][:parts, :], weight[s][:parts, :]).then_inc(rweight_ready, 1)
                dve.wait_ge(std_ready, n + 1)
                nc.vector.reciprocal(rstd[s][:parts, :], std[s][:parts, :]).then_inc(rstd_ready, 1)
                dve.wait_ge(rstd_ready, n + 1)
                nc.vector.scalar_tensor_tensor(shift[s][:parts, :], mean_var[s][:parts, :, 0], -1.0, rstd[s][:parts, :],
                                               ALU.mult, ALU.mult).then_inc(shift_ready, 1)

            def back(i, s, parts):
                n = i * 2 + s
                dve.wait_ge(h_ready, n + 1)
                dve.wait_ge(rweight_ready, n + 1)
                if later(i):
                    dve.wait_ge(turned, n - 1)
                for k in range(PIECE):
                    ins = nc.vector.scalar_tensor_tensor(with_agg[s][:parts, k, :], sums[s][:parts, k, :P], rweight[s][:parts, k:k + 1],
                                                         h[s][:parts, k, :], ALU.mult, ALU.add)
                ins.then_inc(with_agg_ready, 1)
                dve.wait_ge(fifth_ready, n + 1)
                if later(i):
                    dve.wait_ge(result_ready, n - 1)
                for b in range(HALVES):
                    ins = nc.vector.tensor_tensor(leaky[s][:parts, b * TILES:(b + 1) * TILES, :], ps_o[s][b][:parts, :, :],
                                                  fifth[s][:parts, b * TILES:(b + 1) * TILES, :], ALU.max)
                ins.then_inc(leaky_ready, 1)

            staggered(dve, front, back)

        @block.scalar
        def _(act):
            def front(i, s, parts):
                n = i * 2 + s
                act.wait_ge(mean_var_ready, n + 1)
                nc.scalar.activation(std[s][:parts, :], mean_var[s][:parts, :, 1], ACT.Sqrt, bias=eps_col[:parts, :]).then_inc(std_ready, 1)
                act.wait_ge(shift_ready, n + 1)
                if later(i):
                    act.wait_ge(with_agg_ready, n - 1)
                for k in range(PIECE):
                    ins = nc.scalar.activation(h[s][:parts, k, :], x1[s][:parts, k, :], ACT.Relu,
                                               bias=shift[s][:parts, k:k + 1], scale=rstd[s][:parts, k:k + 1])
                ins.then_inc(h_ready, 1)

            def back(i, s, parts):
                n = i * 2 + s
                act.wait_ge(turned, n + 1)
                if later(i):
                    act.wait_ge(multiplied, n - 1)
                for b in range(HALVES):
                    ins = nc.scalar.copy(transposed[s][:, b * TILES:(b + 1) * TILES, :parts], ps_t[s][b][:, :, :parts])
                ins.then_inc(transposed_ready, 1)
                act.wait_ge(multiplied, n + 1)
                if later(i):
                    act.wait_ge(leaky_ready, n - 1)
                for b in range(HALVES):
                    ins = nc.scalar.mul(fifth[s][:parts, b * TILES:(b + 1) * TILES, :], ps_o[s][b][:parts, :, :], 0.2)
                ins.then_inc(fifth_ready, 1)

            staggered(act, front, back)

        @block.tensor
        def _(pe):
            pe.wait_ge(wt_in, 16)

            def both(i, s, parts):
                n = i * 2 + s
                pe.wait_ge(with_agg_ready, n + 1)
                if later(i):
                    pe.wait_ge(transposed_ready, n - 1)
                for k in range(PIECE):
                    ins = nc.tensor.transpose(ps_t[s][k // TILES][:, k % TILES, :parts], with_agg[s][:parts, k, :], ident[:parts, :parts])
                ins.then_inc(turned, 1)
                pe.wait_ge(transposed_ready, n + 1)
                if later(i):
                    pe.wait_ge(leaky_ready, n - 1)
                for k in range(PIECE):
                    ins = nc.tensor.matmul(ps_o[s][k // TILES][:parts, k % TILES, :], transposed[s][:, k, :parts], wt_sb[:, :],
                                           start=True, stop=True)
                ins.then_inc(multiplied, 1)

            in_order(pe, both)


def build(nc, x, cols, dst_row, src_row, type_row, dst_all, conv, rel, wt, out):
    nodes = x.shape[0]
    windows = cols.shape[0]
    assert windows % 2 == 0
    table_rows = -(-(nodes + 1) // (P * PIECE)) * P * PIECE
    pieces = table_rows // (P * PIECE)
    assert pieces == windows
    node_piece = nodes // windows
    node_tail = nodes - node_piece * windows

    def dram(name, shape):
        return nc.dram_tensor(name, shape, F32, kind="Internal").ap()

    table2, table3, x1_table = (dram(n, (table_rows, P)) for n in ("table2", "table3", "x1_table"))
    sums_table = dram("sums_table", (table_rows + WIN, SUM_W))
    f1, f2, f3, xd_stream, et_stream = (dram(n, (windows, P, WIN)) for n in ("f1", "f2", "f3", "xd_stream", "et_stream"))

    ctx = ExitStack()
    with ctx:
        def sb(name, shape, dt=F32):
            return ctx.enter_context(nc.sbuf_tensor(name, shape, dt))

        zeros = sb("zeros", [P, PIECE * SUM_W])
        ones = sb("ones", [P, TILES, WIN])
        ident = sb("ident", [P, P])
        eps_col = sb("eps_col", [P, 1])
        later_mask = sb("later_mask", [P, TILES, WIN])
        spare_i, spare_rows = sb("spare_i", [P, TILES], I32), sb("spare_rows", [P, TILES])
        relation_i, relation_col = sb("relation_i", [RELATIONS, 1], I32), sb("relation_col", [RELATIONS, 1])
        scores = sb("scores", [P, windows * TILES])
        weights = sb("weights", [P, windows * TILES])
        go = ctx.enter_context(nc.semaphore("set_up"))
        banks = [ctx.enter_context(nc.psum_tensor(f"bank{b}", [P, WIN], F32)) for b in range(8)]
        consts = {"banks": banks, "go": go, "ident": ident, "ones": ones, "eps": eps_col, "later_mask": later_mask, "spare_rows": spare_rows,
                  "relation_col": relation_col}

        def clear(sp, table, n, width, sem):
            sp.dma_start(table[bass.ds(n * (P * PIECE), P * PIECE), :].rearrange("(p j) f -> p (j f)", j=PIECE),
                         zeros[:, :PIECE * width]).then_inc(sem, 16)

        with ExitStack() as setup:
            zeros_ready, memset_done = ctx.enter_context(nc.semaphore("zeros_ready")), ctx.enter_context(nc.semaphore("memset_done"))
            iota_done, cleared = ctx.enter_context(nc.semaphore("iota_done")), ctx.enter_context(nc.semaphore("cleared"))
            const_done = ctx.enter_context(nc.semaphore("const_done"))
            block = setup.enter_context(nc.Block())

            @block.gpsimd
            def _(pool):
                nc.gpsimd.memset(ones[:, :, :], 1.0).then_inc(memset_done, 1)
                nc.gpsimd.iota(spare_i[:, :], [[P, TILES]], base=table_rows, channel_multiplier=1).then_inc(iota_done, 1)
                nc.gpsimd.iota(relation_i[:, :], [[0, 1]], base=0, channel_multiplier=1).then_inc(iota_done, 1)
                pool.wait_ge(memset_done, 1)
                nc.gpsimd.affine_select(ident[:, :], ones[:, 0, :P], [[-1, P]], ALU.is_equal, 0.0, base=0, channel_multiplier=1)
                nc.gpsimd.affine_select(later_mask[:, :, :], ones[:, :, :], [[-P, TILES], [1, WIN]], ALU.is_gt, 0.0,
                                        base=0, channel_multiplier=-1)

            @block.vector
            def _(dve):
                nc.vector.memset(zeros[:, :], 0.0).then_inc(zeros_ready, 1)
                nc.vector.memset(eps_col[:, :], EPS).then_inc(go, 1)
                dve.wait_ge(iota_done, 2)
                nc.vector.tensor_copy(spare_rows[:, :], spare_i[:, :])
                nc.vector.tensor_copy(relation_col[:, :], relation_i[:, :]).then_inc(const_done, 1)

            @block.sync
            def _(sp):
                sp.wait_ge(zeros_ready, 1)
                with sp.Fori(0, pieces) as n:
                    clear(sp, table2, n, P, cleared)
                sp.dma_start(x1_table[nodes - node_tail:nodes, :], x[nodes - node_tail:nodes, :]).then_inc(cleared, 16)
                spare = (table_rows - nodes) // PIECE
                sp.dma_start(x1_table[nodes:nodes + spare * PIECE, :].rearrange("(p j) f -> p (j f)", j=PIECE),
                             zeros[:spare, :PIECE * P]).then_inc(cleared, 16)
                sp.dma_start(sums_table[table_rows:, :].rearrange("(p j) f -> p (j f)", j=TILES), zeros[:, :TILES * SUM_W]).then_inc(cleared, 16)
                sp.wait_ge(cleared, 16 * (pieces + 3))

        def copy_x(sp, n, sem):
            size = node_piece * P // 16
            sp.dma_start(x1_table[bass.ds(n * node_piece, node_piece), :].rearrange("r f -> (r f)").rearrange("(a b) -> a b", b=size),
                         x[bass.ds(n * node_piece, node_piece), :].rearrange("r f -> (r f)").rearrange("(a b) -> a b", b=size)).then_inc(sem, 16)

        shared = dict(cols=cols, dst_row=dst_row, xd_stream=xd_stream, windows=windows)
        edge_conv_pass(nc, "c1", consts, first=True, last=False, table_in=None, x_rows=x, table_out=table2, f_in=None, f_out=f1,
                       weights=conv[0], bulk=lambda sp, n, sem: clear(sp, table3, n, P, sem), **shared)
        edge_conv_pass(nc, "c2", consts, first=False, last=False, table_in=table2, x_rows=None, table_out=table3, f_in=f1, f_out=f2,
                       weights=conv[1], bulk=lambda sp, n, sem: copy_x(sp, n, sem), **shared)
        edge_conv_pass(nc, "c3", consts, first=False, last=True, table_in=table3, x_rows=None, table_out=x1_table, f_in=f2, f_out=f3,
                       weights=conv[2], bulk=lambda sp, n, sem: clear(sp, sums_table, n, SUM_W, sem), **shared)
        score_pass(nc, consts, type_row=type_row, x1_table=x1_table, f_in=f3, et_stream=et_stream, rel=rel, scores=scores, **shared)
        softmax_pass(nc, consts, scores=scores, weights=weights, dst_all=dst_all, edges_padded_from=nodes)
        sum_pass(nc, consts, cols=cols, src_row=src_row, et_stream=et_stream, sums_table=sums_table, weights=weights, windows=windows)
        node_pass(nc, consts, x1_table=x1_table, sums_table=sums_table, wt=wt, out=out, nodes=nodes)


def kernel(x, src, dst, edge_type_64, **p):
    import numpy as np
    import concourse.bacc as bacc
    from concourse.bass_utils import run_bass_kernel_spmd as run

    x, src, dst, kinds = (np.asarray(a) for a in (x, src, dst, edge_type_64))
    nodes, edges = x.shape[0], src.shape[0]
    windows = -(-edges // WIN)
    windows += windows % 2
    padded = windows * WIN

    def pad(a, fill):
        return np.concatenate([a, np.full((padded - edges,), fill, a.dtype)])

    def columns(a):
        return a.reshape(windows, TILES, P).transpose(0, 2, 1)

    src_p, dst_g, dst_p, kind_p = pad(src, 0), pad(dst, 0), pad(dst, nodes), pad(kinds, 0)
    none = np.full((1,), -1, dst.dtype)
    around = np.concatenate([none, dst_p, none])
    arrays = {
        "x": x,
        "cols": np.ascontiguousarray(np.concatenate(
            [columns(a) for a in (src_p, dst_g, dst_p, around[2:], around[:-2])], axis=2)),
        "dst_row": np.stack([around[w * WIN:w * WIN + WIN + 2] for w in range(windows)]).reshape(windows, 1, WIN + 2),
        "src_row": src_p.reshape(windows, 1, WIN),
        "type_row": kind_p.reshape(windows, 1, WIN),
        "dst_all": np.ascontiguousarray(columns(dst_p).transpose(1, 0, 2).reshape(P, windows * TILES)),
        "rel": np.asarray(p["L1_gnn_rel_embed_weight"]),
        "wt": np.ascontiguousarray(np.asarray(p["L1_gnn_W"]).T),
    }
    for layer in ("in", "hid", "out"):
        arrays[f"W1_{layer}"] = np.asarray(p[f"L0_gnn_W1_{layer}"])
        arrays[f"W2_{layer}"] = np.asarray(p[f"L0_gnn_W2_{layer}"])
        arrays[f"b1_{layer}"] = np.asarray(p[f"L0_gnn_b1_{layer}"]).reshape(P, 1)
        arrays[f"b2_{layer}"] = np.asarray(p[f"L0_gnn_b2_{layer}"]).reshape(P, 1)

    nc = bacc.Bacc("TRN2", target_bir_lowering=False, num_devices=1)
    ap = {n: nc.dram_tensor(n, a.shape, mybir.dt.from_np(a.dtype), kind="ExternalInput").ap() for n, a in arrays.items()}
    out = nc.dram_tensor("out", x.shape, F32, kind="ExternalOutput").ap()
    conv = [{k: ap[f"{k}_{layer}"] for k in ("W1", "W2", "b1", "b2")} for layer in ("in", "hid", "out")]
    build(nc, ap["x"], ap["cols"], ap["dst_row"], ap["src_row"], ap["type_row"], ap["dst_all"], conv, ap["rel"], ap["wt"], out)
    return run(nc, [arrays], core_ids=[0]).results[0]["out"]
```

```python
import concourse.bass as bass
from concourse import mybir
from contextlib import ExitStack

F32 = mybir.dt.float32
I32 = mybir.dt.int32
ALU = mybir.AluOpType
ACT = mybir.ActivationFunctionType
AX = mybir.AxisListType

P = 128
TILES = 4
WIN = TILES * P
PIECE = 8
SUM_W = P + 4
SKIP = float(1 << 20)
HUGE = 3.0e38
EPS = 1e-5
RELATIONS = 64


def window(ap, w):
    return ap[bass.ds(w, 1)].rearrange("o p n -> (o p) n")


def hold(eng, go, sem, value):
    if not isinstance(value, int):
        value = eng.to_reg(value)
        eng.wait_ge(go, 1)
    eng.wait_ge(sem, value)


def later(i):
    return not isinstance(i, int) or i > 0


def in_steps(eng, count, unroll, *stages):
    deepest = max(lag for _, lag in stages)
    peeled = 1 + -(-deepest // unroll)

    def step(i, s):
        for stage, lag in stages:
            r, t = i + (s - lag) // unroll, (s - lag) % unroll
            if not isinstance(i, int) or 0 <= r * unroll + t < count:
                stage(r, t)

    for n in range(peeled * unroll):
        step(n // unroll, n % unroll)
    with eng.Fori(peeled, count // unroll) as i:
        for s in range(unroll):
            step(i, s)
    for n in range(count // unroll * unroll, count + deepest):
        step(n // unroll, n % unroll)


def edge_conv_pass(nc, tag, consts, *, first, last, dst_row, table_in, x_rows, table_out, f_in, f_out,
                   xd_stream, weights, windows, bulk):
    backward = not first and not last
    rounds = windows // 2
    gathers = 2 * TILES if first else TILES
    ctx = ExitStack()
    with ctx:
        ctx.enter_context(nc.cleanup_on_exit())
        banks = consts["banks"]

        def sb(name, shape, dt=F32):
            return ctx.enter_context(nc.sbuf_tensor(f"{tag}_{name}", shape, dt))

        def sem(name):
            return nc.alloc_semaphore(f"{tag}_{name}")

        ident, eps_col = consts["ident"], consts["eps"]
        w1a, w1b, wd, w2 = sb("w1a", [P, P]), sb("w1b", [P, P]), sb("wd", [P, P]), sb("w2", [P, P])
        b1, b2 = sb("b1", [P, 1]), sb("b2", [P, 1])
        gather_idx = [sb(f"gather_idx{s}", [P, gathers], I32) for s in (0, 1)]
        drow = [sb(f"drow{s}", [P, WIN + 2], I32) for s in (0, 1)]
        rows_in = [sb(f"rows_in{s}", [P, gathers, P]) for s in (0, 1)]
        keep = [sb(f"keep{s}", [P, WIN]) for s in (0, 1)]
        xiT = [sb(f"xiT{s}", [P, WIN]) for s in (0, 1)]
        xjT = [sb(f"xjT{s}", [P, WIN]) for s in (0, 1)]
        hidden = [sb(f"hidden{s}", [P, WIN]) for s in (0, 1)]
        value = [sb(f"value{s}", [P, WIN]) for s in (0, 1)]
        segmax = [sb(f"segmax{s}", [P, WIN]) for s in (0, 1)]
        rows_out = [sb(f"rows_out{s}", [P, TILES, P]) for s in (0, 1)]
        scatter_idx = [sb(f"scatter_idx{s}", [P, TILES], I32) for s in (0, 1)]
        if first:
            stats = [sb(f"stats{s}", [P, gathers, 6]) for s in (0, 1)]
            mean_var = [sb(f"mean_var{s}", [P, gathers, 2]) for s in (0, 1)]
            std = [sb(f"std{s}", [P, gathers]) for s in (0, 1)]
            rstd = [sb(f"rstd{s}", [P, gathers]) for s in (0, 1)]
            shift = [sb(f"shift{s}", [P, gathers]) for s in (0, 1)]
            normed = [sb(f"normed{s}", [P, gathers, P]) for s in (0, 1)]
        else:
            scan_in = [sb(f"scan_in{s}", [P, WIN]) for s in (0, 1)]
        if last:
            penalty = [sb(f"penalty{s}", [P, WIN]) for s in (0, 1)]
            xd = [sb(f"xd{s}", [P, WIN]) for s in (0, 1)]
        ps_xj, ps_xi = banks[0:2], banks[2:4]
        ps_hidden, ps_value, ps_rows = banks[4:7]

        weights_in, wd_ready = sem("weights_in"), sem("wd_ready")
        drow_in = [sem(f"drow_in{s}") for s in (0, 1)]
        gathered = [sem(f"gathered{s}") for s in (0, 1)]
        scattered = [sem(f"scattered{s}") for s in (0, 1)]
        segmax_stored = [sem(f"segmax_stored{s}") for s in (0, 1)]
        if first:
            xd_stored = [sem(f"xd_stored{s}") for s in (0, 1)]
            stats_ready, mean_var_ready, std_ready = sem("stats_ready"), sem("mean_var_ready"), sem("std_ready")
            rstd_ready, shift_ready, normed_ready = sem("rstd_ready"), sem("shift_ready"), sem("normed_ready")
        else:
            scan_in_loaded = [sem(f"scan_in_loaded{s}") for s in (0, 1)]
            xi_ready = sem("xi_ready")
        if last:
            xd_in = [sem(f"xd_in{s}") for s in (0, 1)]
            penalty_ready = sem("penalty_ready")
        bulk_done = sem("bulk_done")
        gather_idx_ready, keep_ready = sem("gather_idx_ready"), sem("keep_ready")
        x_transposed, xT_ready = sem("x_transposed"), sem("xT_ready")
        hidden_summed, hidden_ready = sem("hidden_summed"), sem("hidden_ready")
        value_summed, value_ready = sem("value_summed"), sem("value_ready")
        segmax_ready, scatter_idx_ready = sem("segmax_ready"), sem("scatter_idx_ready")
        rows_transposed, rows_ready = sem("rows_transposed"), sem("rows_ready")

        def at(i, s):
            w = i * 2 + s
            return (windows - 1) - w if backward else w

        def run(t):
            return t[:, ::-1] if backward else t[:, :]

        def end(t):
            return t[:, 0:1] if backward else t[:, WIN - 1:WIN]

        go = consts["go"]
        block = ctx.enter_context(nc.Block())

        @block.sync
        def _(sp):
            for t, a in ((w1a, weights["W1"][0:P, :]), (w1b, weights["W1"][P:2 * P, :]), (w2, weights["W2"]),
                         (b1, weights["b1"]), (b2, weights["b2"])):
                sp.dma_start(t[:, :], a).then_inc(weights_in, 16)

            def load(i, s):
                n = i * 2 + s
                if later(i):
                    hold(sp, go, keep_ready, n - 1)
                sp.dma_start(drow[s][:, :], window(dst_row, at(i, s)).to_broadcast([P, WIN + 2])).then_inc(drow_in[s], 16)
                if not first:
                    if later(i):
                        hold(sp, go, xi_ready, n - 1)
                    sp.dma_start(scan_in[s][:, :], window(f_in, at(i, s))).then_inc(scan_in_loaded[s], 16)

            def load_xd(i, s):
                if later(i):
                    hold(sp, go, rows_ready, i * 2 + s - 1)
                sp.dma_start(xd[s][:, :], window(xd_stream, at(i, s))).then_inc(xd_in[s], 16)

            def store(i, s):
                n = i * 2 + s
                hold(sp, go, segmax_ready, n + 1)
                sp.dma_start(window(f_out, at(i, s)), segmax[s][:, :]).then_inc(segmax_stored[s], 16)
                bulk(sp, n, bulk_done)

            in_steps(sp, windows, 2, (load, 0), (store, 4), *([(load_xd, 2)] if last else []))
            for s in (0, 1):
                sp.wait_ge(segmax_stored[s], 16 * rounds)
                if first:
                    sp.wait_ge(xd_stored[s], 16 * rounds)
            sp.wait_ge(bulk_done, 16 * windows)

        @block.gpsimd
        def _(pool):
            def gather(i, s):
                n = i * 2 + s
                hold(pool, go, gather_idx_ready, n + 1)
                if later(i):
                    if first:
                        hold(pool, go, normed_ready, n - 1)
                        hold(pool, go, xd_stored[s], 16 * i)
                    else:
                        hold(pool, go, x_transposed, n - 1)
                for k in range(gathers):
                    pool.indirect_dma_start(
                        rows_in[s][:, k, :], None, (x_rows if first else table_in)[:, :],
                        bass.IndirectOffsetOnAxis(ap=gather_idx[s][:, k:k + 1], axis=0)).then_inc(gathered[s], 16)

            def scatter(i, s):
                n = i * 2 + s
                hold(pool, go, scatter_idx_ready, n + 1)
                hold(pool, go, rows_ready, n + 1)
                for k in range(TILES):
                    pool.indirect_dma_start(
                        table_out[:, :], bass.IndirectOffsetOnAxis(ap=scatter_idx[s][:, k:k + 1], axis=0),
                        rows_out[s][:, k, :], None,
                        bounds_check=table_out.shape[0] - 1, oob_is_err=False).then_inc(scattered[s], 16)

            in_steps(pool, windows, 2, (gather, 0), (scatter, 3))
            for s in (0, 1):
                pool.wait_ge(scattered[s], 16 * TILES * rounds)

        @block.vector
        def _(dve):
            dve.wait_ge(weights_in, 5 * 16)
            nc.vector.tensor_tensor(wd[:, :], w1a[:, :], w1b[:, :], ALU.subtract).then_inc(wd_ready, 1)

            def next_indices(i, s):
                n = i * 2 + s
                if later(i):
                    hold(dve, go, gathered[s], 16 * gathers * i)
                here = bass.ds(at(i, s) * TILES, TILES)
                ins = nc.vector.tensor_copy(gather_idx[s][:, :TILES], consts["src_all"][:, here])
                if first:
                    ins = nc.vector.tensor_copy(gather_idx[s][:, TILES:], consts["dst_all"][:, here])
                ins.then_inc(gather_idx_ready, 1)

            def moments(i, s):
                n = i * 2 + s
                dve.wait_ge(gathered[s], 16 * gathers * (i + 1))
                for k in range(gathers):
                    ins = nc.vector.bn_stats(stats[s][:, k, :], rows_in[s][:, k, :])
                ins.then_inc(stats_ready, 1)
                hold(dve, go, stats_ready, n + 1)
                for k in range(gathers):
                    ins = nc.vector.bn_aggr(mean_var[s][:, k, :], stats[s][:, k, :])
                ins.then_inc(mean_var_ready, 1)

            def scale_and_shift(i, s):
                n = i * 2 + s
                dve.wait_ge(std_ready, n + 1)
                nc.vector.reciprocal(rstd[s][:, :], std[s][:, :]).then_inc(rstd_ready, 1)
                dve.wait_ge(rstd_ready, n + 1)
                nc.vector.scalar_tensor_tensor(shift[s][:, :], mean_var[s][:, :, 0], -1.0, rstd[s][:, :],
                                               ALU.mult, ALU.mult).then_inc(shift_ready, 1)

            def masks(i, s):
                n = i * 2 + s
                dve.wait_ge(drow_in[s], 16 * (i + 1))
                beside = drow[s][:, 2:] if backward else drow[s][:, :WIN]
                nc.vector.tensor_tensor(keep[s][:, :], drow[s][:, 1:WIN + 1], beside, ALU.is_equal).then_inc(keep_ready, 1)
                if last:
                    dve.wait_ge(keep_ready, n + 1)
                    nc.vector.tensor_scalar(penalty[s][:, :], keep[s][:, :], -1.0, HUGE, ALU.add, ALU.mult).then_inc(penalty_ready, 1)

            def spread(i, s):
                n = i * 2 + s
                dve.wait_ge(scan_in_loaded[s], 16 * (i + 1))
                dve.wait_ge(keep_ready, n + 1)
                if later(i):
                    dve.wait_ge(hidden_summed, n - 1)
                if later(i) or s:
                    dve.wait_ge(xi_ready, n)
                nc.vector.tensor_tensor_scan(run(xiT[s]), run(keep[s]), run(scan_in[s]),
                                             end(xiT[1 - s]) if later(i) or s else 0.0,
                                             ALU.mult, ALU.max).then_inc(xi_ready, 1)

            def maxima(i, s):
                n = i * 2 + s
                dve.wait_ge(value_ready, n + 1)
                dve.wait_ge(keep_ready, n + 1)
                if last:
                    dve.wait_ge(penalty_ready, n + 1)
                if later(i):
                    dve.wait_ge(segmax_stored[s], 16 * i)
                    dve.wait_ge(rows_transposed, n - 1)
                if later(i) or s:
                    dve.wait_ge(segmax_ready, n)
                nc.vector.tensor_tensor_scan(run(segmax[s]), run(penalty[s] if last else keep[s]), run(value[s]),
                                             end(segmax[1 - s]) if later(i) or s else 0.0,
                                             ALU.add if last else ALU.mult, ALU.max).then_inc(segmax_ready, 1)

            def rows(i, s):
                n = i * 2 + s
                if later(i):
                    hold(dve, go, scattered[s], 16 * TILES * i)
                nc.vector.tensor_copy(scatter_idx[s][:, :], consts["firsts" if backward else "ends"][:, bass.ds(at(i, s) * TILES, TILES)]
                                      ).then_inc(scatter_idx_ready, 1)
                dve.wait_ge(rows_transposed, n + 1)
                out = rows_out[s][:, :, :].rearrange("p k f -> p (k f)")
                if last:
                    dve.wait_ge(xd_in[s], 16 * (i + 1))
                    nc.vector.tensor_tensor(out, ps_rows[:, :], xd[s][:, :], ALU.add).then_inc(rows_ready, 1)
                else:
                    nc.vector.tensor_copy(out, ps_rows[:, :]).then_inc(rows_ready, 1)

            if first:
                in_steps(dve, windows, 2, (moments, 2), (maxima, 4), (scale_and_shift, 2), (rows, 4), (masks, 2),
                         (next_indices, 0))
            else:
                in_steps(dve, windows, 2, (maxima, 4), (rows, 4), (masks, 2), (spread, 2), (next_indices, 0))

        @block.scalar
        def _(act):
            act.wait_ge(weights_in, 5 * 16)

            def roots(i, s):
                n = i * 2 + s
                act.wait_ge(mean_var_ready, n + 1)
                nc.scalar.activation(std[s][:, :], mean_var[s][:, :, 1], ACT.Sqrt, bias=eps_col[:, :]).then_inc(std_ready, 1)
                act.dma_start(window(xd_stream, at(i, s)),
                              rows_in[s][:, TILES:, :].rearrange("p k f -> p (k f)")).then_inc(xd_stored[s], 16)

            def normalise(i, s):
                n = i * 2 + s
                act.wait_ge(shift_ready, n + 1)
                if later(i):
                    act.wait_ge(x_transposed, n - 1)
                for k in range(gathers):
                    ins = nc.scalar.activation(normed[s][:, k, :], rows_in[s][:, k, :], ACT.Relu,
                                               bias=shift[s][:, k:k + 1], scale=rstd[s][:, k:k + 1])
                ins.then_inc(normed_ready, 1)

            def move_x(i, s):
                n = i * 2 + s
                act.wait_ge(x_transposed, n + 1)
                if later(i):
                    act.wait_ge(hidden_summed, n - 1)
                if first:
                    nc.scalar.copy(xiT[s][:, :], ps_xi[s][:, :])
                nc.scalar.copy(xjT[s][:, :], ps_xj[s][:, :]).then_inc(xT_ready, 1)

            def layer1(i, s):
                n = i * 2 + s
                act.wait_ge(hidden_summed, n + 1)
                if later(i):
                    act.wait_ge(value_summed, n - 1)
                nc.scalar.activation(hidden[s][:, :], ps_hidden[:, :], ACT.Relu, bias=b1[:, :]).then_inc(hidden_ready, 1)

            def layer2(i, s):
                n = i * 2 + s
                act.wait_ge(value_summed, n + 1)
                if later(i):
                    act.wait_ge(segmax_ready, n - 1)
                nc.scalar.activation(value[s][:, :], ps_value[:, :], ACT.Identity if last else ACT.Relu,
                                     bias=b2[:, :]).then_inc(value_ready, 1)

            if first:
                in_steps(act, windows, 2, (roots, 0), (layer2, 2), (layer1, 1), (normalise, 0), (move_x, 0))
            else:
                in_steps(act, windows, 2, (layer2, 2), (layer1, 1), (move_x, 0))

        @block.tensor
        def _(pe):
            def turn_x(i, s):
                n = i * 2 + s
                if first:
                    pe.wait_ge(normed_ready, n + 1)
                else:
                    pe.wait_ge(gathered[s], 16 * gathers * (i + 1))
                if later(i):
                    pe.wait_ge(xT_ready, n - 1)
                for k in range(gathers):
                    to = (ps_xj if k < TILES else ps_xi)[s]
                    k4 = k % TILES
                    ins = nc.tensor.transpose(to[:, k4 * P:(k4 + 1) * P], (normed if first else rows_in)[s][:, k, :], ident[:, :])
                ins.then_inc(x_transposed, 1)

            def layer1(i, s):
                n = i * 2 + s
                pe.wait_ge(xT_ready, n + 1)
                if not first:
                    pe.wait_ge(xi_ready, n + 1)
                if later(i) or s:
                    pe.wait_ge(hidden_ready, n)
                nc.tensor.matmul(ps_hidden[:, :], w1b[:, :], xjT[s][:, :], start=True, stop=False)
                nc.tensor.matmul(ps_hidden[:, :], wd[:, :], xiT[s][:, :], start=False, stop=True).then_inc(hidden_summed, 1)

            def layer2(i, s):
                n = i * 2 + s
                pe.wait_ge(hidden_ready, n + 1)
                if later(i) or s:
                    pe.wait_ge(value_ready, n)
                nc.tensor.matmul(ps_value[:, :], w2[:, :], hidden[s][:, :], start=True, stop=True).then_inc(value_summed, 1)

            def turn_maxima(i, s):
                n = i * 2 + s
                pe.wait_ge(segmax_ready, n + 1)
                if later(i) or s:
                    pe.wait_ge(rows_ready, n)
                for k in range(TILES):
                    ins = nc.tensor.transpose(ps_rows[:, k * P:(k + 1) * P], segmax[s][:, k * P:(k + 1) * P], ident[:, :])
                ins.then_inc(rows_transposed, 1)

            pe.wait_ge(weights_in, 5 * 16)
            pe.wait_ge(wd_ready, 1)
            in_steps(pe, windows, 2, (layer2, 2), (layer1, 1), (turn_maxima, 2), (turn_x, 0))


def score_pass(nc, consts, *, dst_row, type_row, x1_table, f_in, xd_stream, et_stream, rel, scores, windows):
    ctx = ExitStack()
    with ctx:
        ctx.enter_context(nc.cleanup_on_exit())
        banks = consts["banks"]

        def sb(name, shape, dt=F32):
            return ctx.enter_context(nc.sbuf_tensor(f"sc_{name}", shape, dt))

        def sem(name):
            return nc.alloc_semaphore(f"sc_{name}")

        SIDES = 2 * TILES
        ident, relation_col = consts["ident"], consts["relation_col"]
        rel_sb = sb("rel", [RELATIONS, P])
        gather_idx = [sb(f"gather_idx{s}", [P, TILES], I32) for s in (0, 1)]
        drow = [sb(f"drow{s}", [P, WIN + 2], I32) for s in (0, 1)]
        trow = [sb(f"trow{s}", [RELATIONS, WIN], I32) for s in (0, 1)]
        scan_in = [sb(f"scan_in{s}", [P, WIN]) for s in (0, 1)]
        xd = [sb(f"xd{s}", [P, WIN]) for s in (0, 1)]
        keep = [sb(f"keep{s}", [P, WIN]) for s in (0, 1)]
        penalty = [sb(f"penalty{s}", [P, WIN]) for s in (0, 1)]
        full = [sb(f"full{s}", [P, WIN]) for s in (0, 1)]
        onehot = [sb(f"onehot{s}", [RELATIONS, WIN]) for s in (0, 1)]
        U = 4
        sides = [sb(f"sides{s}", [P, SIDES, P]) for s in range(U)]
        stats = [sb(f"stats{s}", [P, SIDES, 6]) for s in (0, 1)]
        mean_var = [sb(f"mean_var{s}", [P, SIDES, 2]) for s in (0, 1)]
        var_eps = [sb(f"var_eps{s}", [P, SIDES]) for s in (0, 1)]
        rstd = [sb(f"rstd{s}", [P, SIDES]) for s in (0, 1)]
        shift = [sb(f"shift{s}", [P, SIDES]) for s in (0, 1)]
        normed = [sb(f"normed{s}", [P, SIDES, P]) for s in (0, 1)]
        tanh_sb = [sb(f"tanh{s}", [P, WIN]) for s in (0, 1)]
        product = [sb(f"product{s}", [P, TILES, P]) for s in (0, 1)]
        ps_full, ps_arg = banks[0:2], banks[2:4]

        rel_in = sem("rel_in")
        drow_in = [sem(f"drow_in{s}") for s in (0, 1)]
        trow_in = [sem(f"trow_in{s}") for s in (0, 1)]
        scan_in_loaded = [sem(f"scan_in_loaded{s}") for s in (0, 1)]
        xd_in = [sem(f"xd_in{s}") for s in (0, 1)]
        gathered = [sem(f"gathered{s}") for s in (0, 1)]
        et_stored = [sem(f"et_stored{s}") for s in (0, 1)]
        keep_ready, penalty_ready, full_ready, onehot_ready = sem("keep_ready"), sem("penalty_ready"), sem("full_ready"), sem("onehot_ready")
        full_transposed, xt_ready, stats_ready = sem("full_transposed"), sem("xt_ready"), sem("stats_ready")
        mean_var_ready, var_ready, rstd_ready, shift_ready = sem("mean_var_ready"), sem("var_ready"), sem("rstd_ready"), sem("shift_ready")
        gather_idx_ready = sem("gather_idx_ready")
        normed_ready, arg_summed, tanh_ready = sem("normed_ready"), sem("arg_summed"), sem("tanh_ready")
        product_ready, score_ready = sem("product_ready"), sem("score_ready")

        def at(i, s):
            return (windows - 1) - (i * U + s)

        def names(i, s):
            return i * U + s, s % 2, i * (U // 2) + s // 2, later(i) or s > 1

        go = consts["go"]
        block = ctx.enter_context(nc.Block())

        @block.sync
        def _(sp):
            sp.dma_start(rel_sb[:, :], rel).then_inc(rel_in, 16)

            def load_destinations(i, s):
                n, t, before, reused = names(i, s)
                if reused:
                    hold(sp, go, keep_ready, n - 1)
                sp.dma_start(drow[t][:, :], window(dst_row, at(i, s)).to_broadcast([P, WIN + 2])).then_inc(drow_in[t], 16)

            def load_maxima(i, s):
                n, t, before, reused = names(i, s)
                if reused:
                    hold(sp, go, full_ready, n - 1)
                sp.dma_start(scan_in[t][:, :], window(f_in, at(i, s))).then_inc(scan_in_loaded[t], 16)

            def load_xd(i, s):
                n, t, before, reused = names(i, s)
                if reused:
                    hold(sp, go, xt_ready, n - 1)
                sp.dma_start(xd[t][:, :], window(xd_stream, at(i, s))).then_inc(xd_in[t], 16)

            def load_relations(i, s):
                n, t, before, reused = names(i, s)
                if reused:
                    hold(sp, go, onehot_ready, n - 1)
                sp.dma_start(trow[t][:, :], window(type_row, at(i, s)).to_broadcast([RELATIONS, WIN])).then_inc(trow_in[t], 16)

            def store(i, s):
                n, t, before, reused = names(i, s)
                hold(sp, go, normed_ready, n + 1)
                sp.dma_start(window(et_stream, at(i, s)),
                             normed[t][:, TILES:, :].rearrange("p k f -> p (k f)")).then_inc(et_stored[t], 16)

            in_steps(sp, windows, U, (load_destinations, 0), (load_maxima, 1), (load_xd, 2), (load_relations, 2), (store, 6))
            for t in (0, 1):
                sp.wait_ge(et_stored[t], 16 * (windows // 2))

        @block.gpsimd
        def _(pool):
            def gather(i, s):
                n, t, before, reused = names(i, s)
                hold(pool, go, gather_idx_ready, n + 1)
                if later(i):
                    hold(pool, go, normed_ready, n - (U - 1))
                for k in range(TILES):
                    pool.indirect_dma_start(
                        sides[s][:, k, :], None, x1_table[:, :],
                        bass.IndirectOffsetOnAxis(ap=gather_idx[t][:, k:k + 1], axis=0)).then_inc(gathered[t], 16)

            def roots(i, s):
                n, t, before, reused = names(i, s)
                hold(pool, go, var_ready, n + 1)
                nc.gpsimd.tensor_tensor(rstd[t][:, :], var_eps[t][:, :], consts["minus_half"][:, :], ALU.pow).then_inc(rstd_ready, 1)

            in_steps(pool, windows, U, (gather, 0), (roots, 2))

        @block.vector
        def _(dve):
            def next_indices(i, s):
                n, t, before, reused = names(i, s)
                if reused:
                    hold(dve, go, gathered[t], 16 * TILES * before)
                nc.vector.tensor_copy(gather_idx[t][:, :], consts["src_all"][:, bass.ds(at(i, s) * TILES, TILES)]).then_inc(gather_idx_ready, 1)

            def masks(i, s):
                n, t, before, reused = names(i, s)
                dve.wait_ge(drow_in[t], 16 * (before + 1))
                if reused:
                    dve.wait_ge(penalty_ready, n - 1)
                nc.vector.tensor_tensor(keep[t][:, :], drow[t][:, 1:WIN + 1], drow[t][:, 2:], ALU.is_equal).then_inc(keep_ready, 1)

            def relations(i, s):
                n, t, before, reused = names(i, s)
                dve.wait_ge(trow_in[t], 16 * (before + 1))
                if reused:
                    dve.wait_ge(arg_summed, n - 1)
                nc.vector.tensor_scalar(onehot[t][:, :], trow[t][:, :], relation_col[:, :], None, ALU.is_equal).then_inc(onehot_ready, 1)

            def spread(i, s):
                n, t, before, reused = names(i, s)
                dve.wait_ge(scan_in_loaded[t], 16 * (before + 1))
                dve.wait_ge(penalty_ready, n + 1)
                if reused:
                    dve.wait_ge(full_transposed, n - 1)
                if later(i) or s:
                    dve.wait_ge(full_ready, n)
                nc.vector.tensor_tensor_scan(full[t][:, ::-1], penalty[t][:, ::-1], scan_in[t][:, ::-1],
                                             full[1 - t][:, 0:1] if later(i) or s else 0.0,
                                             ALU.add, ALU.max).then_inc(full_ready, 1)

            def moments(i, s):
                n, t, before, reused = names(i, s)
                dve.wait_ge(full_transposed, n + 1)
                dve.wait_ge(xd_in[t], 16 * (before + 1))
                if later(i):
                    dve.wait_ge(normed_ready, n - (U - 1))
                nc.vector.tensor_tensor(sides[s][:, TILES:, :].rearrange("p k f -> p (k f)"), ps_full[t][:, :], xd[t][:, :],
                                        ALU.add).then_inc(xt_ready, 1)
                dve.wait_ge(gathered[t], 16 * TILES * (before + 1))
                for k in range(TILES):
                    nc.vector.bn_stats(stats[t][:, k, :], sides[s][:, k, :])
                dve.wait_ge(xt_ready, n + 1)
                for k in range(TILES, SIDES):
                    ins = nc.vector.bn_stats(stats[t][:, k, :], sides[s][:, k, :])
                ins.then_inc(stats_ready, 1)
                hold(dve, go, stats_ready, n + 1)
                for k in range(SIDES):
                    ins = nc.vector.bn_aggr(mean_var[t][:, k, :], stats[t][:, k, :])
                ins.then_inc(mean_var_ready, 1)
                dve.wait_ge(mean_var_ready, n + 1)
                if reused:
                    dve.wait_ge(rstd_ready, n - 1)
                nc.vector.tensor_scalar(var_eps[t][:, :], mean_var[t][:, :, 1], EPS, None, ALU.add).then_inc(var_ready, 1)

            def shifts(i, s):
                n, t, before, reused = names(i, s)
                dve.wait_ge(rstd_ready, n + 1)
                if reused:
                    dve.wait_ge(normed_ready, n - 1)
                nc.vector.scalar_tensor_tensor(shift[t][:, :], mean_var[t][:, :, 0], -1.0, rstd[t][:, :],
                                               ALU.mult, ALU.mult).then_inc(shift_ready, 1)

            def score(i, s):
                n, t, before, reused = names(i, s)
                dve.wait_ge(tanh_ready, n + 1)
                nc.vector.tensor_tensor(product[t][:, :, :].rearrange("p k f -> p (k f)"), tanh_sb[t][:, :],
                                        normed[t][:, TILES:, :].rearrange("p k f -> p (k f)"), ALU.mult).then_inc(product_ready, 1)
                hold(dve, go, product_ready, n + 1)
                nc.vector.tensor_reduce(scores[:, bass.ds(at(i, s) * TILES, TILES)], product[t][:, :, :], AX.X, ALU.add).then_inc(score_ready, 1)

            in_steps(dve, windows, U, (shifts, 5), (moments, 4), (masks, 2), (relations, 4), (spread, 3), (score, 6), (next_indices, 1))

        @block.scalar
        def _(act):
            def penalties(i, s):
                n, t, before, reused = names(i, s)
                act.wait_ge(keep_ready, n + 1)
                if reused:
                    act.wait_ge(full_ready, n - 1)
                nc.scalar.activation(penalty[t][:, :], keep[t][:, :], ACT.Identity, bias=consts["minus_huge"][:, :],
                                     scale=HUGE).then_inc(penalty_ready, 1)

            def normalise(i, s):
                n, t, before, reused = names(i, s)
                act.wait_ge(shift_ready, n + 1)
                if reused:
                    act.wait_ge(arg_summed, n - 1)
                    act.wait_ge(product_ready, n - 1)
                    act.wait_ge(et_stored[t], 16 * before)
                for k in range(SIDES):
                    ins = nc.scalar.activation(normed[t][:, k, :], sides[s][:, k, :], ACT.Relu,
                                               bias=shift[t][:, k:k + 1], scale=rstd[t][:, k:k + 1])
                ins.then_inc(normed_ready, 1)

            def tanhs(i, s):
                n, t, before, reused = names(i, s)
                act.wait_ge(arg_summed, n + 1)
                if reused:
                    act.wait_ge(product_ready, n - 1)
                nc.scalar.activation(tanh_sb[t][:, :], ps_arg[t][:, :], ACT.Tanh).then_inc(tanh_ready, 1)

            in_steps(act, windows, U, (tanhs, 4), (normalise, 3), (penalties, 0))

        @block.tensor
        def _(pe):
            def turn_maxima(i, s):
                n, t, before, reused = names(i, s)
                pe.wait_ge(full_ready, n + 1)
                if reused:
                    pe.wait_ge(xt_ready, n - 1)
                for k in range(TILES):
                    ins = nc.tensor.transpose(ps_full[t][:, k * P:(k + 1) * P], full[t][:, k * P:(k + 1) * P], ident[:, :])
                ins.then_inc(full_transposed, 1)

            def argument(i, s):
                n, t, before, reused = names(i, s)
                pe.wait_ge(normed_ready, n + 1)
                pe.wait_ge(onehot_ready, n + 1)
                if reused:
                    pe.wait_ge(tanh_ready, n - 1)
                nc.tensor.matmul(ps_arg[t][:, :], ident[:, :], normed[t][:, :TILES, :].rearrange("p k f -> p (k f)"),
                                 start=True, stop=False)
                for k in range(TILES):
                    ins = nc.tensor.matmul(ps_arg[t][:, k * P:(k + 1) * P], onehot[t][:, k * P:(k + 1) * P], rel_sb[:, :],
                                           start=False, stop=k == TILES - 1)
                ins.then_inc(arg_summed, 1)

            pe.wait_ge(rel_in, 16)
            in_steps(pe, windows, U, (argument, 2), (turn_maxima, 0))


def softmax_pass(nc, consts, *, scores, weights, edges_padded_from):
    ctx = ExitStack()
    with ctx:
        ctx.enter_context(nc.cleanup_on_exit())
        n = scores.shape[1]
        dst_sb = consts["dst_seg_all"]
        pad = ctx.enter_context(nc.sbuf_tensor("sm_pad", [P, n], F32))
        masked = ctx.enter_context(nc.sbuf_tensor("sm_masked", [P, n], F32))
        largest = ctx.enter_context(nc.sbuf_tensor("sm_largest", [P, 1], F32))
        largest_one = ctx.enter_context(nc.sbuf_tensor("sm_largest_one", [1, 1], F32))
        as_row, on_all = consts["banks"][0][0:1, :P], consts["banks"][1][:, 0:1]
        minus_largest = ctx.enter_context(nc.sbuf_tensor("sm_minus_largest", [P, 1], F32))
        masked_ready = nc.alloc_semaphore("sm_masked_ready")
        largest_ready = nc.alloc_semaphore("sm_largest_ready")
        row_ready = nc.alloc_semaphore("sm_row_ready")
        all_ready = nc.alloc_semaphore("sm_all_ready")
        minus_ready = nc.alloc_semaphore("sm_minus_ready")
        weights_ready = nc.alloc_semaphore("sm_weights_ready")
        go = consts["go"]
        block = ctx.enter_context(nc.Block())

        @block.vector
        def _(dve):
            nc.vector.tensor_scalar(pad[:, :], dst_sb[:, :], float(edges_padded_from), -HUGE, ALU.is_ge, ALU.mult).then_inc(masked_ready, 1)
            dve.wait_ge(masked_ready, 1)
            nc.vector.tensor_tensor(masked[:, :], scores[:, :], pad[:, :], ALU.add).then_inc(masked_ready, 1)
            dve.wait_ge(masked_ready, 2)
            nc.vector.tensor_reduce(largest[:, :], masked[:, :], AX.X, ALU.max).then_inc(largest_ready, 1)
            dve.wait_ge(row_ready, 1)
            nc.vector.tensor_reduce(largest_one[:, :], as_row[:, :], AX.X, ALU.max).then_inc(largest_ready, 1)
            dve.wait_ge(all_ready, 1)
            nc.vector.tensor_scalar(minus_largest[:, :], on_all[:, :], -1.0, None, ALU.mult).then_inc(minus_ready, 1)

        @block.tensor
        def _(pe):
            pe.wait_ge(largest_ready, 1)
            nc.tensor.transpose(as_row[:, :], largest[:, :], consts["ident"][:, :]).then_inc(row_ready, 1)
            pe.wait_ge(largest_ready, 2)
            nc.tensor.matmul(on_all[:, :], consts["ones"][0:1, 0, :P], largest_one[:, :], start=True, stop=True).then_inc(all_ready, 1)

        @block.scalar
        def _(act):
            act.wait_ge(minus_ready, 1)
            nc.scalar.activation(weights[:, :], masked[:, :], ACT.Exp, bias=minus_largest[:, :]).then_inc(weights_ready, 1)


def sum_pass(nc, consts, *, src_row, et_stream, sums_table, weights, windows):
    rounds = windows // 2
    ctx = ExitStack()
    with ctx:
        ctx.enter_context(nc.cleanup_on_exit())
        banks = consts["banks"]

        def sb(name, shape, dt=F32):
            return ctx.enter_context(nc.sbuf_tensor(f"sum_{name}", shape, dt))

        def sem(name):
            return nc.alloc_semaphore(f"sum_{name}")

        later_mask, spare_rows = consts["later_mask"], consts["spare_rows"]
        src_f = [sb(f"src_f{s}", [P, TILES]) for s in (0, 1)]
        srow = [sb(f"srow{s}", [P, WIN], I32) for s in (0, 1)]
        et = [sb(f"et{s}", [P, TILES, SUM_W]) for s in (0, 1)]
        wcol = [sb(f"wcol{s}", [P, TILES]) for s in (0, 1)]
        weighted = [sb(f"weighted{s}", [P, TILES, SUM_W]) for s in (0, 1)]
        equal = [sb(f"equal{s}", [P, TILES, WIN]) for s in (0, 1)]
        scrap = [sb(f"scrap{s}", [P, TILES, WIN], mybir.dt.bfloat16) for s in (0, 1)]
        n_later = [sb(f"n_later{s}", [P, TILES]) for s in (0, 1)]
        has_later = [sb(f"has_later{s}", [P, TILES]) for s in (0, 1)]
        to_spare = [sb(f"to_spare{s}", [P, TILES]) for s in (0, 1)]
        move = [sb(f"move{s}", [P, TILES]) for s in (0, 1)]
        scatter_idx = [sb(f"scatter_idx{s}", [P, TILES], I32) for s in (0, 1)]
        summed = [sb(f"summed{s}", [P, TILES, SUM_W]) for s in (0, 1)]
        ps_sum = [[t[:, :2 * SUM_W].rearrange("p (k f) -> p k f", k=2) for t in pair] for pair in (banks[0:2], banks[2:4])]

        ones_ready = sem("ones_ready")
        srow_in = [sem(f"srow_in{s}") for s in (0, 1)]
        et_in = [sem(f"et_in{s}") for s in (0, 1)]
        scattered = sem("scattered")
        src_f_ready, wcol_ready, weighted_ready, equal_ready = sem("src_f_ready"), sem("wcol_ready"), sem("weighted_ready"), sem("equal_ready")
        n_later_ready, spare_ready, move_ready, idx_ready = sem("n_later_ready"), sem("spare_ready"), sem("move_ready"), sem("idx_ready")
        sums_made, summed_ready = sem("sums_made"), sem("summed_ready")

        go = consts["go"]
        block = ctx.enter_context(nc.Block())

        @block.sync
        def _(sp):
            sp.wait_ge(ones_ready, 2)

            def load(i, s):
                n = i * 2 + s
                if later(i):
                    hold(sp, go, n_later_ready, n - 1)
                sp.dma_start(srow[s][:, :], window(src_row, n).to_broadcast([P, WIN])).then_inc(srow_in[s], 16)
                if later(i):
                    hold(sp, go, weighted_ready, n - 1)
                sp.dma_start(et[s][:, :, :P], window(et_stream, n).rearrange("p (k f) -> p k f", k=TILES)).then_inc(et_in[s], 16)

            load(0, 0)
            load(0, 1)
            with sp.Fori(1, rounds) as i:
                load(i, 0)
                load(i, 1)

        @block.vector
        def _(dve):
            for s in (0, 1):
                nc.vector.memset(et[s][:, :, P:], 1.0).then_inc(ones_ready, 1)

            def edges(i, s):
                n = i * 2 + s
                here = bass.ds(n * TILES, TILES)
                nc.vector.tensor_copy(src_f[s][:, :], consts["src_all"][:, here]).then_inc(src_f_ready, 1)
                nc.vector.tensor_copy(wcol[s][:, :], weights[:, here]).then_inc(wcol_ready, 1)
                dve.wait_ge(srow_in[s], 16 * (i + 1))
                dve.wait_ge(src_f_ready, n + 1)
                if later(i):
                    dve.wait_ge(sums_made, n - 1)
                for k in range(TILES):
                    ins = nc.vector.tensor_scalar(equal[s][:, k, :], srow[s][:, :], src_f[s][:, k:k + 1], None, ALU.is_equal)
                ins.then_inc(equal_ready, 1)
                dve.wait_ge(et_in[s], 16 * (i + 1))
                dve.wait_ge(wcol_ready, n + 1)
                nc.vector.tensor_tensor(weighted[s][:, :, :], et[s][:, :, :],
                                        wcol[s][:, :].unsqueeze(2).to_broadcast([P, TILES, SUM_W]), ALU.mult).then_inc(weighted_ready, 1)
                dve.wait_ge(equal_ready, n + 1)
                for k in range(TILES):
                    ins = nc.vector.scalar_tensor_tensor(scrap[s][:, k, :], srow[s][:, :], src_f[s][:, k:k + 1], later_mask[:, k, :],
                                                         ALU.is_equal, ALU.mult, accum_out=n_later[s][:, k:k + 1])
                ins.then_inc(n_later_ready, 1)
                nc.vector.tensor_tensor(to_spare[s][:, :], spare_rows[:, :], src_f[s][:, :], ALU.subtract).then_inc(spare_ready, 1)
                dve.wait_ge(n_later_ready, n + 1)
                dve.wait_ge(spare_ready, n + 1)
                nc.vector.scalar_tensor_tensor(move[s][:, :], n_later[s][:, :], 0.0, to_spare[s][:, :],
                                               ALU.is_gt, ALU.mult).then_inc(move_ready, 1)
                dve.wait_ge(move_ready, n + 1)
                if later(i):
                    dve.wait_ge(scattered, 16 * TILES * (n - 1))
                nc.vector.tensor_tensor(scatter_idx[s][:, :], move[s][:, :], src_f[s][:, :], ALU.add).then_inc(idx_ready, 1)

            edges(0, 0)
            edges(0, 1)
            with dve.Fori(1, rounds) as i:
                edges(i, 0)
                edges(i, 1)

        @block.tensor
        def _(pe):
            def sums(i, s):
                n = i * 2 + s
                pe.wait_ge(equal_ready, n + 1)
                pe.wait_ge(weighted_ready, n + 1)
                if later(i):
                    pe.wait_ge(summed_ready, n - 1)
                for a in range(TILES):
                    for b in range(TILES):
                        ins = nc.tensor.matmul(ps_sum[s][a // 2][:, a % 2, :], equal[s][:, b, a * P:(a + 1) * P],
                                               weighted[s][:, b, :], start=b == 0, stop=b == TILES - 1)
                ins.then_inc(sums_made, 1)

            sums(0, 0)
            sums(0, 1)
            with pe.Fori(1, rounds) as i:
                sums(i, 0)
                sums(i, 1)

        @block.scalar
        def _(act):
            def move_out(i, s):
                n = i * 2 + s
                act.wait_ge(sums_made, n + 1)
                if later(i):
                    act.wait_ge(scattered, 16 * TILES * (n - 1))
                nc.scalar.copy(summed[s][:, 0:2, :], ps_sum[s][0])
                nc.scalar.copy(summed[s][:, 2:4, :], ps_sum[s][1]).then_inc(summed_ready, 1)

            move_out(0, 0)
            move_out(0, 1)
            with act.Fori(1, rounds) as i:
                move_out(i, 0)
                move_out(i, 1)

        @block.gpsimd
        def _(pool):
            def scatter(i, s):
                n = i * 2 + s
                hold(pool, go, idx_ready, n + 1)
                hold(pool, go, summed_ready, n + 1)
                if later(i) or s:
                    hold(pool, go, scattered, 16 * TILES * n)
                for k in range(TILES):
                    pool.indirect_dma_start(
                        sums_table[:, :], bass.IndirectOffsetOnAxis(ap=scatter_idx[s][:, k:k + 1], axis=0),
                        summed[s][:, k, :], None, compute_op=ALU.add).then_inc(scattered, 16)

            scatter(0, 0)
            scatter(0, 1)
            with pool.Fori(1, rounds) as i:
                scatter(i, 0)
                scatter(i, 1)
            pool.wait_ge(scattered, 16 * TILES * windows)


def node_pass(nc, consts, *, x1_table, sums_table, wt, out, nodes):
    rows = P * PIECE
    full_pieces = nodes // rows
    tail = (nodes - full_pieces * rows) // PIECE
    pieces = full_pieces + (1 if tail else 0)
    assert tail * PIECE == nodes - full_pieces * rows
    U = 6
    HALVES = PIECE // TILES
    ctx = ExitStack()
    with ctx:
        ctx.enter_context(nc.cleanup_on_exit())
        banks = consts["banks"]

        def sb(name, shape, slots):
            return [ctx.enter_context(nc.sbuf_tensor(f"n_{name}{s}", shape, F32)) for s in range(slots)]

        def sem(name):
            return nc.alloc_semaphore(f"n_{name}")

        ident, eps_col = consts["ident"], consts["eps"]
        wt_sb = sb("wt", [P, P], 1)[0]
        x1, sums = sb("x1", [P, PIECE, P], U), sb("sums", [P, PIECE, SUM_W], U)
        stats, mean_var = sb("stats", [P, PIECE, 6], 2), sb("mean_var", [P, PIECE, 2], 2)
        std, rstd, shift = sb("std", [P, PIECE], 2), sb("rstd", [P, PIECE], 2), sb("shift", [P, PIECE], 2)
        weight, rweight = sb("weight", [P, PIECE], 2), sb("rweight", [P, PIECE], 2)
        h, mean_agg, with_agg = sb("h", [P, PIECE, P], 2), sb("mean_agg", [P, PIECE, P], 2), sb("with_agg", [P, PIECE, P], 2)
        transposed, fifth = sb("transposed", [P, PIECE, P], 2), sb("fifth", [P, PIECE, P], 2)
        leaky, result = sb("leaky", [P, PIECE, P], 2), sb("result", [P, PIECE, P], 2)
        by_tile = [t[:, :].rearrange("p (k f) -> p k f", k=TILES) for t in banks]
        ps_t, ps_o = (by_tile[0:2], by_tile[2:4]), (by_tile[4:6], by_tile[6:8])

        wt_in = sem("wt_in")
        x1_in = [sem(f"x1_in{s}") for s in range(U)]
        sums_in = [sem(f"sums_in{s}") for s in range(U)]
        stored = [sem(f"stored{s}") for s in range(U)]
        stats_ready, mean_var_ready, std_ready, rstd_ready, shift_ready = (
            sem("stats_ready"), sem("mean_var_ready"), sem("std_ready"), sem("rstd_ready"), sem("shift_ready"))
        weight_ready, rweight_ready, h_ready = sem("weight_ready"), sem("rweight_ready"), sem("h_ready")
        mean_agg_ready, with_agg_ready = sem("mean_agg_ready"), sem("with_agg_ready")
        turned, transposed_ready, multiplied = sem("turned"), sem("transposed_ready"), sem("multiplied")
        fifth_ready, leaky_ready, result_ready = sem("fifth_ready"), sem("leaky_ready"), sem("result_ready")
        go = consts["go"]
        block = ctx.enter_context(nc.Block())

        def piece(table, n, parts):
            return table[bass.ds(n * rows, parts * PIECE), :].rearrange("(p j) f -> p j f", j=PIECE)

        def parts_of(i, s):
            return tail if tail and isinstance(i, int) and i * U + s == full_pieces else P

        def has_before(i, s):
            return later(i) or s > 1

        @block.sync
        def _(sp):
            sp.dma_start(wt_sb[:, :], wt).then_inc(wt_in, 16)

            def load(i, s):
                n, p = i * U + s, parts_of(i, s)
                if later(i):
                    hold(sp, go, result_ready, n - (U - 1))
                sp.dma_start(x1[s][:p, :, :], piece(x1_table, n, p)).then_inc(x1_in[s], 16)
                if later(i):
                    hold(sp, go, mean_agg_ready, n - (U - 1))
                sp.dma_start(sums[s][:p, :, :], piece(sums_table, n, p)).then_inc(sums_in[s], 16)

            def store(i, s):
                n, p = i * U + s, parts_of(i, s)
                hold(sp, go, result_ready, n + 1)
                sp.dma_start(piece(out, n, p), result[s % 2][:p, :, :]).then_inc(stored[s], 16)

            in_steps(sp, pieces, U, (store, 6), (load, 0))
            for s in range(U):
                sp.wait_ge(stored[s], 16 * (-(-(pieces - s) // U)))

        @block.gpsimd
        def _(pool):
            def finish(i, s):
                n, p = i * U + s, parts_of(i, s)
                pool.wait_ge(leaky_ready, n + 1)
                if has_before(i, s):
                    pool.wait_ge(stored[(s - 2) % U], 16 * (i + 1 if s > 1 else i))
                nc.gpsimd.tensor_tensor(result[s % 2][:p, :, :], leaky[s % 2][:p, :, :], x1[s][:p, :, :], ALU.add).then_inc(result_ready, 1)

            def means(i, s):
                n, p, t = i * U + s, parts_of(i, s), s % 2
                pool.wait_ge(rweight_ready, n + 1)
                if has_before(i, s):
                    pool.wait_ge(with_agg_ready, n - 1)
                nc.gpsimd.tensor_tensor(mean_agg[t][:p, :, :], sums[s][:p, :, :P],
                                        rweight[t][:p, :].unsqueeze(2).to_broadcast([p, PIECE, P]), ALU.mult).then_inc(mean_agg_ready, 1)

            in_steps(pool, pieces, U, (means, 0), (finish, 3))

        @block.vector
        def _(dve):
            def moments(i, s):
                n, p, t = i * U + s, parts_of(i, s), s % 2
                dve.wait_ge(x1_in[s], 16 * (i + 1))
                for k in range(PIECE):
                    ins = nc.vector.bn_stats(stats[t][:p, k, :], x1[s][:p, k, :])
                ins.then_inc(stats_ready, 1)
                dve.wait_ge(sums_in[s], 16 * (i + 1))
                nc.vector.tensor_scalar(weight[t][:p, :], sums[s][:p, :, P], 1e-10, None, ALU.add).then_inc(weight_ready, 1)
                hold(dve, go, stats_ready, n + 1)
                for k in range(PIECE):
                    ins = nc.vector.bn_aggr(mean_var[t][:p, k, :], stats[t][:p, k, :])
                ins.then_inc(mean_var_ready, 1)
                dve.wait_ge(weight_ready, n + 1)
                nc.vector.reciprocal(rweight[t][:p, :], weight[t][:p, :]).then_inc(rweight_ready, 1)

            def scale_and_shift(i, s):
                n, p, t = i * U + s, parts_of(i, s), s % 2
                dve.wait_ge(std_ready, n + 1)
                nc.vector.reciprocal(rstd[t][:p, :], std[t][:p, :]).then_inc(rstd_ready, 1)
                dve.wait_ge(rstd_ready, n + 1)
                nc.vector.scalar_tensor_tensor(shift[t][:p, :], mean_var[t][:p, :, 0], -1.0, rstd[t][:p, :],
                                               ALU.mult, ALU.mult).then_inc(shift_ready, 1)

            def attention(i, s):
                n, p, t = i * U + s, parts_of(i, s), s % 2
                dve.wait_ge(h_ready, n + 1)
                dve.wait_ge(mean_agg_ready, n + 1)
                if has_before(i, s):
                    dve.wait_ge(turned, n - 1)
                nc.vector.tensor_tensor(with_agg[t][:p, :, :], mean_agg[t][:p, :, :], h[t][:p, :, :], ALU.add).then_inc(with_agg_ready, 1)

            def leak(i, s):
                n, p, t = i * U + s, parts_of(i, s), s % 2
                dve.wait_ge(fifth_ready, n + 1)
                if has_before(i, s):
                    dve.wait_ge(result_ready, n - 1)
                for b in range(HALVES):
                    ins = nc.vector.tensor_tensor(leaky[t][:p, b * TILES:(b + 1) * TILES, :], ps_o[t][b][:p, :, :],
                                                  fifth[t][:p, b * TILES:(b + 1) * TILES, :], ALU.max)
                ins.then_inc(leaky_ready, 1)

            in_steps(dve, pieces, U, (attention, 2), (moments, 0), (leak, 3), (scale_and_shift, 0))

        @block.scalar
        def _(act):
            def roots(i, s):
                n, p, t = i * U + s, parts_of(i, s), s % 2
                act.wait_ge(mean_var_ready, n + 1)
                nc.scalar.activation(std[t][:p, :], mean_var[t][:p, :, 1], ACT.Sqrt, bias=eps_col[:p, :]).then_inc(std_ready, 1)

            def normalise(i, s):
                n, p, t = i * U + s, parts_of(i, s), s % 2
                act.wait_ge(shift_ready, n + 1)
                if has_before(i, s):
                    act.wait_ge(with_agg_ready, n - 1)
                for k in range(PIECE):
                    ins = nc.scalar.activation(h[t][:p, k, :], x1[s][:p, k, :], ACT.Relu,
                                               bias=shift[t][:p, k:k + 1], scale=rstd[t][:p, k:k + 1])
                ins.then_inc(h_ready, 1)

            def move_turned(i, s):
                n, p, t = i * U + s, parts_of(i, s), s % 2
                act.wait_ge(turned, n + 1)
                if has_before(i, s):
                    act.wait_ge(multiplied, n - 1)
                for b in range(HALVES):
                    ins = nc.scalar.copy(transposed[t][:, b * TILES:(b + 1) * TILES, :p], ps_t[t][b][:, :, :p])
                ins.then_inc(transposed_ready, 1)

            def fifths(i, s):
                n, p, t = i * U + s, parts_of(i, s), s % 2
                act.wait_ge(multiplied, n + 1)
                if has_before(i, s):
                    act.wait_ge(leaky_ready, n - 1)
                for b in range(HALVES):
                    ins = nc.scalar.mul(fifth[t][:p, b * TILES:(b + 1) * TILES, :], ps_o[t][b][:p, :, :], 0.2)
                ins.then_inc(fifth_ready, 1)

            in_steps(act, pieces, U, (roots, 0), (fifths, 3), (move_turned, 2), (normalise, 0))

        @block.tensor
        def _(pe):
            pe.wait_ge(wt_in, 16)

            def turn(i, s):
                n, p, t = i * U + s, parts_of(i, s), s % 2
                pe.wait_ge(with_agg_ready, n + 1)
                if has_before(i, s):
                    pe.wait_ge(transposed_ready, n - 1)
                for k in range(PIECE):
                    ins = nc.tensor.transpose(ps_t[t][k // TILES][:, k % TILES, :p], with_agg[t][:p, k, :], ident[:p, :p])
                ins.then_inc(turned, 1)

            def multiply(i, s):
                n, p, t = i * U + s, parts_of(i, s), s % 2
                pe.wait_ge(transposed_ready, n + 1)
                if has_before(i, s):
                    pe.wait_ge(leaky_ready, n - 1)
                for k in range(PIECE):
                    ins = nc.tensor.matmul(ps_o[t][k // TILES][:p, k % TILES, :], transposed[t][:, k, :p], wt_sb[:, :],
                                           start=True, stop=True)
                ins.then_inc(multiplied, 1)

            in_steps(pe, pieces, U, (multiply, 3), (turn, 2))


def build(nc, x, by_edge, dst_row, src_row, type_row, conv, rel, wt, out):
    nodes = x.shape[0]
    windows = dst_row.shape[0]
    edge_tiles = windows * TILES
    assert windows % 2 == 0
    table_rows = -(-(nodes + 1) // (P * PIECE)) * P * PIECE
    pieces = table_rows // (P * PIECE)
    assert pieces == windows
    node_piece = nodes // windows
    node_tail = nodes - node_piece * windows

    def dram(name, shape):
        return nc.dram_tensor(name, shape, F32, kind="Internal").ap()

    table2, table3, x1_table = (dram(n, (table_rows, P)) for n in ("table2", "table3", "x1_table"))
    sums_table = dram("sums_table", (table_rows + WIN, SUM_W))
    f1, f2, f3, xd_stream, et_stream = (dram(n, (windows, P, WIN)) for n in ("f1", "f2", "f3", "xd_stream", "et_stream"))

    ctx = ExitStack()
    with ctx:
        def sb(name, shape, dt=F32):
            return ctx.enter_context(nc.sbuf_tensor(name, shape, dt))

        zeros = sb("zeros", [P, PIECE * SUM_W])
        ones = sb("ones", [P, TILES, WIN])
        ident = sb("ident", [P, P])
        eps_col = sb("eps_col", [P, 1])
        later_mask = sb("later_mask", [P, TILES, WIN])
        spare_i, spare_rows = sb("spare_i", [P, TILES], I32), sb("spare_rows", [P, TILES])
        relation_i, relation_col = sb("relation_i", [RELATIONS, 1], I32), sb("relation_col", [RELATIONS, 1])
        scores = sb("scores", [P, windows * TILES])
        weights = sb("weights", [P, windows * TILES])
        src_all, dst_all, dst_seg_all, next_all, prev_all = (
            sb(n, [P, edge_tiles], I32) for n in ("src_all", "dst_all", "dst_seg_all", "next_all", "prev_all"))
        ends, firsts = sb("ends", [P, edge_tiles], I32), sb("firsts", [P, edge_tiles], I32)
        inner = [sb(f"inner{k}", [P, edge_tiles]) for k in (0, 1)]
        minus_half, minus_huge = sb("minus_half", [P, 2 * TILES]), sb("minus_huge", [P, 1])
        go = ctx.enter_context(nc.semaphore("set_up"))
        banks = [ctx.enter_context(nc.psum_tensor(f"bank{b}", [P, WIN], F32)) for b in range(8)]
        consts = {"banks": banks, "go": go, "ident": ident, "ones": ones, "eps": eps_col, "later_mask": later_mask, "spare_rows": spare_rows,
                  "relation_col": relation_col, "minus_half": minus_half,
                  "minus_huge": minus_huge, "src_all": src_all, "dst_all": dst_all, "dst_seg_all": dst_seg_all, "ends": ends,
                  "firsts": firsts}

        def clear(sp, table, n, width, sem):
            sp.dma_start(table[bass.ds(n * (P * PIECE), P * PIECE), :].rearrange("(p j) f -> p (j f)", j=PIECE),
                         zeros[:, :PIECE * width]).then_inc(sem, 16)

        with ExitStack() as setup:
            zeros_ready, memset_done = ctx.enter_context(nc.semaphore("zeros_ready")), ctx.enter_context(nc.semaphore("memset_done"))
            iota_done, cleared = ctx.enter_context(nc.semaphore("iota_done")), ctx.enter_context(nc.semaphore("cleared"))
            const_done = ctx.enter_context(nc.semaphore("const_done"))
            by_edge_in, inner_ready = ctx.enter_context(nc.semaphore("by_edge_in")), ctx.enter_context(nc.semaphore("inner_ready"))
            block = setup.enter_context(nc.Block())

            @block.gpsimd
            def _(pool):
                nc.gpsimd.memset(ones[:, :, :], 1.0).then_inc(memset_done, 1)
                nc.gpsimd.iota(spare_i[:, :], [[P, TILES]], base=table_rows, channel_multiplier=1).then_inc(iota_done, 1)
                nc.gpsimd.iota(relation_i[:, :], [[0, 1]], base=0, channel_multiplier=1).then_inc(iota_done, 1)
                pool.wait_ge(memset_done, 1)
                nc.gpsimd.affine_select(ident[:, :], ones[:, 0, :P], [[-1, P]], ALU.is_equal, 0.0, base=0, channel_multiplier=1)
                nc.gpsimd.affine_select(later_mask[:, :, :], ones[:, :, :], [[-P, TILES], [1, WIN]], ALU.is_gt, 0.0,
                                        base=0, channel_multiplier=-1)

            @block.vector
            def _(dve):
                nc.vector.memset(zeros[:, :], 0.0).then_inc(zeros_ready, 1)
                nc.vector.memset(eps_col[:, :], EPS).then_inc(go, 1)
                dve.wait_ge(iota_done, 2)
                nc.vector.tensor_copy(spare_rows[:, :], spare_i[:, :])
                nc.vector.tensor_copy(relation_col[:, :], relation_i[:, :]).then_inc(const_done, 1)
                nc.vector.memset(minus_half[:, :], -0.5)
                nc.vector.memset(minus_huge[:, :], -HUGE)
                dve.wait_ge(by_edge_in, 5 * 16)
                for k, beside in enumerate((next_all, prev_all)):
                    nc.vector.tensor_tensor(inner[k][:, :], dst_seg_all[:, :], beside[:, :], ALU.is_equal).then_inc(inner_ready, 1)
                for k, made in enumerate((ends, firsts)):
                    dve.wait_ge(inner_ready, k + 1)
                    nc.vector.scalar_tensor_tensor(made[:, :], inner[k][:, :], SKIP, dst_seg_all[:, :], ALU.mult, ALU.add)

            @block.sync
            def _(sp):
                for k, t in enumerate((src_all, dst_all, dst_seg_all, next_all, prev_all)):
                    sp.dma_start(t[:, :], by_edge[k]).then_inc(by_edge_in, 16)
                sp.wait_ge(zeros_ready, 1)
                with sp.Fori(0, pieces) as n:
                    clear(sp, table2, n, P, cleared)
                sp.dma_start(x1_table[nodes - node_tail:nodes, :], x[nodes - node_tail:nodes, :]).then_inc(cleared, 16)
                spare = (table_rows - nodes) // PIECE
                sp.dma_start(x1_table[nodes:nodes + spare * PIECE, :].rearrange("(p j) f -> p (j f)", j=PIECE),
                             zeros[:spare, :PIECE * P]).then_inc(cleared, 16)
                sp.dma_start(sums_table[table_rows:, :].rearrange("(p j) f -> p (j f)", j=TILES), zeros[:, :TILES * SUM_W]).then_inc(cleared, 16)
                sp.wait_ge(cleared, 16 * (pieces + 3))

        def copy_x(sp, n, sem):
            size = node_piece * P // 16
            sp.dma_start(x1_table[bass.ds(n * node_piece, node_piece), :].rearrange("r f -> (r f)").rearrange("(a b) -> a b", b=size),
                         x[bass.ds(n * node_piece, node_piece), :].rearrange("r f -> (r f)").rearrange("(a b) -> a b", b=size)).then_inc(sem, 16)

        shared = dict(dst_row=dst_row, xd_stream=xd_stream, windows=windows)
        edge_conv_pass(nc, "c1", consts, first=True, last=False, table_in=None, x_rows=x, table_out=table2, f_in=None, f_out=f1,
                       weights=conv[0], bulk=lambda sp, n, sem: clear(sp, table3, n, P, sem), **shared)
        edge_conv_pass(nc, "c2", consts, first=False, last=False, table_in=table2, x_rows=None, table_out=table3, f_in=f1, f_out=f2,
                       weights=conv[1], bulk=lambda sp, n, sem: copy_x(sp, n, sem), **shared)
        edge_conv_pass(nc, "c3", consts, first=False, last=True, table_in=table3, x_rows=None, table_out=x1_table, f_in=f2, f_out=f3,
                       weights=conv[2], bulk=lambda sp, n, sem: clear(sp, sums_table, n, SUM_W, sem), **shared)
        score_pass(nc, consts, type_row=type_row, x1_table=x1_table, f_in=f3, et_stream=et_stream, rel=rel, scores=scores, **shared)
        softmax_pass(nc, consts, scores=scores, weights=weights, edges_padded_from=nodes)
        sum_pass(nc, consts, src_row=src_row, et_stream=et_stream, sums_table=sums_table, weights=weights, windows=windows)
        node_pass(nc, consts, x1_table=x1_table, sums_table=sums_table, wt=wt, out=out, nodes=nodes)


def kernel(x, src, dst, edge_type_64, **p):
    import numpy as np
    import concourse.bacc as bacc
    from concourse.bass_utils import run_bass_kernel_spmd as run

    x, src, dst, kinds = (np.asarray(a) for a in (x, src, dst, edge_type_64))
    nodes, edges = x.shape[0], src.shape[0]
    windows = -(-edges // WIN)
    windows += windows % 2
    padded = windows * WIN

    def pad(a, fill):
        return np.concatenate([a, np.full((padded - edges,), fill, a.dtype)])

    def columns(a):
        return a.reshape(windows * TILES, P).T

    src_p, dst_g, dst_p, kind_p = pad(src, 0), pad(dst, 0), pad(dst, nodes), pad(kinds, 0)
    none = np.full((1,), -1, dst.dtype)
    around = np.concatenate([none, dst_p, none])
    arrays = {
        "x": x,
        "by_edge": np.stack([columns(a) for a in (src_p, dst_g, dst_p, around[2:], around[:-2])]),
        "dst_row": np.stack([around[w * WIN:w * WIN + WIN + 2] for w in range(windows)]).reshape(windows, 1, WIN + 2),
        "src_row": src_p.reshape(windows, 1, WIN),
        "type_row": kind_p.reshape(windows, 1, WIN),
        "rel": np.asarray(p["L1_gnn_rel_embed_weight"]),
        "wt": np.ascontiguousarray(np.asarray(p["L1_gnn_W"]).T),
    }
    for layer in ("in", "hid", "out"):
        arrays[f"W1_{layer}"] = np.asarray(p[f"L0_gnn_W1_{layer}"])
        arrays[f"W2_{layer}"] = np.asarray(p[f"L0_gnn_W2_{layer}"])
        arrays[f"b1_{layer}"] = np.asarray(p[f"L0_gnn_b1_{layer}"]).reshape(P, 1)
        arrays[f"b2_{layer}"] = np.asarray(p[f"L0_gnn_b2_{layer}"]).reshape(P, 1)

    nc = bacc.Bacc("TRN2", target_bir_lowering=False, num_devices=1)
    ap = {n: nc.dram_tensor(n, a.shape, mybir.dt.from_np(a.dtype), kind="ExternalInput").ap() for n, a in arrays.items()}
    out = nc.dram_tensor("out", x.shape, F32, kind="ExternalOutput").ap()
    conv = [{k: ap[f"{k}_{layer}"] for k in ("W1", "W2", "b1", "b2")} for layer in ("in", "hid", "out")]
    build(nc, ap["x"], ap["by_edge"], ap["dst_row"], ap["src_row"], ap["type_row"], conv, ap["rel"], ap["wt"], out)
    return run(nc, [arrays], core_ids=[0]).results[0]["out"]
```

```python
import concourse.bass as bass
from concourse import mybir
from contextlib import ExitStack

F32 = mybir.dt.float32
I32 = mybir.dt.int32
ALU = mybir.AluOpType
ACT = mybir.ActivationFunctionType
AX = mybir.AxisListType

P = 128
TILES = 4
WIN = TILES * P
PIECE = 8
SUM_W = P + 4
SKIP = float(1 << 20)
HUGE = 3.0e38
EPS = 1e-5
EARLY = 28
GROUP_TILES = 8
GROUP = GROUP_TILES * P
RELATIONS = 64


def window(ap, w):
    return ap[bass.ds(w, 1)].rearrange("o p n -> (o p) n")


def hold(eng, go, sem, value):
    if not isinstance(value, int):
        value = eng.to_reg(value)
        eng.wait_ge(go, 1)
    eng.wait_ge(sem, value)


def later(i):
    return not isinstance(i, int) or i > 0


def in_steps(eng, count, unroll, *stages, start=0):
    deepest = max(lag for _, lag in stages)
    peeled = 1 + -(-(start + deepest) // unroll)

    def step(i, s):
        for stage, lag in stages:
            r, t = i + (s - lag) // unroll, (s - lag) % unroll
            if not isinstance(i, int) or 0 <= r * unroll + t < count:
                stage(r, t)

    for n in range(peeled * unroll):
        step(n // unroll, n % unroll)
    with eng.Fori(peeled, count // unroll) as i:
        for s in range(unroll):
            step(i, s)
    for n in range(count // unroll * unroll, count + deepest):
        step(n // unroll, n % unroll)


def edge_conv_pass(nc, tag, consts, *, first, last, dst_row, table_in, x_rows, table_out, f_in, f_out,
                   xd_stream, weights, windows, bulk, early=0, clear_out=None):
    backward = not first and not last
    rounds = windows // 2
    gathers = 2 * TILES if first else TILES
    ctx = ExitStack()
    with ctx:
        ctx.enter_context(nc.cleanup_on_exit())
        banks = consts["banks"]

        def sb(name, shape, dt=F32):
            return ctx.enter_context(nc.sbuf_tensor(f"{tag}_{name}", shape, dt))

        def sem(name):
            return nc.alloc_semaphore(f"{tag}_{name}")

        ident, eps_col = consts["ident"], consts["eps"]
        w1a, w1b, wd, w2 = sb("w1a", [P, P]), sb("w1b", [P, P]), sb("wd", [P, P]), sb("w2", [P, P])
        b1, b2 = sb("b1", [P, 1]), sb("b2", [P, 1])
        gather_idx = [sb(f"gather_idx{s}", [P, gathers], I32) for s in (0, 1)]
        drow = [sb(f"drow{s}", [P, WIN + 2], I32) for s in (0, 1)]
        rows_in = [sb(f"rows_in{s}", [P, gathers, P]) for s in (0, 1)]
        keep = [sb(f"keep{s}", [P, WIN]) for s in (0, 1)]
        xiT = [sb(f"xiT{s}", [P, WIN]) for s in (0, 1)]
        xjT = [sb(f"xjT{s}", [P, WIN]) for s in (0, 1)]
        hidden = [sb(f"hidden{s}", [P, WIN]) for s in (0, 1)]
        value = [sb(f"value{s}", [P, WIN]) for s in (0, 1)]
        segmax = [sb(f"segmax{s}", [P, WIN]) for s in (0, 1)]
        rows_out = [sb(f"rows_out{s}", [P, TILES, P]) for s in (0, 1)]
        scatter_idx = [sb(f"scatter_idx{s}", [P, TILES], I32) for s in (0, 1)]
        if early:
            early_rows = sb("early_rows", [P, early * TILES, P])
            cleared, early_scattered = sem("cleared"), sem("early_scattered")
        if first:
            stats = [sb(f"stats{s}", [P, gathers, 6]) for s in (0, 1)]
            mean_var = [sb(f"mean_var{s}", [P, gathers, 2]) for s in (0, 1)]
            std = [sb(f"std{s}", [P, gathers]) for s in (0, 1)]
            rstd = [sb(f"rstd{s}", [P, gathers]) for s in (0, 1)]
            shift = [sb(f"shift{s}", [P, gathers]) for s in (0, 1)]
            normed = [sb(f"normed{s}", [P, gathers, P]) for s in (0, 1)]
        else:
            scan_in = [sb(f"scan_in{s}", [P, WIN]) for s in (0, 1)]
        if last:
            penalty = [sb(f"penalty{s}", [P, WIN]) for s in (0, 1)]
            xd = [sb(f"xd{s}", [P, WIN]) for s in (0, 1)]
        ps_xj, ps_xi = banks[0:2], banks[2:4]
        ps_hidden, ps_value, ps_rows = banks[4:7]

        weights_in, wd_ready = sem("weights_in"), sem("wd_ready")
        drow_in = [sem(f"drow_in{s}") for s in (0, 1)]
        gathered = [sem(f"gathered{s}") for s in (0, 1)]
        scattered = [sem(f"scattered{s}") for s in (0, 1)]
        segmax_stored = [sem(f"segmax_stored{s}") for s in (0, 1)]
        if first:
            xd_stored = [sem(f"xd_stored{s}") for s in (0, 1)]
            stats_ready, mean_var_ready, std_ready = sem("stats_ready"), sem("mean_var_ready"), sem("std_ready")
            rstd_ready, shift_ready, normed_ready = sem("rstd_ready"), sem("shift_ready"), sem("normed_ready")
        else:
            scan_in_loaded = [sem(f"scan_in_loaded{s}") for s in (0, 1)]
            xi_ready = sem("xi_ready")
        if last:
            xd_in = [sem(f"xd_in{s}") for s in (0, 1)]
            penalty_ready = sem("penalty_ready")
        bulk_done = sem("bulk_done")
        gather_idx_ready, keep_ready = sem("gather_idx_ready"), sem("keep_ready")
        x_transposed, xT_ready = sem("x_transposed"), sem("xT_ready")
        hidden_summed, hidden_ready = sem("hidden_summed"), sem("hidden_ready")
        value_summed, value_ready = sem("value_summed"), sem("value_ready")
        segmax_ready, scatter_idx_ready = sem("segmax_ready"), sem("scatter_idx_ready")
        rows_transposed, rows_ready = sem("rows_transposed"), sem("rows_ready")

        def at(i, s):
            w = i * 2 + s
            return (windows - 1) - w if backward else w

        def is_early(i, s):
            return isinstance(i, int) and i * 2 + s < early

        def after_early(i):
            return not isinstance(i, int) or i > early // 2

        def run(t):
            return t[:, ::-1] if backward else t[:, :]

        def end(t):
            return t[:, 0:1] if backward else t[:, WIN - 1:WIN]

        go = consts["go"]
        block = ctx.enter_context(nc.Block())

        @block.sync
        def _(sp):
            for t, a in ((w1a, weights["W1"][0:P, :]), (w1b, weights["W1"][P:2 * P, :]), (w2, weights["W2"]),
                         (b1, weights["b1"]), (b2, weights["b2"])):
                sp.dma_start(t[:, :], a).then_inc(weights_in, 16)

            def load(i, s):
                n = i * 2 + s
                if later(i):
                    hold(sp, go, keep_ready, n - 1)
                sp.dma_start(drow[s][:, :], window(dst_row, at(i, s)).to_broadcast([P, WIN + 2])).then_inc(drow_in[s], 16)
                if not first:
                    if later(i):
                        hold(sp, go, xi_ready, n - 1)
                    sp.dma_start(scan_in[s][:, :], window(f_in, at(i, s))).then_inc(scan_in_loaded[s], 16)

            def load_xd(i, s):
                if later(i):
                    hold(sp, go, rows_ready, i * 2 + s - 1)
                sp.dma_start(xd[s][:, :], window(xd_stream, at(i, s))).then_inc(xd_in[s], 16)

            def store(i, s):
                n = i * 2 + s
                hold(sp, go, segmax_ready, n + 1)
                sp.dma_start(window(f_out, at(i, s)), segmax[s][:, :]).then_inc(segmax_stored[s], 16)
                bulk(sp, n, bulk_done)

            def clear_share(i, s):
                if is_early(i, s):
                    n = i * 2 + s
                    for w in range(n * windows // early, (n + 1) * windows // early):
                        clear_out(sp, w, cleared)

            in_steps(sp, windows, 2, (load, 0), (store, 4), *([(load_xd, 2)] if last else []),
                     *([(clear_share, 0)] if early else []), start=early)
            for s in (0, 1):
                sp.wait_ge(segmax_stored[s], 16 * rounds)
                if first:
                    sp.wait_ge(xd_stored[s], 16 * rounds)
            sp.wait_ge(bulk_done, 16 * windows)

        @block.gpsimd
        def _(pool):
            def gather(i, s):
                n = i * 2 + s
                hold(pool, go, gather_idx_ready, n + 1)
                if later(i):
                    if first:
                        hold(pool, go, normed_ready, n - 1)
                        hold(pool, go, xd_stored[s], 16 * i)
                    else:
                        hold(pool, go, x_transposed, n - 1)
                for k in range(gathers):
                    pool.indirect_dma_start(
                        rows_in[s][:, k, :], None, (x_rows if first else table_in)[:, :],
                        bass.IndirectOffsetOnAxis(ap=gather_idx[s][:, k:k + 1], axis=0)).then_inc(gathered[s], 16)

            def scatter_early():
                pool.wait_ge(cleared, 16 * windows)
                for n in range(early):
                    pool.wait_ge(rows_ready, n + 1)
                    for k in range(n * TILES, (n + 1) * TILES):
                        pool.indirect_dma_start(
                            table_out[:, :], bass.IndirectOffsetOnAxis(ap=consts["ends"][:, k:k + 1], axis=0),
                            early_rows[:, k, :], None,
                            bounds_check=table_out.shape[0] - 1, oob_is_err=False).then_inc(early_scattered, 16)

            def scatter(i, s):
                n = i * 2 + s
                if is_early(i, s):
                    if n == early - 1:
                        scatter_early()
                    return
                hold(pool, go, scatter_idx_ready, n + 1 - early)
                hold(pool, go, rows_ready, n + 1)
                for k in range(TILES):
                    pool.indirect_dma_start(
                        table_out[:, :], bass.IndirectOffsetOnAxis(ap=scatter_idx[s][:, k:k + 1], axis=0),
                        rows_out[s][:, k, :], None,
                        bounds_check=table_out.shape[0] - 1, oob_is_err=False).then_inc(scattered[s], 16)

            in_steps(pool, windows, 2, (gather, 0), (scatter, 3), start=early)
            for s in (0, 1):
                pool.wait_ge(scattered[s], 16 * TILES * (rounds - early // 2))
            if early:
                pool.wait_ge(early_scattered, 16 * TILES * early)

        @block.vector
        def _(dve):
            dve.wait_ge(weights_in, 5 * 16)
            nc.vector.tensor_tensor(wd[:, :], w1a[:, :], w1b[:, :], ALU.subtract).then_inc(wd_ready, 1)

            def next_indices(i, s):
                n = i * 2 + s
                if later(i):
                    hold(dve, go, gathered[s], 16 * gathers * i)
                here = bass.ds(at(i, s) * TILES, TILES)
                ins = nc.vector.tensor_copy(gather_idx[s][:, :TILES], consts["src_all"][:, here])
                if first:
                    ins = nc.vector.tensor_copy(gather_idx[s][:, TILES:], consts["dst_all"][:, here])
                ins.then_inc(gather_idx_ready, 1)

            def moments(i, s):
                n = i * 2 + s
                dve.wait_ge(gathered[s], 16 * gathers * (i + 1))
                for k in range(gathers):
                    ins = nc.vector.bn_stats(stats[s][:, k, :], rows_in[s][:, k, :])
                ins.then_inc(stats_ready, 1)
                hold(dve, go, stats_ready, n + 1)
                for k in range(gathers):
                    ins = nc.vector.bn_aggr(mean_var[s][:, k, :], stats[s][:, k, :])
                ins.then_inc(mean_var_ready, 1)

            def scale_and_shift(i, s):
                n = i * 2 + s
                dve.wait_ge(std_ready, n + 1)
                nc.vector.reciprocal(rstd[s][:, :], std[s][:, :]).then_inc(rstd_ready, 1)
                dve.wait_ge(rstd_ready, n + 1)
                nc.vector.scalar_tensor_tensor(shift[s][:, :], mean_var[s][:, :, 0], -1.0, rstd[s][:, :],
                                               ALU.mult, ALU.mult).then_inc(shift_ready, 1)

            def masks(i, s):
                n = i * 2 + s
                dve.wait_ge(drow_in[s], 16 * (i + 1))
                beside = drow[s][:, 2:] if backward else drow[s][:, :WIN]
                nc.vector.tensor_tensor(keep[s][:, :], drow[s][:, 1:WIN + 1], beside, ALU.is_equal).then_inc(keep_ready, 1)
                if last:
                    dve.wait_ge(keep_ready, n + 1)
                    nc.vector.tensor_scalar(penalty[s][:, :], keep[s][:, :], -1.0, HUGE, ALU.add, ALU.mult).then_inc(penalty_ready, 1)

            def spread(i, s):
                n = i * 2 + s
                dve.wait_ge(scan_in_loaded[s], 16 * (i + 1))
                dve.wait_ge(keep_ready, n + 1)
                if later(i):
                    dve.wait_ge(hidden_summed, n - 1)
                if later(i) or s:
                    dve.wait_ge(xi_ready, n)
                nc.vector.tensor_tensor_scan(run(xiT[s]), run(keep[s]), run(scan_in[s]),
                                             end(xiT[1 - s]) if later(i) or s else 0.0,
                                             ALU.mult, ALU.max).then_inc(xi_ready, 1)

            def maxima(i, s):
                n = i * 2 + s
                dve.wait_ge(value_ready, n + 1)
                dve.wait_ge(keep_ready, n + 1)
                if last:
                    dve.wait_ge(penalty_ready, n + 1)
                if later(i):
                    dve.wait_ge(segmax_stored[s], 16 * i)
                    dve.wait_ge(rows_transposed, n - 1)
                if later(i) or s:
                    dve.wait_ge(segmax_ready, n)
                nc.vector.tensor_tensor_scan(run(segmax[s]), run(penalty[s] if last else keep[s]), run(value[s]),
                                             end(segmax[1 - s]) if later(i) or s else 0.0,
                                             ALU.add if last else ALU.mult, ALU.max).then_inc(segmax_ready, 1)

            def rows(i, s):
                n = i * 2 + s
                if is_early(i, s):
                    dve.wait_ge(rows_transposed, n + 1)
                    nc.vector.tensor_copy(early_rows[:, n * TILES:(n + 1) * TILES, :].rearrange("p k f -> p (k f)"),
                                          ps_rows[:, :]).then_inc(rows_ready, 1)
                    return
                if after_early(i):
                    hold(dve, go, scattered[s], 16 * TILES * (i - early // 2))
                nc.vector.tensor_copy(scatter_idx[s][:, :], consts["firsts" if backward else "ends"][:, bass.ds(at(i, s) * TILES, TILES)]
                                      ).then_inc(scatter_idx_ready, 1)
                dve.wait_ge(rows_transposed, n + 1)
                out = rows_out[s][:, :, :].rearrange("p k f -> p (k f)")
                if last:
                    dve.wait_ge(xd_in[s], 16 * (i + 1))
                    nc.vector.tensor_tensor(out, ps_rows[:, :], xd[s][:, :], ALU.add).then_inc(rows_ready, 1)
                else:
                    nc.vector.tensor_copy(out, ps_rows[:, :]).then_inc(rows_ready, 1)

            if first:
                in_steps(dve, windows, 2, (moments, 2), (maxima, 4), (scale_and_shift, 2), (rows, 4), (masks, 2),
                         (next_indices, 0), start=early)
            else:
                in_steps(dve, windows, 2, (maxima, 4), (rows, 4), (masks, 2), (spread, 2), (next_indices, 0))

        @block.scalar
        def _(act):
            act.wait_ge(weights_in, 5 * 16)

            def roots(i, s):
                n = i * 2 + s
                act.wait_ge(mean_var_ready, n + 1)
                nc.scalar.activation(std[s][:, :], mean_var[s][:, :, 1], ACT.Sqrt, bias=eps_col[:, :]).then_inc(std_ready, 1)
                act.dma_start(window(xd_stream, at(i, s)),
                              rows_in[s][:, TILES:, :].rearrange("p k f -> p (k f)")).then_inc(xd_stored[s], 16)

            def normalise(i, s):
                n = i * 2 + s
                act.wait_ge(shift_ready, n + 1)
                if later(i):
                    act.wait_ge(x_transposed, n - 1)
                for k in range(gathers):
                    ins = nc.scalar.activation(normed[s][:, k, :], rows_in[s][:, k, :], ACT.Relu,
                                               bias=shift[s][:, k:k + 1], scale=rstd[s][:, k:k + 1])
                ins.then_inc(normed_ready, 1)

            def move_x(i, s):
                n = i * 2 + s
                act.wait_ge(x_transposed, n + 1)
                if later(i):
                    act.wait_ge(hidden_summed, n - 1)
                if first:
                    nc.scalar.copy(xiT[s][:, :], ps_xi[s][:, :])
                nc.scalar.copy(xjT[s][:, :], ps_xj[s][:, :]).then_inc(xT_ready, 1)

            def layer1(i, s):
                n = i * 2 + s
                act.wait_ge(hidden_summed, n + 1)
                if later(i):
                    act.wait_ge(value_summed, n - 1)
                nc.scalar.activation(hidden[s][:, :], ps_hidden[:, :], ACT.Relu, bias=b1[:, :]).then_inc(hidden_ready, 1)

            def layer2(i, s):
                n = i * 2 + s
                act.wait_ge(value_summed, n + 1)
                if later(i):
                    act.wait_ge(segmax_ready, n - 1)
                nc.scalar.activation(value[s][:, :], ps_value[:, :], ACT.Identity if last else ACT.Relu,
                                     bias=b2[:, :]).then_inc(value_ready, 1)

            if first:
                in_steps(act, windows, 2, (roots, 0), (layer2, 2), (layer1, 1), (normalise, 0), (move_x, 0))
            else:
                in_steps(act, windows, 2, (layer2, 2), (layer1, 1), (move_x, 0))

        @block.tensor
        def _(pe):
            def turn_x(i, s):
                n = i * 2 + s
                if first:
                    pe.wait_ge(normed_ready, n + 1)
                else:
                    pe.wait_ge(gathered[s], 16 * gathers * (i + 1))
                if later(i):
                    pe.wait_ge(xT_ready, n - 1)
                for k in range(gathers):
                    to = (ps_xj if k < TILES else ps_xi)[s]
                    k4 = k % TILES
                    ins = nc.tensor.transpose(to[:, k4 * P:(k4 + 1) * P], (normed if first else rows_in)[s][:, k, :], ident[:, :])
                ins.then_inc(x_transposed, 1)

            def layer1(i, s):
                n = i * 2 + s
                pe.wait_ge(xT_ready, n + 1)
                if not first:
                    pe.wait_ge(xi_ready, n + 1)
                if later(i) or s:
                    pe.wait_ge(hidden_ready, n)
                nc.tensor.matmul(ps_hidden[:, :], w1b[:, :], xjT[s][:, :], start=True, stop=False)
                nc.tensor.matmul(ps_hidden[:, :], wd[:, :], xiT[s][:, :], start=False, stop=True).then_inc(hidden_summed, 1)

            def layer2(i, s):
                n = i * 2 + s
                pe.wait_ge(hidden_ready, n + 1)
                if later(i) or s:
                    pe.wait_ge(value_ready, n)
                nc.tensor.matmul(ps_value[:, :], w2[:, :], hidden[s][:, :], start=True, stop=True).then_inc(value_summed, 1)

            def turn_maxima(i, s):
                n = i * 2 + s
                pe.wait_ge(segmax_ready, n + 1)
                if later(i) or s:
                    pe.wait_ge(rows_ready, n)
                for k in range(TILES):
                    ins = nc.tensor.transpose(ps_rows[:, k * P:(k + 1) * P], segmax[s][:, k * P:(k + 1) * P], ident[:, :])
                ins.then_inc(rows_transposed, 1)

            pe.wait_ge(weights_in, 5 * 16)
            pe.wait_ge(wd_ready, 1)
            in_steps(pe, windows, 2, (layer2, 2), (layer1, 1), (turn_maxima, 2), (turn_x, 0))


def score_pass(nc, consts, *, dst_row, type_row, x1_table, f_in, xd_stream, et_stream, rel, scores, windows):
    ctx = ExitStack()
    with ctx:
        ctx.enter_context(nc.cleanup_on_exit())
        banks = consts["banks"]

        def sb(name, shape, dt=F32):
            return ctx.enter_context(nc.sbuf_tensor(f"sc_{name}", shape, dt))

        def sem(name):
            return nc.alloc_semaphore(f"sc_{name}")

        SIDES = 2 * TILES
        ident, relation_col = consts["ident"], consts["relation_col"]
        rel_sb = sb("rel", [RELATIONS, P])
        gather_idx = [sb(f"gather_idx{s}", [P, TILES], I32) for s in (0, 1)]
        drow = [sb(f"drow{s}", [P, WIN + 2], I32) for s in (0, 1)]
        trow = [sb(f"trow{s}", [RELATIONS, WIN], I32) for s in (0, 1)]
        scan_in = [sb(f"scan_in{s}", [P, WIN]) for s in (0, 1)]
        xd = [sb(f"xd{s}", [P, WIN]) for s in (0, 1)]
        keep = [sb(f"keep{s}", [P, WIN]) for s in (0, 1)]
        penalty = [sb(f"penalty{s}", [P, WIN]) for s in (0, 1)]
        full = [sb(f"full{s}", [P, WIN]) for s in (0, 1)]
        onehot = [sb(f"onehot{s}", [RELATIONS, WIN]) for s in (0, 1)]
        U = 4
        sides = [sb(f"sides{s}", [P, SIDES, P]) for s in range(U)]
        stats = [sb(f"stats{s}", [P, SIDES, 6]) for s in (0, 1)]
        mean_var = [sb(f"mean_var{s}", [P, SIDES, 2]) for s in (0, 1)]
        var_eps = [sb(f"var_eps{s}", [P, SIDES]) for s in (0, 1)]
        rstd = [sb(f"rstd{s}", [P, SIDES]) for s in (0, 1)]
        shift = [sb(f"shift{s}", [P, SIDES]) for s in (0, 1)]
        normed = [sb(f"normed{s}", [P, SIDES, P]) for s in range(U)]
        tanh_sb = [sb(f"tanh{s}", [P, WIN]) for s in (0, 1)]
        product = [sb(f"product{s}", [P, TILES, P]) for s in (0, 1)]
        ps_full, ps_arg = banks[0:2], banks[2:4]

        rel_in = sem("rel_in")
        drow_in = [sem(f"drow_in{s}") for s in (0, 1)]
        trow_in = [sem(f"trow_in{s}") for s in (0, 1)]
        scan_in_loaded = [sem(f"scan_in_loaded{s}") for s in (0, 1)]
        xd_in = [sem(f"xd_in{s}") for s in (0, 1)]
        gathered = [sem(f"gathered{s}") for s in (0, 1)]
        et_stored = [sem(f"et_stored{s}") for s in range(U)]
        keep_ready, penalty_ready, full_ready, onehot_ready = sem("keep_ready"), sem("penalty_ready"), sem("full_ready"), sem("onehot_ready")
        full_transposed, xt_ready, stats_ready = sem("full_transposed"), sem("xt_ready"), sem("stats_ready")
        mean_var_ready, var_ready, rstd_ready, shift_ready = sem("mean_var_ready"), sem("var_ready"), sem("rstd_ready"), sem("shift_ready")
        gather_idx_ready = sem("gather_idx_ready")
        normed_ready, arg_summed, tanh_ready = sem("normed_ready"), sem("arg_summed"), sem("tanh_ready")
        product_ready, score_ready = sem("product_ready"), sem("score_ready")

        def at(i, s):
            return (windows - 1) - (i * U + s)

        def names(i, s):
            return i * U + s, s % 2, i * (U // 2) + s // 2, later(i) or s > 1

        go = consts["go"]
        block = ctx.enter_context(nc.Block())

        @block.sync
        def _(sp):
            sp.dma_start(rel_sb[:, :], rel).then_inc(rel_in, 16)

            def load_destinations(i, s):
                n, t, before, reused = names(i, s)
                if reused:
                    hold(sp, go, keep_ready, n - 1)
                sp.dma_start(drow[t][:, :], window(dst_row, at(i, s)).to_broadcast([P, WIN + 2])).then_inc(drow_in[t], 16)

            def load_maxima(i, s):
                n, t, before, reused = names(i, s)
                if reused:
                    hold(sp, go, full_ready, n - 1)
                sp.dma_start(scan_in[t][:, :], window(f_in, at(i, s))).then_inc(scan_in_loaded[t], 16)

            def load_xd(i, s):
                n, t, before, reused = names(i, s)
                if reused:
                    hold(sp, go, xt_ready, n - 1)
                sp.dma_start(xd[t][:, :], window(xd_stream, at(i, s))).then_inc(xd_in[t], 16)

            def load_relations(i, s):
                n, t, before, reused = names(i, s)
                if reused:
                    hold(sp, go, onehot_ready, n - 1)
                sp.dma_start(trow[t][:, :], window(type_row, at(i, s)).to_broadcast([RELATIONS, WIN])).then_inc(trow_in[t], 16)

            def store(i, s):
                n, t, before, reused = names(i, s)
                hold(sp, go, normed_ready, n + 1)
                sp.dma_start(window(et_stream, at(i, s)),
                             normed[s][:, TILES:, :].rearrange("p k f -> p (k f)")).then_inc(et_stored[s], 16)

            in_steps(sp, windows, U, (load_destinations, 0), (load_maxima, 1), (load_xd, 2), (load_relations, 2), (store, 6))
            for s in range(U):
                sp.wait_ge(et_stored[s], 16 * (-(-(windows - s) // U)))

        @block.gpsimd
        def _(pool):
            def gather(i, s):
                n, t, before, reused = names(i, s)
                hold(pool, go, gather_idx_ready, n + 1)
                if later(i):
                    hold(pool, go, normed_ready, n - (U - 1))
                for k in range(TILES):
                    pool.indirect_dma_start(
                        sides[s][:, k, :], None, x1_table[:, :],
                        bass.IndirectOffsetOnAxis(ap=gather_idx[t][:, k:k + 1], axis=0)).then_inc(gathered[t], 16)

            def roots(i, s):
                n, t, before, reused = names(i, s)
                hold(pool, go, var_ready, n + 1)
                if reused:
                    hold(pool, go, normed_ready, n - 1)
                nc.gpsimd.tensor_tensor(rstd[t][:, :], var_eps[t][:, :], consts["minus_half"][:, :], ALU.pow).then_inc(rstd_ready, 1)

            in_steps(pool, windows, U, (gather, 0), (roots, 2))

        @block.vector
        def _(dve):
            def next_indices(i, s):
                n, t, before, reused = names(i, s)
                if reused:
                    hold(dve, go, gathered[t], 16 * TILES * before)
                nc.vector.tensor_copy(gather_idx[t][:, :], consts["src_all"][:, bass.ds(at(i, s) * TILES, TILES)]).then_inc(gather_idx_ready, 1)

            def masks(i, s):
                n, t, before, reused = names(i, s)
                dve.wait_ge(drow_in[t], 16 * (before + 1))
                if reused:
                    dve.wait_ge(penalty_ready, n - 1)
                nc.vector.tensor_tensor(keep[t][:, :], drow[t][:, 1:WIN + 1], drow[t][:, 2:], ALU.is_equal).then_inc(keep_ready, 1)

            def relations(i, s):
                n, t, before, reused = names(i, s)
                dve.wait_ge(trow_in[t], 16 * (before + 1))
                if reused:
                    dve.wait_ge(arg_summed, n - 1)
                nc.vector.tensor_scalar(onehot[t][:, :], trow[t][:, :], relation_col[:, :], None, ALU.is_equal).then_inc(onehot_ready, 1)

            def spread(i, s):
                n, t, before, reused = names(i, s)
                dve.wait_ge(scan_in_loaded[t], 16 * (before + 1))
                dve.wait_ge(penalty_ready, n + 1)
                if reused:
                    dve.wait_ge(full_transposed, n - 1)
                if later(i) or s:
                    dve.wait_ge(full_ready, n)
                nc.vector.tensor_tensor_scan(full[t][:, ::-1], penalty[t][:, ::-1], scan_in[t][:, ::-1],
                                             full[1 - t][:, 0:1] if later(i) or s else 0.0,
                                             ALU.add, ALU.max).then_inc(full_ready, 1)

            def moments(i, s):
                n, t, before, reused = names(i, s)
                dve.wait_ge(full_transposed, n + 1)
                dve.wait_ge(xd_in[t], 16 * (before + 1))
                if later(i):
                    dve.wait_ge(normed_ready, n - (U - 1))
                nc.vector.tensor_tensor(sides[s][:, TILES:, :].rearrange("p k f -> p (k f)"), ps_full[t][:, :], xd[t][:, :],
                                        ALU.add).then_inc(xt_ready, 1)
                dve.wait_ge(gathered[t], 16 * TILES * (before + 1))
                for k in range(TILES):
                    nc.vector.bn_stats(stats[t][:, k, :], sides[s][:, k, :])
                dve.wait_ge(xt_ready, n + 1)
                for k in range(TILES, SIDES):
                    ins = nc.vector.bn_stats(stats[t][:, k, :], sides[s][:, k, :])
                ins.then_inc(stats_ready, 1)

            def aggregates(i, s):
                n, t, before, reused = names(i, s)
                hold(dve, go, stats_ready, n + 1)
                for k in range(SIDES):
                    ins = nc.vector.bn_aggr(mean_var[t][:, k, :], stats[t][:, k, :])
                ins.then_inc(mean_var_ready, 1)

            def variances(i, s):
                n, t, before, reused = names(i, s)
                dve.wait_ge(mean_var_ready, n + 1)
                if reused:
                    dve.wait_ge(rstd_ready, n - 1)
                nc.vector.tensor_scalar(var_eps[t][:, :], mean_var[t][:, :, 1], EPS, None, ALU.add).then_inc(var_ready, 1)

            def shifts(i, s):
                n, t, before, reused = names(i, s)
                dve.wait_ge(rstd_ready, n + 1)
                if reused:
                    dve.wait_ge(normed_ready, n - 1)
                nc.vector.scalar_tensor_tensor(shift[t][:, :], mean_var[t][:, :, 0], -1.0, rstd[t][:, :],
                                               ALU.mult, ALU.mult).then_inc(shift_ready, 1)

            def products(i, s):
                n, t, before, reused = names(i, s)
                dve.wait_ge(tanh_ready, n + 1)
                nc.vector.tensor_tensor(product[t][:, :, :].rearrange("p k f -> p (k f)"), tanh_sb[t][:, :],
                                        normed[s][:, TILES:, :].rearrange("p k f -> p (k f)"), ALU.mult).then_inc(product_ready, 1)

            def score(i, s):
                n, t, before, reused = names(i, s)
                hold(dve, go, product_ready, n + 1)
                nc.vector.tensor_reduce(scores[:, bass.ds(at(i, s) * TILES, TILES)], product[t][:, :, :], AX.X, ALU.add).then_inc(score_ready, 1)

            in_steps(dve, windows, U, (spread, 3), (moments, 4), (next_indices, 1), (aggregates, 4), (variances, 4),
                     (masks, 2), (products, 7), (relations, 4), (score, 7), (shifts, 4))

        @block.scalar
        def _(act):
            def penalties(i, s):
                n, t, before, reused = names(i, s)
                act.wait_ge(keep_ready, n + 1)
                if reused:
                    act.wait_ge(full_ready, n - 1)
                nc.scalar.activation(penalty[t][:, :], keep[t][:, :], ACT.Identity, bias=consts["minus_huge"][:, :],
                                     scale=HUGE).then_inc(penalty_ready, 1)

            def normalise(i, s):
                n, t, before, reused = names(i, s)
                act.wait_ge(shift_ready, n + 1)
                if later(i):
                    act.wait_ge(arg_summed, n - (U - 1))
                    act.wait_ge(product_ready, n - (U - 1))
                    act.wait_ge(et_stored[s], 16 * i)
                for k in range(SIDES):
                    ins = nc.scalar.activation(normed[s][:, k, :], sides[s][:, k, :], ACT.Relu,
                                               bias=shift[t][:, k:k + 1], scale=rstd[t][:, k:k + 1])
                ins.then_inc(normed_ready, 1)

            def tanhs(i, s):
                n, t, before, reused = names(i, s)
                act.wait_ge(arg_summed, n + 1)
                if reused:
                    act.wait_ge(product_ready, n - 1)
                nc.scalar.activation(tanh_sb[t][:, :], ps_arg[t][:, :], ACT.Tanh).then_inc(tanh_ready, 1)

            in_steps(act, windows, U, (penalties, 0), (tanhs, 4), (normalise, 2))

        @block.tensor
        def _(pe):
            def turn_maxima(i, s):
                n, t, before, reused = names(i, s)
                pe.wait_ge(full_ready, n + 1)
                if reused:
                    pe.wait_ge(xt_ready, n - 1)
                for k in range(TILES):
                    ins = nc.tensor.transpose(ps_full[t][:, k * P:(k + 1) * P], full[t][:, k * P:(k + 1) * P], ident[:, :])
                ins.then_inc(full_transposed, 1)

            def argument(i, s):
                n, t, before, reused = names(i, s)
                pe.wait_ge(normed_ready, n + 1)
                pe.wait_ge(onehot_ready, n + 1)
                if reused:
                    pe.wait_ge(tanh_ready, n - 1)
                nc.tensor.matmul(ps_arg[t][:, :], ident[:, :], normed[s][:, :TILES, :].rearrange("p k f -> p (k f)"),
                                 start=True, stop=False)
                for k in range(TILES):
                    ins = nc.tensor.matmul(ps_arg[t][:, k * P:(k + 1) * P], onehot[t][:, k * P:(k + 1) * P], rel_sb[:, :],
                                           start=False, stop=k == TILES - 1)
                ins.then_inc(arg_summed, 1)

            pe.wait_ge(rel_in, 16)
            in_steps(pe, windows, U, (argument, 3), (turn_maxima, 0))


def softmax_pass(nc, consts, *, scores, weights, edges_padded_from):
    ctx = ExitStack()
    with ctx:
        ctx.enter_context(nc.cleanup_on_exit())
        n = scores.shape[1]
        dst_sb = consts["dst_seg_all"]
        pad = ctx.enter_context(nc.sbuf_tensor("sm_pad", [P, n], F32))
        masked = ctx.enter_context(nc.sbuf_tensor("sm_masked", [P, n], F32))
        largest = ctx.enter_context(nc.sbuf_tensor("sm_largest", [P, 1], F32))
        largest_one = ctx.enter_context(nc.sbuf_tensor("sm_largest_one", [1, 1], F32))
        as_row, on_all = consts["banks"][0][0:1, :P], consts["banks"][1][:, 0:1]
        minus_largest = ctx.enter_context(nc.sbuf_tensor("sm_minus_largest", [P, 1], F32))
        masked_ready = nc.alloc_semaphore("sm_masked_ready")
        largest_ready = nc.alloc_semaphore("sm_largest_ready")
        row_ready = nc.alloc_semaphore("sm_row_ready")
        all_ready = nc.alloc_semaphore("sm_all_ready")
        minus_ready = nc.alloc_semaphore("sm_minus_ready")
        weights_ready = nc.alloc_semaphore("sm_weights_ready")
        go = consts["go"]
        block = ctx.enter_context(nc.Block())

        @block.vector
        def _(dve):
            nc.vector.tensor_scalar(pad[:, :], dst_sb[:, :], float(edges_padded_from), -HUGE, ALU.is_ge, ALU.mult).then_inc(masked_ready, 1)
            dve.wait_ge(masked_ready, 1)
            nc.vector.tensor_tensor(masked[:, :], scores[:, :], pad[:, :], ALU.add).then_inc(masked_ready, 1)
            dve.wait_ge(masked_ready, 2)
            nc.vector.tensor_reduce(largest[:, :], masked[:, :], AX.X, ALU.max).then_inc(largest_ready, 1)
            dve.wait_ge(row_ready, 1)
            nc.vector.tensor_reduce(largest_one[:, :], as_row[:, :], AX.X, ALU.max).then_inc(largest_ready, 1)
            dve.wait_ge(all_ready, 1)
            nc.vector.tensor_scalar(minus_largest[:, :], on_all[:, :], -1.0, None, ALU.mult).then_inc(minus_ready, 1)

        @block.tensor
        def _(pe):
            pe.wait_ge(largest_ready, 1)
            nc.tensor.transpose(as_row[:, :], largest[:, :], consts["ident"][:, :]).then_inc(row_ready, 1)
            pe.wait_ge(largest_ready, 2)
            nc.tensor.matmul(on_all[:, :], consts["ones"][0:1, :P], largest_one[:, :], start=True, stop=True).then_inc(all_ready, 1)

        @block.scalar
        def _(act):
            act.wait_ge(minus_ready, 1)
            nc.scalar.activation(weights[:, :], masked[:, :], ACT.Exp, bias=minus_largest[:, :]).then_inc(weights_ready, 1)


def sum_pass(nc, consts, *, src_row, et_stream, sums_table, weights, windows):
    U = 2
    groups = windows * WIN // GROUP
    per_group = GROUP // WIN
    first_column = [sum(GROUP_TILES - c for c in range(b)) * P for b in range(GROUP_TILES + 1)]
    ctx = ExitStack()
    with ctx:
        ctx.enter_context(nc.cleanup_on_exit())
        banks = consts["banks"]

        def sb(name, shape, dt=F32):
            return [ctx.enter_context(nc.sbuf_tensor(f"sum_{name}{s}", shape, dt)) for s in range(U)]

        def sem(name):
            return nc.alloc_semaphore(f"sum_{name}")

        not_before, spare_rows = consts["not_before"], consts["spare_rows"]
        src_f, wcol, srow = sb("src_f", [P, GROUP_TILES]), sb("wcol", [P, GROUP_TILES]), sb("srow", [P, GROUP], I32)
        et, weighted = sb("et", [P, GROUP_TILES, SUM_W]), sb("weighted", [P, GROUP_TILES, SUM_W])
        equal = sb("equal", [P, first_column[-1]])
        n_from, to_spare, move = sb("n_from", [P, GROUP_TILES]), sb("to_spare", [P, GROUP_TILES]), sb("move", [P, GROUP_TILES])
        scatter_idx = sb("scatter_idx", [P, GROUP_TILES], I32)
        summed = sb("summed", [P, GROUP_TILES, SUM_W])
        half = GROUP_TILES // 2
        ps_sum = [[t[:, :2 * SUM_W].rearrange("p (k f) -> p k f", k=2) for t in banks[s * half:(s + 1) * half]] for s in range(U)]

        ones_ready = sem("ones_ready")
        srow_in, et_in = [sem(f"srow_in{s}") for s in range(U)], [sem(f"et_in{s}") for s in range(U)]
        scattered = sem("scattered")
        src_f_ready, wcol_ready, weighted_ready, equal_ready = sem("src_f_ready"), sem("wcol_ready"), sem("weighted_ready"), sem("equal_ready")
        spare_ready, move_ready, idx_ready = sem("spare_ready"), sem("move_ready"), sem("idx_ready")
        sums_made, summed_ready = sem("sums_made"), sem("summed_ready")

        go = consts["go"]
        block = ctx.enter_context(nc.Block())

        @block.sync
        def _(sp):
            sp.wait_ge(ones_ready, U)

            def load(i, s):
                n = i * U + s
                if later(i):
                    hold(sp, go, equal_ready, n - 1)
                sp.dma_start(srow[s][:, :].rearrange("p (w e) -> p w e", w=per_group),
                             src_row[bass.ds(n * per_group, per_group)].rearrange("w o e -> o w e").to_broadcast([P, per_group, WIN])
                             ).then_inc(srow_in[s], 16)
                if later(i):
                    hold(sp, go, weighted_ready, n - 1)
                for w in range(per_group):
                    sp.dma_start(et[s][:, w * TILES:(w + 1) * TILES, :P],
                                 window(et_stream, n * per_group + w).rearrange("p (k f) -> p k f", k=TILES)).then_inc(et_in[s], 16)

            in_steps(sp, groups, U, (load, 0))

        @block.vector
        def _(dve):
            for s in range(U):
                nc.vector.memset(et[s][:, :, P:], 1.0).then_inc(ones_ready, 1)

            def edges(i, s):
                n = i * U + s
                here = bass.ds(n * GROUP_TILES, GROUP_TILES)
                nc.vector.tensor_copy(src_f[s][:, :], consts["src_all"][:, here]).then_inc(src_f_ready, 1)
                nc.vector.tensor_copy(wcol[s][:, :], weights[:, here]).then_inc(wcol_ready, 1)
                dve.wait_ge(srow_in[s], 16 * (i + 1))
                dve.wait_ge(src_f_ready, n + 1)
                if later(i):
                    dve.wait_ge(sums_made, n - 1)
                for b in range(GROUP_TILES):
                    ins = nc.vector.scalar_tensor_tensor(equal[s][:, first_column[b]:first_column[b + 1]], srow[s][:, b * P:],
                                                         src_f[s][:, b:b + 1], not_before[:, :GROUP - b * P],
                                                         ALU.is_equal, ALU.mult, accum_out=n_from[s][:, b:b + 1])
                ins.then_inc(equal_ready, 1)
                dve.wait_ge(et_in[s], 16 * per_group * (i + 1))
                dve.wait_ge(wcol_ready, n + 1)
                nc.vector.tensor_tensor(weighted[s][:, :, :], et[s][:, :, :],
                                        wcol[s][:, :].unsqueeze(2).to_broadcast([P, GROUP_TILES, SUM_W]), ALU.mult).then_inc(weighted_ready, 1)
                nc.vector.tensor_tensor(to_spare[s][:, :], spare_rows[:, :], src_f[s][:, :], ALU.subtract).then_inc(spare_ready, 1)
                dve.wait_ge(equal_ready, n + 1)
                dve.wait_ge(spare_ready, n + 1)
                nc.vector.scalar_tensor_tensor(move[s][:, :], n_from[s][:, :], 1.0, to_spare[s][:, :],
                                               ALU.is_gt, ALU.mult).then_inc(move_ready, 1)
                dve.wait_ge(move_ready, n + 1)
                if later(i):
                    dve.wait_ge(scattered, 16 * GROUP_TILES * (n - 1))
                nc.vector.tensor_tensor(scatter_idx[s][:, :], move[s][:, :], src_f[s][:, :], ALU.add).then_inc(idx_ready, 1)

            in_steps(dve, groups, U, (edges, 0))

        @block.tensor
        def _(pe):
            def sums(i, s):
                n = i * U + s
                pe.wait_ge(equal_ready, n + 1)
                pe.wait_ge(weighted_ready, n + 1)
                if later(i):
                    pe.wait_ge(summed_ready, n - 1)
                for a in range(GROUP_TILES):
                    for b in range(a + 1):
                        column = first_column[b] + (a - b) * P
                        ins = nc.tensor.matmul(ps_sum[s][a // 2][:, a % 2, :], equal[s][:, column:column + P],
                                               weighted[s][:, b, :], start=b == 0, stop=b == a)
                ins.then_inc(sums_made, 1)

            in_steps(pe, groups, U, (sums, 0))

        @block.scalar
        def _(act):
            def move_out(i, s):
                n = i * U + s
                act.wait_ge(sums_made, n + 1)
                if later(i):
                    act.wait_ge(scattered, 16 * GROUP_TILES * (n - 1))
                for b in range(half):
                    ins = nc.scalar.copy(summed[s][:, 2 * b:2 * b + 2, :], ps_sum[s][b])
                ins.then_inc(summed_ready, 1)

            in_steps(act, groups, U, (move_out, 0))

        @block.gpsimd
        def _(pool):
            def scatter(i, s):
                n = i * U + s
                hold(pool, go, idx_ready, n + 1)
                hold(pool, go, summed_ready, n + 1)
                if later(i) or s:
                    hold(pool, go, scattered, 16 * GROUP_TILES * n)
                for k in range(GROUP_TILES):
                    pool.indirect_dma_start(
                        sums_table[:, :], bass.IndirectOffsetOnAxis(ap=scatter_idx[s][:, k:k + 1], axis=0),
                        summed[s][:, k, :], None, compute_op=ALU.add).then_inc(scattered, 16)

            in_steps(pool, groups, U, (scatter, 0))
            pool.wait_ge(scattered, 16 * GROUP_TILES * groups)


def node_pass(nc, consts, *, x1_table, sums_table, wt, out, nodes):
    rows = P * PIECE
    full_pieces = nodes // rows
    tail = (nodes - full_pieces * rows) // PIECE
    pieces = full_pieces + (1 if tail else 0)
    assert tail * PIECE == nodes - full_pieces * rows
    U = 8
    HALVES = PIECE // TILES
    ctx = ExitStack()
    with ctx:
        ctx.enter_context(nc.cleanup_on_exit())
        banks = consts["banks"]

        def sb(name, shape, slots):
            return [ctx.enter_context(nc.sbuf_tensor(f"n_{name}{s}", shape, F32)) for s in range(slots)]

        def sem(name):
            return nc.alloc_semaphore(f"n_{name}")

        ident, eps_col = consts["ident"], consts["eps"]
        wt_sb = sb("wt", [P, P], 1)[0]
        x1, sums = sb("x1", [P, PIECE, P], U), sb("sums", [P, PIECE, SUM_W], U)
        stats, mean_var = sb("stats", [P, PIECE, 6], 2), sb("mean_var", [P, PIECE, 2], 2)
        std, rstd, shift = sb("std", [P, PIECE], 2), sb("rstd", [P, PIECE], 2), sb("shift", [P, PIECE], 2)
        weight, rweight = sb("weight", [P, PIECE], 2), sb("rweight", [P, PIECE], 2)
        h, mean_agg, with_agg = sb("h", [P, PIECE, P], 2), sb("mean_agg", [P, PIECE, P], 2), sb("with_agg", [P, PIECE, P], 2)
        transposed, fifth = sb("transposed", [P, PIECE, P], 2), sb("fifth", [P, PIECE, P], 2)
        leaky, result = sb("leaky", [P, PIECE, P], 2), sb("result", [P, PIECE, P], 2)
        by_tile = [t[:, :].rearrange("p (k f) -> p k f", k=TILES) for t in banks]
        ps_t, ps_o = (by_tile[0:2], by_tile[2:4]), (by_tile[4:6], by_tile[6:8])

        wt_in = sem("wt_in")
        x1_in = [sem(f"x1_in{s}") for s in range(U)]
        sums_in = [sem(f"sums_in{s}") for s in range(U)]
        stored = [sem(f"stored{s}") for s in range(U)]
        stats_ready, mean_var_ready, std_ready, rstd_ready, shift_ready = (
            sem("stats_ready"), sem("mean_var_ready"), sem("std_ready"), sem("rstd_ready"), sem("shift_ready"))
        weight_ready, rweight_ready, h_ready = sem("weight_ready"), sem("rweight_ready"), sem("h_ready")
        mean_agg_ready, with_agg_ready = sem("mean_agg_ready"), sem("with_agg_ready")
        turned, transposed_ready, multiplied = sem("turned"), sem("transposed_ready"), sem("multiplied")
        fifth_ready, leaky_ready, result_ready = sem("fifth_ready"), sem("leaky_ready"), sem("result_ready")
        go = consts["go"]
        block = ctx.enter_context(nc.Block())

        def piece(table, n, parts):
            return table[bass.ds(n * rows, parts * PIECE), :].rearrange("(p j) f -> p j f", j=PIECE)

        def parts_of(i, s):
            return tail if tail and isinstance(i, int) and i * U + s == full_pieces else P

        def has_before(i, s):
            return later(i) or s > 1

        @block.sync
        def _(sp):
            sp.dma_start(wt_sb[:, :], wt).then_inc(wt_in, 16)

            def load(i, s):
                n, p = i * U + s, parts_of(i, s)
                if later(i):
                    hold(sp, go, result_ready, n - (U - 1))
                sp.dma_start(x1[s][:p, :, :], piece(x1_table, n, p)).then_inc(x1_in[s], 16)
                if later(i):
                    hold(sp, go, mean_agg_ready, n - (U - 1))
                sp.dma_start(sums[s][:p, :, :], piece(sums_table, n, p)).then_inc(sums_in[s], 16)

            def store(i, s):
                n, p = i * U + s, parts_of(i, s)
                hold(sp, go, result_ready, n + 1)
                sp.dma_start(piece(out, n, p), result[s % 2][:p, :, :]).then_inc(stored[s], 16)

            in_steps(sp, pieces, U, (store, 8), (load, 0))
            for s in range(U):
                sp.wait_ge(stored[s], 16 * (-(-(pieces - s) // U)))

        @block.gpsimd
        def _(pool):
            def finish(i, s):
                n, p = i * U + s, parts_of(i, s)
                pool.wait_ge(leaky_ready, n + 1)
                if has_before(i, s):
                    pool.wait_ge(stored[(s - 2) % U], 16 * (i + 1 if s > 1 else i))
                nc.gpsimd.tensor_tensor(result[s % 2][:p, :, :], leaky[s % 2][:p, :, :], x1[s][:p, :, :], ALU.add).then_inc(result_ready, 1)

            def means(i, s):
                n, p, t = i * U + s, parts_of(i, s), s % 2
                pool.wait_ge(rweight_ready, n + 1)
                if has_before(i, s):
                    pool.wait_ge(with_agg_ready, n - 1)
                nc.gpsimd.tensor_tensor(mean_agg[t][:p, :, :], sums[s][:p, :, :P],
                                        rweight[t][:p, :].unsqueeze(2).to_broadcast([p, PIECE, P]), ALU.mult).then_inc(mean_agg_ready, 1)

            in_steps(pool, pieces, U, (finish, 4), (means, 0))

        @block.vector
        def _(dve):
            def moments(i, s):
                n, p, t = i * U + s, parts_of(i, s), s % 2
                dve.wait_ge(x1_in[s], 16 * (i + 1))
                for k in range(PIECE):
                    ins = nc.vector.bn_stats(stats[t][:p, k, :], x1[s][:p, k, :])
                ins.then_inc(stats_ready, 1)
                dve.wait_ge(sums_in[s], 16 * (i + 1))
                nc.vector.tensor_scalar(weight[t][:p, :], sums[s][:p, :, P], 1e-10, None, ALU.add).then_inc(weight_ready, 1)
                hold(dve, go, stats_ready, n + 1)
                for k in range(PIECE):
                    ins = nc.vector.bn_aggr(mean_var[t][:p, k, :], stats[t][:p, k, :])
                ins.then_inc(mean_var_ready, 1)
                dve.wait_ge(weight_ready, n + 1)
                if has_before(i, s):
                    dve.wait_ge(mean_agg_ready, n - 1)
                nc.vector.reciprocal(rweight[t][:p, :], weight[t][:p, :]).then_inc(rweight_ready, 1)

            def scale_and_shift(i, s):
                n, p, t = i * U + s, parts_of(i, s), s % 2
                dve.wait_ge(std_ready, n + 1)
                nc.vector.reciprocal(rstd[t][:p, :], std[t][:p, :]).then_inc(rstd_ready, 1)
                dve.wait_ge(rstd_ready, n + 1)
                nc.vector.scalar_tensor_tensor(shift[t][:p, :], mean_var[t][:p, :, 0], -1.0, rstd[t][:p, :],
                                               ALU.mult, ALU.mult).then_inc(shift_ready, 1)

            def attention(i, s):
                n, p, t = i * U + s, parts_of(i, s), s % 2
                dve.wait_ge(h_ready, n + 1)
                dve.wait_ge(mean_agg_ready, n + 1)
                if has_before(i, s):
                    dve.wait_ge(turned, n - 1)
                nc.vector.tensor_tensor(with_agg[t][:p, :, :], mean_agg[t][:p, :, :], h[t][:p, :, :], ALU.add).then_inc(with_agg_ready, 1)

            def leak(i, s):
                n, p, t = i * U + s, parts_of(i, s), s % 2
                dve.wait_ge(fifth_ready, n + 1)
                if has_before(i, s):
                    dve.wait_ge(result_ready, n - 1)
                for b in range(HALVES):
                    ins = nc.vector.tensor_tensor(leaky[t][:p, b * TILES:(b + 1) * TILES, :], ps_o[t][b][:p, :, :],
                                                  fifth[t][:p, b * TILES:(b + 1) * TILES, :], ALU.max)
                ins.then_inc(leaky_ready, 1)

            in_steps(dve, pieces, U, (scale_and_shift, 1), (attention, 2), (moments, 0), (leak, 4))

        @block.scalar
        def _(act):
            def roots(i, s):
                n, p, t = i * U + s, parts_of(i, s), s % 2
                act.wait_ge(mean_var_ready, n + 1)
                nc.scalar.activation(std[t][:p, :], mean_var[t][:p, :, 1], ACT.Sqrt, bias=eps_col[:p, :]).then_inc(std_ready, 1)

            def normalise(i, s):
                n, p, t = i * U + s, parts_of(i, s), s % 2
                act.wait_ge(shift_ready, n + 1)
                if has_before(i, s):
                    act.wait_ge(with_agg_ready, n - 1)
                for k in range(PIECE):
                    ins = nc.scalar.activation(h[t][:p, k, :], x1[s][:p, k, :], ACT.Relu,
                                               bias=shift[t][:p, k:k + 1], scale=rstd[t][:p, k:k + 1])
                ins.then_inc(h_ready, 1)

            def move_turned(i, s):
                n, p, t = i * U + s, parts_of(i, s), s % 2
                act.wait_ge(turned, n + 1)
                if has_before(i, s):
                    act.wait_ge(multiplied, n - 1)
                for b in range(HALVES):
                    ins = nc.scalar.copy(transposed[t][:, b * TILES:(b + 1) * TILES, :p], ps_t[t][b][:, :, :p])
                ins.then_inc(transposed_ready, 1)

            def fifths(i, s):
                n, p, t = i * U + s, parts_of(i, s), s % 2
                act.wait_ge(multiplied, n + 1)
                if has_before(i, s):
                    act.wait_ge(leaky_ready, n - 1)
                for b in range(HALVES):
                    ins = nc.scalar.mul(fifth[t][:p, b * TILES:(b + 1) * TILES, :], ps_o[t][b][:p, :, :], 0.2)
                ins.then_inc(fifth_ready, 1)

            in_steps(act, pieces, U, (normalise, 1), (fifths, 3), (roots, 0), (move_turned, 2))

        @block.tensor
        def _(pe):
            pe.wait_ge(wt_in, 16)

            def turn(i, s):
                n, p, t = i * U + s, parts_of(i, s), s % 2
                pe.wait_ge(with_agg_ready, n + 1)
                if has_before(i, s):
                    pe.wait_ge(transposed_ready, n - 1)
                for k in range(PIECE):
                    ins = nc.tensor.transpose(ps_t[t][k // TILES][:, k % TILES, :p], with_agg[t][:p, k, :], ident[:p, :p])
                ins.then_inc(turned, 1)

            def multiply(i, s):
                n, p, t = i * U + s, parts_of(i, s), s % 2
                pe.wait_ge(transposed_ready, n + 1)
                if has_before(i, s):
                    pe.wait_ge(leaky_ready, n - 1)
                for k in range(PIECE):
                    ins = nc.tensor.matmul(ps_o[t][k // TILES][:p, k % TILES, :], transposed[t][:, k, :p], wt_sb[:, :],
                                           start=True, stop=True)
                ins.then_inc(multiplied, 1)

            in_steps(pe, pieces, U, (multiply, 3), (turn, 2))


def build(nc, x, by_edge, dst_row, src_row, type_row, conv, rel, wt, out):
    nodes = x.shape[0]
    windows = dst_row.shape[0]
    edge_tiles = windows * TILES
    assert windows % 2 == 0
    table_rows = -(-(nodes + 1) // (P * PIECE)) * P * PIECE
    pieces = table_rows // (P * PIECE)
    assert pieces == windows
    node_piece = nodes // windows
    node_tail = nodes - node_piece * windows

    def dram(name, shape):
        return nc.dram_tensor(name, shape, F32, kind="Internal").ap()

    table2, table3, x1_table = (dram(n, (table_rows, P)) for n in ("table2", "table3", "x1_table"))
    sums_table = dram("sums_table", (table_rows + GROUP, SUM_W))
    f1, f2, f3, xd_stream, et_stream = (dram(n, (windows, P, WIN)) for n in ("f1", "f2", "f3", "xd_stream", "et_stream"))

    ctx = ExitStack()
    with ctx:
        def sb(name, shape, dt=F32):
            return ctx.enter_context(nc.sbuf_tensor(name, shape, dt))

        zeros = sb("zeros", [P, PIECE * SUM_W])
        ones = sb("ones", [P, GROUP])
        ident = sb("ident", [P, P])
        eps_col = sb("eps_col", [P, 1])
        not_before = sb("not_before", [P, GROUP])
        spare_i, spare_rows = sb("spare_i", [P, GROUP_TILES], I32), sb("spare_rows", [P, GROUP_TILES])
        relation_i, relation_col = sb("relation_i", [RELATIONS, 1], I32), sb("relation_col", [RELATIONS, 1])
        scores = sb("scores", [P, windows * TILES])
        weights = sb("weights", [P, windows * TILES])
        src_all, dst_all, dst_seg_all, next_all, prev_all = (
            sb(n, [P, edge_tiles], I32) for n in ("src_all", "dst_all", "dst_seg_all", "next_all", "prev_all"))
        ends, firsts = sb("ends", [P, edge_tiles], I32), sb("firsts", [P, edge_tiles], I32)
        inner = [sb(f"inner{k}", [P, edge_tiles]) for k in (0, 1)]
        minus_half, minus_huge = sb("minus_half", [P, 2 * TILES]), sb("minus_huge", [P, 1])
        go = ctx.enter_context(nc.semaphore("set_up"))
        banks = [ctx.enter_context(nc.psum_tensor(f"bank{b}", [P, WIN], F32)) for b in range(8)]
        consts = {"banks": banks, "go": go, "ident": ident, "ones": ones, "eps": eps_col, "not_before": not_before, "spare_rows": spare_rows,
                  "relation_col": relation_col, "minus_half": minus_half,
                  "minus_huge": minus_huge, "src_all": src_all, "dst_all": dst_all, "dst_seg_all": dst_seg_all, "ends": ends,
                  "firsts": firsts}

        def clear(sp, table, n, width, sem):
            sp.dma_start(table[bass.ds(n * (P * PIECE), P * PIECE), :].rearrange("(p j) f -> p (j f)", j=PIECE),
                         zeros[:, :PIECE * width]).then_inc(sem, 16)

        with ExitStack() as setup:
            zeros_ready, memset_done = ctx.enter_context(nc.semaphore("zeros_ready")), ctx.enter_context(nc.semaphore("memset_done"))
            iota_done, cleared = ctx.enter_context(nc.semaphore("iota_done")), ctx.enter_context(nc.semaphore("cleared"))
            const_done = ctx.enter_context(nc.semaphore("const_done"))
            by_edge_in, inner_ready = ctx.enter_context(nc.semaphore("by_edge_in")), ctx.enter_context(nc.semaphore("inner_ready"))
            block = setup.enter_context(nc.Block())

            @block.gpsimd
            def _(pool):
                nc.gpsimd.memset(ones[:, :], 1.0).then_inc(memset_done, 1)
                nc.gpsimd.iota(spare_i[:, :], [[P, GROUP_TILES]], base=table_rows, channel_multiplier=1).then_inc(iota_done, 1)
                nc.gpsimd.iota(relation_i[:, :], [[0, 1]], base=0, channel_multiplier=1).then_inc(iota_done, 1)
                pool.wait_ge(memset_done, 1)
                nc.gpsimd.affine_select(ident[:, :], ones[:, :P], [[-1, P]], ALU.is_equal, 0.0, base=0, channel_multiplier=1)
                nc.gpsimd.affine_select(not_before[:, :], ones[:, :], [[1, GROUP]], ALU.is_gt, 0.0, base=1, channel_multiplier=-1)

            @block.vector
            def _(dve):
                nc.vector.memset(zeros[:, :], 0.0).then_inc(zeros_ready, 1)
                nc.vector.memset(eps_col[:, :], EPS).then_inc(go, 1)
                dve.wait_ge(iota_done, 2)
                nc.vector.tensor_copy(spare_rows[:, :], spare_i[:, :])
                nc.vector.tensor_copy(relation_col[:, :], relation_i[:, :]).then_inc(const_done, 1)
                nc.vector.memset(minus_half[:, :], -0.5)
                nc.vector.memset(minus_huge[:, :], -HUGE)
                dve.wait_ge(by_edge_in, 5 * 16)
                for k, beside in enumerate((next_all, prev_all)):
                    nc.vector.tensor_tensor(inner[k][:, :], dst_seg_all[:, :], beside[:, :], ALU.is_equal).then_inc(inner_ready, 1)
                for k, made in enumerate((ends, firsts)):
                    dve.wait_ge(inner_ready, k + 1)
                    nc.vector.scalar_tensor_tensor(made[:, :], inner[k][:, :], SKIP, dst_seg_all[:, :], ALU.mult, ALU.add)

            @block.sync
            def _(sp):
                for k, t in enumerate((src_all, dst_all, dst_seg_all, next_all, prev_all)):
                    sp.dma_start(t[:, :], by_edge[k]).then_inc(by_edge_in, 16)
                sp.wait_ge(zeros_ready, 1)
                sp.dma_start(x1_table[nodes - node_tail:nodes, :], x[nodes - node_tail:nodes, :]).then_inc(cleared, 16)
                spare = (table_rows - nodes) // PIECE
                sp.dma_start(x1_table[nodes:nodes + spare * PIECE, :].rearrange("(p j) f -> p (j f)", j=PIECE),
                             zeros[:spare, :PIECE * P]).then_inc(cleared, 16)
                sp.dma_start(sums_table[table_rows:, :].rearrange("(p j) f -> p (j f)", j=GROUP_TILES),
                             zeros[:, :GROUP_TILES * SUM_W]).then_inc(cleared, 16)
                sp.wait_ge(cleared, 16 * 3)

        def copy_x(sp, n, sem):
            size = node_piece * P // 16
            sp.dma_start(x1_table[bass.ds(n * node_piece, node_piece), :].rearrange("r f -> (r f)").rearrange("(a b) -> a b", b=size),
                         x[bass.ds(n * node_piece, node_piece), :].rearrange("r f -> (r f)").rearrange("(a b) -> a b", b=size)).then_inc(sem, 16)

        shared = dict(dst_row=dst_row, xd_stream=xd_stream, windows=windows)
        edge_conv_pass(nc, "c1", consts, first=True, last=False, table_in=None, x_rows=x, table_out=table2, f_in=None, f_out=f1,
                       weights=conv[0], early=EARLY, clear_out=lambda sp, n, sem: clear(sp, table2, n, P, sem), bulk=lambda sp, n, sem: clear(sp, table3, n, P, sem), **shared)
        edge_conv_pass(nc, "c2", consts, first=False, last=False, table_in=table2, x_rows=None, table_out=table3, f_in=f1, f_out=f2,
                       weights=conv[1], bulk=lambda sp, n, sem: copy_x(sp, n, sem), **shared)
        edge_conv_pass(nc, "c3", consts, first=False, last=True, table_in=table3, x_rows=None, table_out=x1_table, f_in=f2, f_out=f3,
                       weights=conv[2], bulk=lambda sp, n, sem: clear(sp, sums_table, n, SUM_W, sem), **shared)
        score_pass(nc, consts, type_row=type_row, x1_table=x1_table, f_in=f3, et_stream=et_stream, rel=rel, scores=scores, **shared)
        softmax_pass(nc, consts, scores=scores, weights=weights, edges_padded_from=nodes)
        sum_pass(nc, consts, src_row=src_row, et_stream=et_stream, sums_table=sums_table, weights=weights, windows=windows)
        node_pass(nc, consts, x1_table=x1_table, sums_table=sums_table, wt=wt, out=out, nodes=nodes)


def kernel(x, src, dst, edge_type_64, **p):
    import numpy as np
    import concourse.bacc as bacc
    from concourse.bass_utils import run_bass_kernel_spmd as run

    x, src, dst, kinds = (np.asarray(a) for a in (x, src, dst, edge_type_64))
    nodes, edges = x.shape[0], src.shape[0]
    windows = -(-edges // WIN)
    windows += windows % 2
    padded = windows * WIN

    def pad(a, fill):
        return np.concatenate([a, np.full((padded - edges,), fill, a.dtype)])

    def columns(a):
        return a.reshape(windows * TILES, P).T

    src_p, dst_g, dst_p, kind_p = pad(src, 0), pad(dst, 0), pad(dst, nodes), pad(kinds, 0)
    none = np.full((1,), -1, dst.dtype)
    around = np.concatenate([none, dst_p, none])
    arrays = {
        "x": x,
        "by_edge": np.stack([columns(a) for a in (src_p, dst_g, dst_p, around[2:], around[:-2])]),
        "dst_row": np.stack([around[w * WIN:w * WIN + WIN + 2] for w in range(windows)]).reshape(windows, 1, WIN + 2),
        "src_row": src_p.reshape(windows, 1, WIN),
        "type_row": kind_p.reshape(windows, 1, WIN),
        "rel": np.asarray(p["L1_gnn_rel_embed_weight"]),
        "wt": np.ascontiguousarray(np.asarray(p["L1_gnn_W"]).T),
    }
    for layer in ("in", "hid", "out"):
        arrays[f"W1_{layer}"] = np.asarray(p[f"L0_gnn_W1_{layer}"])
        arrays[f"W2_{layer}"] = np.asarray(p[f"L0_gnn_W2_{layer}"])
        arrays[f"b1_{layer}"] = np.asarray(p[f"L0_gnn_b1_{layer}"]).reshape(P, 1)
        arrays[f"b2_{layer}"] = np.asarray(p[f"L0_gnn_b2_{layer}"]).reshape(P, 1)

    nc = bacc.Bacc("TRN2", target_bir_lowering=False, num_devices=1)
    ap = {n: nc.dram_tensor(n, a.shape, mybir.dt.from_np(a.dtype), kind="ExternalInput").ap() for n, a in arrays.items()}
    out = nc.dram_tensor("out", x.shape, F32, kind="ExternalOutput").ap()
    conv = [{k: ap[f"{k}_{layer}"] for k in ("W1", "W2", "b1", "b2")} for layer in ("in", "hid", "out")]
    build(nc, ap["x"], ap["by_edge"], ap["dst_row"], ap["src_row"], ap["type_row"], conv, ap["rel"], ap["wt"], out)
    return run(nc, [arrays], core_ids=[0]).results[0]["out"]
```
